# Optimizing a Trainium2 kernel written in Bass

```python
import numpy as np
import jax
import jax.numpy as jnp

def _softmax(x, axis=-1):
    return jax.nn.softmax(x, axis=axis)

def _gelu(x):
    return jax.nn.gelu(x, approximate=True)

def _silu(x):
    return jax.nn.silu(x)

def _sigmoid(x):
    return jax.nn.sigmoid(x)

def _layernorm(x, axis=-1, eps=1e-05):
    m = jnp.mean(x, axis=axis, keepdims=True)
    v = jnp.var(x, axis=axis, keepdims=True)
    return (x - m) / jnp.sqrt(v + eps)

def _scatter_add(tgt, idx, src, axis=0):
    return tgt.at[idx].add(src)

def _segment_sum(src, seg, n):
    return jax.ops.segment_sum(src, seg, n)
kernel_name = 'mk_decoder_preln_d1_seqx_r8_54ce37'

def setup_inputs(seed: int=0):
    np.random.seed(seed)
    _w = jnp.asarray

    def _rec_inputs():
        import jax
        import jax.numpy as jnp
        _rk = jax.random.key(seed)
        x = -0.0002928 + 1 * jax.random.normal(jax.random.fold_in(_rk, 1), (16, 256, 128), jnp.float32)
        _lenS = 256 - jax.random.randint(jax.random.fold_in(_rk, 7), (16,), 0, max(1, 256 // 4) + 1, jnp.int32)
        _lenS2 = 64 - jax.random.randint(jax.random.fold_in(_rk, 8), (16,), 0, max(1, 64 // 4) + 1, jnp.int32)
        _ctx_512P = jax.random.normal(jax.random.fold_in(_rk, 11), (16, 16, 64), jnp.float32)
        _ctx_512c = jax.random.dirichlet(jax.random.fold_in(_rk, 511), 0.3 * jnp.ones((16,), jnp.float32), (16, 64))
        _ctx_512t = jnp.einsum('bsk,bkd->bsd', _ctx_512c, _ctx_512P)
        _ctx_512t = _ctx_512t * jax.lax.rsqrt(jnp.mean(jnp.square(_ctx_512t)) + 1e-12) * 0.953939
        ctx_512 = 0.00222621 + 0.99962 * (_ctx_512t + 0.3 * jax.random.normal(jax.random.fold_in(_rk, 611), (16, 64, 64), jnp.float32))
        return (x, ctx_512)
    x, ctx_512 = _rec_inputs()

    def _L0_attn_setup():
        import jax, jax.numpy as jnp
        import numpy as np
        EMBED_DIM = 128
        NUM_HEADS = 16
        HEAD_DIM = EMBED_DIM // NUM_HEADS
        WINDOW_SIZE = 32
        SCALE = 1.0 / np.sqrt(HEAD_DIM)

        def _band_mask(T):
            i = jnp.arange(T)[:, None]
            j = jnp.arange(T)[None, :]
            full = j > i
            band = full & (j >= i - (WINDOW_SIZE - 1))
            return band
        key = jax.random.key(seed)
        kx, kq, kk, kv, ko = jax.random.split(key, 5)
        B, T, C = (2, 256, EMBED_DIM)
        x = jax.random.normal(kx, (B, T, C), dtype=jnp.float32)
        s = 1.0 / np.sqrt(C)
        Wq = jax.random.uniform(kq, (C, C), dtype=jnp.float32, minval=-s, maxval=s)
        Wk = jax.random.uniform(kk, (C, C), dtype=jnp.float32, minval=-s, maxval=s)
        Wv = jax.random.uniform(kv, (C, C), dtype=jnp.float32, minval=-s, maxval=s)
        Wo = jax.random.uniform(ko, (C, C), dtype=jnp.float32, minval=-s, maxval=s)
        return {'x': x, 'Wq': Wq, 'Wk': Wk, 'Wv': Wv, 'Wo': Wo}
    _L0_attn_all = _L0_attn_setup()
    _L0_attn_in = {k: v for k, v in _L0_attn_all.items() if k in ('Wq', 'Wk', 'Wv', 'Wo')}
    del _L0_attn_all

    def _L0_xattn_setup():
        import jax, jax.numpy as jnp
        import numpy as np
        B, T, TC, C, CC, H = (2, 256, 64, 128, 64, 16)
        D = C // H

        def _heads(t):
            b, l, _ = t.shape
            return t.reshape(b, l, H, D).transpose(0, 2, 1, 3)
        key = jax.random.key(seed)
        ks = jax.random.split(key, 18)
        w = lambda k, i, o: jax.random.normal(k, (i, o), jnp.float32) / np.sqrt(i).astype(np.float32)
        return {'x': jax.random.normal(ks[0], (B, T, C), jnp.float32), 'cross_input': jax.random.normal(ks[1], (B, TC, CC), jnp.float32), 'Wk': w(ks[2], C, C), 'bk': jnp.zeros((C,), jnp.float32), 'Wq': w(ks[3], C, C), 'bq': jnp.zeros((C,), jnp.float32), 'Wv': w(ks[4], C, C), 'bv': jnp.zeros((C,), jnp.float32), 'Wck': w(ks[5], CC, C), 'bck': jnp.zeros((C,), jnp.float32), 'Wcq': w(ks[6], C, C), 'bcq': jnp.zeros((C,), jnp.float32), 'Wcv': w(ks[7], CC, C), 'bcv': jnp.zeros((C,), jnp.float32), 'Wp': w(ks[8], C, C), 'bp': jnp.zeros((C,), jnp.float32)}
    _L0_xattn_all = _L0_xattn_setup()
    _L0_xattn_in = {k: v for k, v in _L0_xattn_all.items() if k in ('Wk', 'bk', 'Wq', 'bq', 'Wv', 'bv', 'Wck', 'bck', 'Wcq', 'bcq', 'Wcv', 'bcv', 'Wp', 'bp')}
    del _L0_xattn_all

    def _L0_ffn_setup():
        import jax, jax.numpy as jnp
        import numpy as np
        DIM = 128
        DEPTH = 6
        HEADS = 16
        DIM_HEAD = 64
        WINDOW = 32
        INNER = HEADS * DIM_HEAD
        DIM_INNER = int(DIM * 4 * 2 / 3)
        QK_SCALE = 8.0

        def shift_tokens(t):
            a, s = jnp.split(t, 2, -1)
            s = jnp.pad(s, ((0, 0), (1, 0), (0, 0)))[:, :-1]
            return jnp.concatenate([a, s], -1)

        def l2norm(t):
            return t / jnp.maximum(jnp.linalg.norm(t, axis=-1, keepdims=True), 1e-12)

        def rotate_half(x):
            x1, x2 = jnp.split(x, 2, -1)
            return jnp.concatenate([-x2, x1], -1)

        def rotary_tables(n):
            half = jnp.arange(0, DIM_HEAD, 2, dtype=jnp.float32)
            inv_freq = 1.0 / 10000.0 ** (half / DIM_HEAD)
            t = jnp.arange(n, dtype=jnp.float32)
            freqs = t[:, None] * inv_freq[None, :]
            freqs = jnp.concatenate([freqs, freqs], -1)
            base_scale = (half + 0.4 * DIM_HEAD) / (1.4 * DIM_HEAD)
            power = (t - n // 2) / (WINDOW // 2)
            scale = base_scale[None, :] ** power[:, None]
            scale = jnp.concatenate([scale, scale], -1)
            return (freqs, scale)

        def local_attention(q, k, v):
            b, h, n, d = q.shape
            w = WINDOW
            nw = n // w
            bq = q.reshape(b, h, nw, w, d)
            bk = k.reshape(b, h, nw, w, d)
            bv = v.reshape(b, h, nw, w, d)

            def look(t):
                p = jnp.pad(t, ((0, 0), (0, 0), (1, 0), (0, 0), (0, 0)))
                return jnp.concatenate([p[:, :, :nw], p[:, :, 1:]], axis=3)
            bk2, bv2 = (look(bk), look(bv))
            seq = jnp.arange(n).reshape(nw, w)
            seq_p = jnp.pad(seq, ((1, 0), (0, 0)), constant_values=-1)
            jt = jnp.concatenate([seq_p[:nw], seq_p[1:]], axis=1)
            it = seq[:, :, None]
            jb = jt[:, None, :]
            mask = (it < jb) | (it > jb + w) | (jb == -1)
            sim = jnp.einsum('bhwie,bhwje->bhwij', bq, bk2) * QK_SCALE
            sim = jnp.where(mask, -jnp.finfo(sim.dtype).max, sim)
            attn = jax.nn.softmax(sim, -1)
            out = jnp.einsum('bhwij,bhwje->bhwie', attn, bv2)
            return out.reshape(b, h, n, d)

        def attn_layer(x, Wqkv, qs, ksc, Wo):
            b, n, _ = x.shape
            qkv = x @ Wqkv
            q, k, v = jnp.split(qkv, 3, -1)
            sh = lambda t: t.reshape(b, n, HEADS, DIM_HEAD).transpose(0, 2, 1, 3)
            q, k, v = (sh(q), sh(k), sh(v))
            q = l2norm(q) * qs
            k = l2norm(k) * ksc
            freqs, scale = rotary_tables(n)
            cos, sin = (jnp.cos(freqs), jnp.sin(freqs))
            q = q * cos * scale + rotate_half(q) * sin * scale
            inv = 1.0 / scale
            k = k * cos * inv + rotate_half(k) * sin * inv
            out = local_attention(q, k, v)
            out = out.transpose(0, 2, 1, 3).reshape(b, n, INNER)
            return out @ Wo

        def ffn_layer(x, g, bln, W1, b1, W2, b2):
            mu = x.mean(-1, keepdims=True)
            var = ((x - mu) ** 2).mean(-1, keepdims=True)
            xn = (x - mu) / jnp.sqrt(var + 1e-05) * g + bln
            hg = xn @ W1 + b1
            a, gate = jnp.split(hg, 2, -1)
            return a * jax.nn.gelu(gate, approximate=False) @ W2 + b2
        key = jax.random.key(seed)
        ks = jax.random.split(key, 8)
        B, N = (2, 256)
        init = lambda k, shape: jax.random.normal(k, shape, jnp.float32) * 0.02
        return {'x': jax.random.normal(ks[0], (B, N, DIM), jnp.float32), 'Wqkv': init(ks[1], (DEPTH, DIM, 3 * INNER)), 'q_scale': jnp.ones((DEPTH, DIM_HEAD), jnp.float32), 'k_scale': jnp.ones((DEPTH, DIM_HEAD), jnp.float32), 'Wo': init(ks[2], (DEPTH, INNER, DIM)), 'ln_g': jnp.ones((DEPTH, DIM), jnp.float32), 'ln_b': jnp.zeros((DEPTH, DIM), jnp.float32), 'W1': init(ks[3], (DEPTH, DIM, 2 * DIM_INNER)), 'b1': jnp.zeros((DEPTH, 2 * DIM_INNER), jnp.float32), 'W2': init(ks[4], (DEPTH, DIM_INNER, DIM)), 'b2': jnp.zeros((DEPTH, DIM), jnp.float32)}
    _L0_ffn_all = _L0_ffn_setup()
    _L0_ffn_in = {k: v for k, v in _L0_ffn_all.items() if k in ('Wqkv', 'q_scale', 'k_scale', 'Wo', 'ln_g', 'ln_b', 'W1', 'b1', 'W2', 'b2')}
    del _L0_ffn_all
    return {'x': x, 'ctx_512': ctx_512, 'L0_attn_Wq': _L0_attn_in['Wq'], 'L0_attn_Wk': _L0_attn_in['Wk'], 'L0_attn_Wv': _L0_attn_in['Wv'], 'L0_attn_Wo': _L0_attn_in['Wo'], 'L0_xattn_Wk': _L0_xattn_in['Wk'], 'L0_xattn_bk': _L0_xattn_in['bk'], 'L0_xattn_Wq': _L0_xattn_in['Wq'], 'L0_xattn_bq': _L0_xattn_in['bq'], 'L0_xattn_Wv': _L0_xattn_in['Wv'], 'L0_xattn_bv': _L0_xattn_in['bv'], 'L0_xattn_Wck': _L0_xattn_in['Wck'], 'L0_xattn_bck': _L0_xattn_in['bck'], 'L0_xattn_Wcq': _L0_xattn_in['Wcq'], 'L0_xattn_bcq': _L0_xattn_in['bcq'], 'L0_xattn_Wcv': _L0_xattn_in['Wcv'], 'L0_xattn_bcv': _L0_xattn_in['bcv'], 'L0_xattn_Wp': _L0_xattn_in['Wp'], 'L0_xattn_bp': _L0_xattn_in['bp'], 'L0_ffn_Wqkv': _L0_ffn_in['Wqkv'], 'L0_ffn_q_scale': _L0_ffn_in['q_scale'], 'L0_ffn_k_scale': _L0_ffn_in['k_scale'], 'L0_ffn_Wo': _L0_ffn_in['Wo'], 'L0_ffn_ln_g': _L0_ffn_in['ln_g'], 'L0_ffn_ln_b': _L0_ffn_in['ln_b'], 'L0_ffn_W1': _L0_ffn_in['W1'], 'L0_ffn_b1': _L0_ffn_in['b1'], 'L0_ffn_W2': _L0_ffn_in['W2'], 'L0_ffn_b2': _L0_ffn_in['b2']}

def reference(x, ctx_512, L0_attn_Wq, L0_attn_Wk, L0_attn_Wv, L0_attn_Wo, L0_xattn_Wk, L0_xattn_bk, L0_xattn_Wq, L0_xattn_bq, L0_xattn_Wv, L0_xattn_bv, L0_xattn_Wck, L0_xattn_bck, L0_xattn_Wcq, L0_xattn_bcq, L0_xattn_Wcv, L0_xattn_bcv, L0_xattn_Wp, L0_xattn_bp, L0_ffn_Wqkv, L0_ffn_q_scale, L0_ffn_k_scale, L0_ffn_Wo, L0_ffn_ln_g, L0_ffn_ln_b, L0_ffn_W1, L0_ffn_b1, L0_ffn_W2, L0_ffn_b2):
    import jax
    import jax.numpy as jnp

    def _L0_attn_ref(x, Wq, Wk, Wv, Wo):
        import jax, jax.numpy as jnp
        import numpy as np
        EMBED_DIM = 128
        NUM_HEADS = 16
        HEAD_DIM = EMBED_DIM // NUM_HEADS
        WINDOW_SIZE = 32
        SCALE = 1.0 / np.sqrt(HEAD_DIM)

        def _band_mask(T):
            i = jnp.arange(T)[:, None]
            j = jnp.arange(T)[None, :]
            full = j > i
            band = full & (j >= i - (WINDOW_SIZE - 1))
            return band
        B, T, C = x.shape
        H, D = (NUM_HEADS, HEAD_DIM)
        q = jnp.einsum('btc,oc->bto', x, Wq).reshape(B, T, H, D)
        k = jnp.einsum('btc,oc->bto', x, Wk).reshape(B, T, H, D)
        v = jnp.einsum('btc,oc->bto', x, Wv).reshape(B, T, H, D)
        att = jnp.einsum('bqhd,bkhd->bhqk', q, k) * SCALE
        mask = _band_mask(T)
        att = jnp.where(mask[None, None, :, :], -jnp.inf, att)
        att = jax.nn.softmax(att, axis=-1)
        out = jnp.einsum('bhqk,bkhd->bqhd', att, v).reshape(B, T, C)
        return jnp.einsum('btc,oc->bto', out, Wo)

    def _L0_xattn_ref(x, cross_input, Wk, bk, Wq, bq, Wv, bv, Wck, bck, Wcq, bcq, Wcv, bcv, Wp, bp):
        import jax, jax.numpy as jnp
        import numpy as np
        B, T, TC, C, CC, H = (2, 256, 64, 128, 64, 16)
        D = C // H

        def _heads(t):
            b, l, _ = t.shape
            return t.reshape(b, l, H, D).transpose(0, 2, 1, 3)
        scale = np.float32(1.0 / np.sqrt(D))
        q = _heads(x @ Wq + bq)
        k = _heads(x @ Wk + bk)
        v = _heads(x @ Wv + bv)
        att = jnp.einsum('bhqd,bhkd->bhqk', q, k) * scale
        causal = jnp.tril(jnp.ones((T, T), bool))
        att = jnp.where(causal[None, None], att, -jnp.inf)
        y = jnp.einsum('bhqk,bhkd->bhqd', jax.nn.softmax(att, axis=-1), v)
        qc = _heads(x @ Wcq + bcq)
        kc = _heads(cross_input @ Wck + bck)
        vc = _heads(cross_input @ Wcv + bcv)
        attc = jnp.einsum('bhqd,bhkd->bhqk', qc, kc) * scale
        y = y + jnp.einsum('bhqk,bhkd->bhqd', jax.nn.softmax(attc, axis=-1), vc)
        y = y.transpose(0, 2, 1, 3).reshape(x.shape[0], T, C)
        return y @ Wp + bp

    def _L0_ffn_ref(x, Wqkv, q_scale, k_scale, Wo, ln_g, ln_b, W1, b1, W2, b2):
        import jax, jax.numpy as jnp
        import numpy as np
        DIM = 128
        DEPTH = 6
        HEADS = 16
        DIM_HEAD = 64
        WINDOW = 32
        INNER = HEADS * DIM_HEAD
        DIM_INNER = int(DIM * 4 * 2 / 3)
        QK_SCALE = 8.0

        def shift_tokens(t):
            a, s = jnp.split(t, 2, -1)
            s = jnp.pad(s, ((0, 0), (1, 0), (0, 0)))[:, :-1]
            return jnp.concatenate([a, s], -1)

        def l2norm(t):
            return t / jnp.maximum(jnp.linalg.norm(t, axis=-1, keepdims=True), 1e-12)

        def rotate_half(x):
            x1, x2 = jnp.split(x, 2, -1)
            return jnp.concatenate([-x2, x1], -1)

        def rotary_tables(n):
            half = jnp.arange(0, DIM_HEAD, 2, dtype=jnp.float32)
            inv_freq = 1.0 / 10000.0 ** (half / DIM_HEAD)
            t = jnp.arange(n, dtype=jnp.float32)
            freqs = t[:, None] * inv_freq[None, :]
            freqs = jnp.concatenate([freqs, freqs], -1)
            base_scale = (half + 0.4 * DIM_HEAD) / (1.4 * DIM_HEAD)
            power = (t - n // 2) / (WINDOW // 2)
            scale = base_scale[None, :] ** power[:, None]
            scale = jnp.concatenate([scale, scale], -1)
            return (freqs, scale)

        def local_attention(q, k, v):
            b, h, n, d = q.shape
            w = WINDOW
            nw = n // w
            bq = q.reshape(b, h, nw, w, d)
            bk = k.reshape(b, h, nw, w, d)
            bv = v.reshape(b, h, nw, w, d)

            def look(t):
                p = jnp.pad(t, ((0, 0), (0, 0), (1, 0), (0, 0), (0, 0)))
                return jnp.concatenate([p[:, :, :nw], p[:, :, 1:]], axis=3)
            bk2, bv2 = (look(bk), look(bv))
            seq = jnp.arange(n).reshape(nw, w)
            seq_p = jnp.pad(seq, ((1, 0), (0, 0)), constant_values=-1)
            jt = jnp.concatenate([seq_p[:nw], seq_p[1:]], axis=1)
            it = seq[:, :, None]
            jb = jt[:, None, :]
            mask = (it < jb) | (it > jb + w) | (jb == -1)
            sim = jnp.einsum('bhwie,bhwje->bhwij', bq, bk2) * QK_SCALE
            sim = jnp.where(mask, -jnp.finfo(sim.dtype).max, sim)
            attn = jax.nn.softmax(sim, -1)
            out = jnp.einsum('bhwij,bhwje->bhwie', attn, bv2)
            return out.reshape(b, h, n, d)

        def attn_layer(x, Wqkv, qs, ksc, Wo):
            b, n, _ = x.shape
            qkv = x @ Wqkv
            q, k, v = jnp.split(qkv, 3, -1)
            sh = lambda t: t.reshape(b, n, HEADS, DIM_HEAD).transpose(0, 2, 1, 3)
            q, k, v = (sh(q), sh(k), sh(v))
            q = l2norm(q) * qs
            k = l2norm(k) * ksc
            freqs, scale = rotary_tables(n)
            cos, sin = (jnp.cos(freqs), jnp.sin(freqs))
            q = q * cos * scale + rotate_half(q) * sin * scale
            inv = 1.0 / scale
            k = k * cos * inv + rotate_half(k) * sin * inv
            out = local_attention(q, k, v)
            out = out.transpose(0, 2, 1, 3).reshape(b, n, INNER)
            return out @ Wo

        def ffn_layer(x, g, bln, W1, b1, W2, b2):
            mu = x.mean(-1, keepdims=True)
            var = ((x - mu) ** 2).mean(-1, keepdims=True)
            xn = (x - mu) / jnp.sqrt(var + 1e-05) * g + bln
            hg = xn @ W1 + b1
            a, gate = jnp.split(hg, 2, -1)
            return a * jax.nn.gelu(gate, approximate=False) @ W2 + b2
        for i in range(DEPTH):
            x = attn_layer(shift_tokens(x), Wqkv[i], q_scale[i], k_scale[i], Wo[i]) + x
            x = ffn_layer(shift_tokens(x), ln_g[i], ln_b[i], W1[i], b1[i], W2[i], b2[i]) + x
        return x
    x = x + _L0_attn_ref(_layernorm(x, axis=-1), L0_attn_Wq, L0_attn_Wk, L0_attn_Wv, L0_attn_Wo)
    x = x + _L0_xattn_ref(_layernorm(x, axis=-1), ctx_512, L0_xattn_Wk, L0_xattn_bk, L0_xattn_Wq, L0_xattn_bq, L0_xattn_Wv, L0_xattn_bv, L0_xattn_Wck, L0_xattn_bck, L0_xattn_Wcq, L0_xattn_bcq, L0_xattn_Wcv, L0_xattn_bcv, L0_xattn_Wp, L0_xattn_bp)
    x = x + _L0_ffn_ref(_layernorm(x, axis=-1), L0_ffn_Wqkv, L0_ffn_q_scale, L0_ffn_k_scale, L0_ffn_Wo, L0_ffn_ln_g, L0_ffn_ln_b, L0_ffn_W1, L0_ffn_b1, L0_ffn_W2, L0_ffn_b2)
    return x

_drawn_inputs = setup_inputs


def setup_inputs(seed=0):
    import zlib

    import numpy as np

    out = dict(_drawn_inputs(seed))
    spreads = {'L0_xattn_bk': (0.0, 0.8),
     'L0_xattn_bq': (0.0, 0.467),
     'L0_xattn_bv': (0.0, 0.1),
     'L0_xattn_bck': (0.0, 0.8),
     'L0_xattn_bcq': (0.0, 0.376),
     'L0_xattn_bcv': (0.0, 0.1),
     'L0_xattn_bp': (0.0, 0.1),
     'L0_ffn_q_scale': (1.0, 0.6),
     'L0_ffn_k_scale': (1.0, 0.6),
     'L0_ffn_ln_g': (1.0, 0.6),
     'L0_ffn_ln_b': (0.0, 0.8),
     'L0_ffn_b1': (0.0, 0.8),
     'L0_ffn_b2': (0.0, 0.1)}
    factors = {'L0_attn_Wq': 3.042, 'L0_attn_Wk': 2.981, 'L0_ffn_W1': 3.978, 'L0_ffn_W2': 3.889}
    for name, (base, spread) in spreads.items():
        noise = np.random.default_rng([zlib.crc32(name.encode()), seed]).standard_normal(out[name].shape)
        drawn = base * np.exp(spread * noise) if base else spread * noise
        out[name] = jnp.asarray(drawn.astype(out[name].dtype))
    for name, factor in factors.items():
        out[name] = (out[name] * factor).astype(out[name].dtype)
    return out
```

```python
from contextlib import ExitStack

import concourse.bass as bass
from concourse import mybir

P = 128
B, T, DIM = 16, 256, 128
DEPTH, HEADS, DIM_HEAD, WINDOW = 6, 16, 64, 32
INNER = HEADS * DIM_HEAD
DIM_INNER = int(DIM * 4 * 2 / 3)
NT = 2 * T
PAIRS = B // 2
QUADS = HEADS // 4
GROUPS = NT // P
FRONT = 3 * WINDOW
QK_SCALE = 8.0
LN_EPS = 1e-5
MASKED = -1e30
VEC = 16

def spans(*widths):
    out, at = [], 0
    for w in widths:
        out.append((at, at + w))
        at += w
    return out

W_QK, W_V, W_O, W_1, W_2, W_VEC = spans(2 * INNER, INNER, INNER, 6 * P, 3 * P, VEC)
W_COLS = W_VEC[1]
C_IDENT, C_MEAN, C_MASK, C_SUM, C_SPREAD, C_TRIG, C_CAUSAL, C_HEAD = spans(P, P, 512, 64, QUADS * P, 4 * T, 384, 4)
C_COLS = C_HEAD[1]
A_SELF, A_CQ, A_CK, A_CV, A_BP, A_BIAS = 4, 8, 9, 10, 11, 12 * P
B_ZERO, B_Q, B_K, B_V, B_CQ, B_CK, B_CV = range(7)
A_COLS = A_BIAS + 8

F32 = mybir.dt.float32
ALU = mybir.AluOpType
ACT = mybir.ActivationFunctionType
AX = mybir.AxisListType

def layer_weights(np, inp):
    wqkv = np.asarray(inp["L0_ffn_Wqkv"])
    w = np.zeros((DEPTH, P, W_COLS), np.float32)
    for t, third in ((0, 1), (1, 0)):
        part = wqkv[:, :, third * INNER:(third + 1) * INNER].reshape(DEPTH, DIM, QUADS, 4, 2, 32)
        w[:, :, W_QK[0] + t * INNER:W_QK[0] + (t + 1) * INNER] = \
            part.transpose(0, 1, 2, 4, 3, 5).reshape(DEPTH, DIM, INNER)
    wv = wqkv[:, :, 2 * INNER:].reshape(DEPTH, DIM, 8, P)
    w[:, :, W_V[0]:W_V[1]] = wv.transpose(0, 3, 2, 1).reshape(DEPTH, P, INNER)
    wo = np.asarray(inp["L0_ffn_Wo"]).reshape(DEPTH, 8, P, DIM)
    w[:, :, W_O[0]:W_O[1]] = wo.transpose(0, 2, 1, 3).reshape(DEPTH, P, INNER)
    for half in range(2):
        at = W_1[0] + half * 3 * P
        w[:, :, at:at + DIM_INNER] = np.asarray(inp["L0_ffn_W1"])[:, :, half * DIM_INNER:(half + 1) * DIM_INNER]
        b = np.zeros((DEPTH, 3 * P), np.float32)
        b[:, :DIM_INNER] = np.asarray(inp["L0_ffn_b1"])[:, half * DIM_INNER:(half + 1) * DIM_INNER]
        w[:, :, W_VEC[0] + 6 + 3 * half:W_VEC[0] + 9 + 3 * half] = b.reshape(DEPTH, 3, P).transpose(0, 2, 1)
    w2 = np.zeros((DEPTH, 3 * P, DIM), np.float32)
    w2[:, :DIM_INNER] = np.asarray(inp["L0_ffn_W2"])
    w[:, :, W_2[0]:W_2[1]] = w2.reshape(DEPTH, 3, P, DIM).transpose(0, 2, 1, 3).reshape(DEPTH, P, 3 * DIM)
    for t, name in ((0, "L0_ffn_k_scale"), (1, "L0_ffn_q_scale")):
        s = np.asarray(inp[name]).reshape(DEPTH, 1, 2, 32)
        w[:, :, W_VEC[0] + 2 * t:W_VEC[0] + 2 * t + 2] = \
            np.broadcast_to(s, (DEPTH, 4, 2, 32)).transpose(0, 1, 3, 2).reshape(DEPTH, P, 2)
    for n, name in ((4, "L0_ffn_ln_g"), (5, "L0_ffn_ln_b"), (12, "L0_ffn_b2")):
        w[:, :, W_VEC[0] + n] = np.asarray(inp[name])
    return w

def constants(np):
    c = np.zeros((P, C_COLS), np.float32)
    c[:, C_IDENT[0]:C_IDENT[1]] = np.eye(P)
    c[:, C_MEAN[0]:C_MEAN[1]] = 1.0 / DIM
    r, s = np.arange(P)[:, None] % 32, np.arange(32)[None, :]
    before = np.where(s >= r, 0.0, MASKED)
    first = np.where(np.arange(P)[:, None] < 32, MASKED, before)
    own = np.where(s <= r, 0.0, MASKED)
    per_group = [np.concatenate([first if g % 2 == 0 else before, own] * 2, 1) for g in range(GROUPS)]
    c[:, C_MASK[0]:C_MASK[1]] = np.concatenate(per_group, 1)
    head = np.arange(P) // 32
    for i in range(4):
        c[head == i, C_SUM[0] + 4 + i] = 1.0
        c[head == i, C_SUM[0] + 32 + i] = 1.0
        for j in range(QUADS):
            c[32 * j + 4 + i, C_SPREAD[0] + j * P + 32 * i:C_SPREAD[0] + j * P + 32 * i + 32] = 1.0
    q, k = np.arange(P)[:, None], np.arange(P)[None, :]
    causal = np.where(k > q, MASKED, 0.0)
    c[:, C_CAUSAL[0]:C_CAUSAL[1]] = np.concatenate([causal, np.zeros((P, P)), causal], 1)
    for n in range(4):
        c[(np.arange(P) // 8) % 4 == n, C_HEAD[0] + n] = 1.0
    f32 = np.float32
    half = np.arange(0, DIM_HEAD, 2, dtype=f32)
    inv_freq = (f32(1.0) / f32(10000.0) ** (half / f32(DIM_HEAD))).astype(f32)
    t = np.arange(T, dtype=f32)
    freqs = (t[:, None] * inv_freq[None, :]).astype(f32)
    base = ((half + f32(0.4 * DIM_HEAD)) / f32(1.4 * DIM_HEAD)).astype(f32)
    power = (t - T // 2) / f32(WINDOW // 2)
    scale = (base[None, :] ** power[:, None]).astype(f32)
    rows = [np.cos(freqs) * scale, np.sin(freqs) * scale, np.cos(freqs) / scale, np.sin(freqs) / scale]
    c[:, C_TRIG[0]:C_TRIG[1]] = np.concatenate([np.tile(x.T.astype(f32), (4, 1)) for x in rows], 1)
    return c

def attention_weights(np, inp):
    w = np.zeros((P, A_COLS), np.float32)
    for n, name in enumerate(("Wq", "Wk", "Wv", "Wo")):
        w[:, n * P:(n + 1) * P] = np.asarray(inp["L0_attn_" + name]).T
    for n, name in ((4, "Wq"), (5, "Wk"), (6, "Wv"), (7, "Wp"), (A_CQ, "Wcq"), (A_CK, "Wck"), (A_CV, "Wcv")):
        m = np.asarray(inp["L0_xattn_" + name])
        w[:m.shape[0], n * P:(n + 1) * P] = m
    w[0, A_BP * P:(A_BP + 1) * P] = np.asarray(inp["L0_xattn_bp"])
    for n, name in ((B_Q, "bq"), (B_K, "bk"), (B_V, "bv"), (B_CQ, "bcq"), (B_CK, "bck"), (B_CV, "bcv")):
        w[:, A_BIAS + n] = np.asarray(inp["L0_xattn_" + name])
    return w

def attention_blocks(nc, c, x_in_dram, ctx_dram, w_attn, x2, state):
    BF16, F32R = mybir.dt.bfloat16, mybir.dt.float32r
    UNITS = 20
    BLOCK_END = (7, 11, 19)
    SELF_SCALE = float(1.0 / (DIM // HEADS) ** 0.5)

    with ExitStack() as ctx:
        def sb(name, shape, dt=F32):
            return ctx.enter_context(nc.sbuf_tensor("a_" + name, shape, dt))

        def sem(name):
            return ctx.enter_context(nc.semaphore("a_" + name))

        w = sb("w", [P, A_COLS])
        ident = sb("ident", [P, P])
        ident_r = sb("ident_r", [P, P], F32R)
        ident_b = sb("ident_b", [P, P], BF16)
        ones = sb("ones", [P, P])
        causal32 = sb("causal32", [P, 384])
        causal = sb("causal", [P, 384], BF16)
        head_of = sb("head_of", [P, 4])
        bias_v = sb("bias_v", [P, 2])
        x = sb("x", [P, 2, DIM])
        x_mid = sb("x_mid", [P, 2, DIM])
        x_out = sb("x_out", [P, 2, DIM])
        stats = sb("stats", [P, 2, 6])
        moments = sb("moments", [P, 2, 2])
        rstd = sb("rstd", [P, 2])
        xn = sb("xn", [P, 2, DIM])
        h_t = sb("h_t", [P, T])
        ctx_t = sb("ctx_t", [64, P])
        q_m = sb("q_m", [P, 4, T])
        qc_m = sb("qc_m", [P, 4, T])
        k_t = sb("k_t", [P, T])
        kc_t = sb("kc_t", [P, 64])
        v_a = sb("v_a", [P, 2, HEADS, 32])
        vc_a = sb("vc_a", [P, HEADS, 32])
        negmax = sb("negmax", [P, 2, 8], F32R)
        prob = sb("prob", [P, 2, 2, 384])
        prob_t = sb("prob_t", [P, 2, 2, 384])
        o_t = sb("o_t", [P, 4, T])
        rden = sb("rden", [P, 32])
        o_n = sb("o_n", [P, 2, DIM])
        o_c = sb("o_c", [P, 2, DIM])
        on_t = sb("on_t", [P, T])

        bank = [ctx.enter_context(nc.psum_tensor(f"a_ps{i}", [P, 2, 512], F32)) for i in range(4)]
        p_prob, p_out = bank[2], bank[3]

        consts_in, consts_set, pads_set, ones_set = (sem(n) for n in ("consts_in", "consts_set", "pads_set", "ones_set"))
        x_in, x_free, stored = sem("x_in"), sem("x_free"), sem("stored")
        moment, rooted, normed, h_sum, h_set = (sem(n) for n in ("moment", "rooted", "normed", "h_sum", "h_set"))
        projected, operands = sem("projected"), sem("operands")
        scored, maxed, shifted, exped, turned, turned_out, mixed = (sem(n) for n in (
            "scored", "maxed", "shifted", "exped", "turned", "turned_out", "mixed"))
        o_out, o_turned, o_inv, o_normed, on_sum, on_set, y_sum, y_set, state_set = (sem(n) for n in (
            "o_out", "o_turned", "o_inv", "o_normed", "on_sum", "on_set", "y_sum", "y_set", "state_set"))

        block = ctx.enter_context(nc.Block())

        def at(it, per, n):
            return it * per + (n + 1)

        def weight(n):
            return w[:, n * P:(n + 1) * P]

        def bias(n):
            return w[:, A_BIAS + n:A_BIAS + n + 1]

        def is_cross(u):
            return 8 <= u < 12

        def shape_of(u):
            return (1, 512) if is_cross(u) else (2, 384)

        @block.sync
        def _(sp):
            for dst, a, b in ((ident[:], *C_IDENT), (causal32[:], *C_CAUSAL), (head_of[:], *C_HEAD)):
                sp.dma_start(dst, c[:, a:b]).then_inc(consts_in, 16)
            sp.dma_start(w[:], w_attn).then_inc(consts_in, 16)
            for s in (x_in, stored):
                sp.sem_inc(s, 1)
            with sp.Fori(0, B) as it:
                sp.wait_ge(x_free, at(it, 1, 0))
                sp.dma_start(x[:], x_in_dram[it].rearrange("(t p) n -> p t n", t=2)).then_inc(x_in, 16)
                for n in range(2):
                    sp.dma_start(ctx_t[:, 64 * n:64 * n + 64], ctx_dram[it]).then_inc(x_in, 16)
                sp.wait_ge(y_set, at(it, 2, 2))
                sp.dma_start(x2[it].rearrange("(t p) n -> p t n", t=2), x_out[:]).then_inc(stored, 16)
                sp.wait_ge(h_set, at(it, 3, 3))
                sp.dma_start(state[:, bass.ts(it, T)], h_t[:]).then_inc(stored, 16)
                sp.wait_ge(stored, at(it, 32, 32))
                sp.sem_inc(state_set, 1)

        @block.gpsimd
        def _(pool):
            nc.gpsimd.memset(ones[:], 1.0)
            nc.gpsimd.memset(v_a[:], 0.0)
            nc.gpsimd.memset(vc_a[:], 0.0).then_inc(pads_set, 1)
            pool.wait_ge(pads_set, 1)
            nc.gpsimd.memset(v_a[:, :, :, 8:9], 1.0).then_inc(pads_set, 1)
            pool.wait_ge(pads_set, 2)
            nc.gpsimd.memset(vc_a[0:64, 0::2, 8:9], 1.0).then_inc(ones_set, 1)
            pool.wait_ge(ones_set, 1)
            nc.gpsimd.memset(vc_a[64:P, 1::2, 8:9], 1.0).then_inc(ones_set, 1)

        @block.scalar
        def _(act):
            act.wait_ge(consts_in, 64)
            nc.scalar.copy(ident_r[:], ident[:]).then_inc(consts_set, 1)
            nc.scalar.copy(ident_b[:], ident[:]).then_inc(consts_set, 1)
            nc.scalar.copy(causal[:], causal32[:]).then_inc(consts_set, 1)
            for s in (rooted, h_set, exped, turned_out, on_set):
                act.sem_inc(s, 1)
            with act.Fori(0, B) as it:
                def norm_and_turn(r):
                    act.wait_ge(moment, at(it, 3, r + 1))
                    nc.scalar.activation(rstd[:], rstd[:], ACT.Sqrt).then_inc(rooted, 1)
                    act.wait_ge(h_sum, at(it, 3, r + 1))
                    nc.scalar.copy(h_t[:], p_prob[:, 0, 0:T]).then_inc(h_set, 1)

                def units(first, last):
                    def copy_out(u):
                        if is_cross(u) or u % 2:
                            act.wait_ge(turned, at(it, UNITS, u + 1))
                            if u >= 2:
                                act.wait_ge(mixed, at(it, UNITS, u - 1))
                            n, k = shape_of(u)
                            if is_cross(u):
                                nc.scalar.copy(prob_t[:, u % 2].rearrange("p a b -> p (a b)")[:, 0:512],
                                               p_prob[:, u % 2, :]).then_inc(turned_out, 1)
                            else:
                                nc.scalar.copy(prob_t[:, u % 2], p_prob[:, :, 0:384]).then_inc(turned_out, 1)

                    for u in range(first, last):
                        n, k = shape_of(u)
                        act.wait_ge(shifted, at(it, UNITS, u + 1))
                        if u >= 2:
                            act.wait_ge(turned, at(it, UNITS, u - 1))
                        out = prob[:, u % 2].rearrange("p a b -> p (a b)")[:, 0:n * k] \
                            .rearrange("p (a b) -> p a b", a=n)
                        nc.scalar.activation(out, bank[u % 2][:, 0:n, 0:k], ACT.Exp, scale=SELF_SCALE)\
                            .then_inc(exped, 1)
                        if u > first:
                            copy_out(u - 1)
                    copy_out(last - 1)

                norm_and_turn(0)
                units(0, 8)
                act.wait_ge(on_sum, at(it, 2, 1))
                nc.scalar.activation(on_t[:], p_prob[:, 0, 0:T], ACT.Identity, bias=bias_v[:, 0:1])\
                    .then_inc(on_set, 1)
                norm_and_turn(1)
                units(8, 12)
                units(12, 20)
                act.wait_ge(on_sum, at(it, 2, 2))
                nc.scalar.activation(on_t[:], p_prob[:, 0, 0:T], ACT.Identity, bias=bias_v[:, 1:2])\
                    .then_inc(on_set, 1)
                act.wait_ge(moment, at(it, 3, 3))
                nc.scalar.activation(rstd[:], rstd[:], ACT.Sqrt).then_inc(rooted, 1)
                act.wait_ge(h_sum, at(it, 3, 3))
                nc.scalar.copy(h_t[:], p_prob[:, 0, 0:T]).then_inc(h_set, 1)

        @block.vector
        def _(dve):
            for s in (x_free, moment, normed, operands, maxed, turned_out, o_out, o_inv, o_normed, y_set):
                if s is not turned_out:
                    dve.sem_inc(s, 1)
            dve.wait_ge(consts_in, 64)
            dve.wait_ge(ones_set, 2)
            nc.vector.memset(bias_v[:, 0:1], 0.0)
            nc.vector.tensor_tensor(out=bias_v[:, 1:2], in0=bias(B_V), in1=bias(B_CV), op=ALU.add)\
                .then_inc(consts_set, 1)
            with dve.Fori(0, B) as it:
                def norm(r, src):
                    steps = at(it, 9, 3 * r)
                    for t in range(2):
                        last = nc.vector.bn_stats(stats[:, t, :], src[:, t, :])
                    last.then_inc(normed, 1)
                    dve.wait_ge(normed, steps + 1)
                    nc.vector.memset(rstd[:], LN_EPS)
                    for t in range(2):
                        last = nc.vector.bn_aggr(moments[:, t, :], stats[:, t, :])
                    last.then_inc(normed, 1)
                    dve.wait_ge(normed, steps + 2)
                    nc.vector.tensor_tensor(out=rstd[:], in0=moments[:, :, 1:2].rearrange("p t o -> p (t o)"),
                                            in1=rstd[:], op=ALU.add).then_inc(moment, 1)
                    dve.wait_ge(rooted, at(it, 3, r + 1))
                    nc.vector.reciprocal(rstd[:], rstd[:]).then_inc(o_inv, 1)
                    dve.wait_ge(o_inv, at(it, 6, (1, 3, 6)[r]))
                    for t in range(2):
                        last = nc.vector.tensor_scalar(xn[:, t, :], src[:, t, :], moments[:, t, 0:1],
                                                       rstd[:, t:t + 1], ALU.subtract, ALU.mult)
                    last.then_inc(normed, 1)

                def heads(out, src, b):
                    for n in range(4):
                        last = nc.vector.tensor_scalar(out[:, n, :], src, b, head_of[:, n:n + 1], ALU.add, ALU.mult)
                    return last

                def take_projections(blk):
                    dve.wait_ge(projected, at(it, 2, blk + 1))
                    heads(q_m, p_out[:, 0, 0:T], bias(B_Q if blk else B_ZERO))
                    nc.vector.tensor_scalar(k_t[:], p_out[:, 0, T:2 * T], bias(B_K if blk else B_ZERO), None, ALU.add)
                    for t in range(2):
                        last = nc.vector.tensor_copy(v_a[:, t, :, 0:8],
                                                     p_out[:, 1, t * P:(t + 1) * P].rearrange("p (h d) -> p h d", d=8))
                    if blk:
                        heads(qc_m, p_out[:, 1, T:2 * T], bias(B_CQ))
                        nc.vector.tensor_scalar(kc_t[:], p_prob[:, 1, 0:64], bias(B_CK), None, ALU.add)
                        for n in range(2):
                            r = slice(64 * n, 64 * n + 64)
                            last = nc.vector.tensor_copy(
                                vc_a[r, n::2, 0:8], p_prob[r, 1, P:2 * P].rearrange("p (h d) -> p h d", d=8)[:, n::2])
                    last.then_inc(operands, 1)

                def units(first, last):
                    def copy_out(u):
                        if not is_cross(u) and u % 2 == 0:
                            dve.wait_ge(turned, at(it, UNITS, u + 1))
                            if u >= 2:
                                dve.wait_ge(mixed, at(it, UNITS, u - 1))
                            nc.vector.tensor_copy(prob_t[:, u % 2], p_prob[:, :, 0:384]).then_inc(turned_out, 1)

                    for u in range(first, last):
                        dve.wait_ge(scored, at(it, UNITS, u + 1))
                        if u >= 2:
                            dve.wait_ge(shifted, at(it, UNITS, u - 1))
                        if is_cross(u):
                            nc.vector.tensor_reduce(negmax[:, u % 2, :],
                                                    bank[u % 2][:, 0, :].rearrange("p (c k) -> p c k", k=64), AX.X,
                                                    ALU.max, negate=True).then_inc(maxed, 1)
                        else:
                            nc.vector.tensor_reduce(negmax[:, u % 2, 0:2], bank[u % 2][:, :, 0:P], AX.X, ALU.max,
                                                    negate=True)
                            nc.vector.tensor_reduce(negmax[:, u % 2, 2:4], bank[u % 2][:, :, P:384], AX.X, ALU.max,
                                                    negate=True).then_inc(maxed, 1)
                        if u > first:
                            copy_out(u - 1)
                    copy_out(last - 1)

                def take_outputs(n, out):
                    dve.wait_ge(mixed, at(it, UNITS, BLOCK_END[n] + 1))
                    nc.vector.tensor_copy(o_t[:].rearrange("p a b -> p (a b)"), p_out[:].rearrange("p a b -> p (a b)"))\
                        .then_inc(o_out, 1)
                    dve.wait_ge(o_turned, at(it, 3, n + 1))
                    o = p_prob[:].rearrange("p a (h k) -> p (a h) k", k=32)
                    nc.vector.reciprocal(rden[:], o[:, :, 8:9].rearrange("p a b -> p (a b)")).then_inc(o_inv, 1)
                    dve.wait_ge(o_inv, at(it, 6, (2, 4, 5)[n]))
                    nc.vector.tensor_tensor(out=out[:].rearrange("p t (h d) -> p (t h) d", d=8), in0=o[:, :, 0:8],
                                            in1=rden[:].unsqueeze(2).broadcast_to([P, 32, 8]), op=ALU.mult)\
                        .then_inc(o_normed, 1)

                dve.wait_ge(x_in, at(it, 48, 48))
                norm(0, x)
                take_projections(0)
                units(0, 8)
                take_outputs(0, o_n)
                dve.wait_ge(y_sum, at(it, 2, 1))
                nc.vector.tensor_tensor(out=x_mid[:].rearrange("p t n -> p (t n)"), in0=p_prob[:, 1, 0:T],
                                        in1=x[:].rearrange("p t n -> p (t n)"), op=ALU.add).then_inc(y_set, 1)
                dve.wait_ge(y_set, at(it, 2, 1))
                norm(1, x_mid)
                take_projections(1)
                dve.sem_inc(x_free, 1)
                units(8, 12)
                take_outputs(1, o_c)
                units(12, 20)
                take_outputs(2, o_n)
                dve.wait_ge(o_normed, at(it, 4, 3))
                nc.vector.tensor_tensor(out=o_n[:], in0=o_n[:], in1=o_c[:], op=ALU.add).then_inc(o_normed, 1)
                dve.wait_ge(y_sum, at(it, 2, 2))
                dve.wait_ge(state_set, at(it, 1, 0))
                nc.vector.tensor_tensor(out=x_out[:].rearrange("p t n -> p (t n)"), in0=p_prob[:, 1, 0:T],
                                        in1=x_mid[:].rearrange("p t n -> p (t n)"), op=ALU.add).then_inc(y_set, 1)
                dve.wait_ge(y_set, at(it, 2, 2))
                norm(2, x_out)

        @block.tensor
        def _(pe):
            for s in (h_sum, projected, scored, shifted, turned, mixed, o_turned, on_sum, y_sum, state_set):
                pe.sem_inc(s, 1)
            pe.wait_ge(consts_in, 64)
            pe.wait_ge(consts_set, 4)
            pe.wait_ge(ones_set, 2)
            with pe.Fori(0, B) as it:
                def turn_tokens(r):
                    pe.wait_ge(normed, at(it, 9, 3 * r + 3))
                    if r == 0:
                        pe.wait_ge(state_set, at(it, 1, 0))
                    for t in range(2):
                        last = nc.tensor.transpose(p_prob[:, 0, t * P:(t + 1) * P], xn[:, t, :], ident[:])
                    last.then_inc(h_sum, 1)

                def project(blk):
                    pe.wait_ge(h_set, at(it, 3, blk + 1))
                    wq, wk, wv = (weight(n + (A_SELF if blk else 0)) for n in range(3))
                    nc.tensor.matmul(p_out[:, 0, 0:T], wq, h_t[:], start=True, stop=True)
                    nc.tensor.matmul(p_out[:, 0, T:2 * T], wk, h_t[:], start=True, stop=True)
                    for t in range(2):
                        last = nc.tensor.matmul(p_out[:, 1, t * P:(t + 1) * P], h_t[:, t * P:(t + 1) * P], wv,
                                                start=True, stop=True)
                    if blk:
                        nc.tensor.matmul(p_out[:, 1, T:2 * T], weight(A_CQ), h_t[:], start=True, stop=True)
                        nc.tensor.matmul(p_prob[:, 1, 0:64], weight(A_CK)[0:64], ctx_t[:, 0:64], start=True, stop=True)
                        last = nc.tensor.matmul(p_prob[:, 1, P:2 * P], ctx_t[:], weight(A_CV)[0:64], start=True,
                                                stop=True)
                    last.then_inc(projected, 1)
                    pe.wait_ge(operands, at(it, 2, blk + 1))

                def scores(u):
                    s = bank[u % 2]
                    if u >= 2:
                        pe.wait_ge(exped, at(it, UNITS, u - 1))
                    if is_cross(u):
                        g = u - 8
                        r = slice(32 * g, 32 * g + 32)
                        for t in range(2):
                            for n in range(4):
                                col = t * 256 + n * 64
                                last = nc.tensor.matmul(s[:, 0, col:col + 64], qc_m[r, n, t * P:(t + 1) * P],
                                                        kc_t[r, :], start=not col, stop=True,
                                                        skip_group_check=True)
                    else:
                        d = u if u < 8 else u - 12
                        for n in range(2):
                            h = 2 * d + n
                            r = slice(32 * (h // 4), 32 * (h // 4) + 32)
                            q = q_m[r, h % 4, :]
                            nc.tensor.matmul(s[:, n, 0:384], ident_b[:], causal[:], start=True, stop=True)
                            nc.tensor.matmul(s[:, n, 0:P], q[:, 0:P], k_t[r, 0:P], start=False, stop=True,
                                             skip_group_check=True)
                            last = nc.tensor.matmul(s[:, n, P:384], q[:, P:T], k_t[r, :], start=False, stop=True,
                                                    skip_group_check=True)
                    last.then_inc(scored, 1)

                def shift(u):
                    s = bank[u % 2]
                    pe.wait_ge(maxed, at(it, UNITS, u + 1))
                    if is_cross(u):
                        last = nc.tensor.matmul(s[:, 0, :].rearrange("p (c k) -> p c k", k=64), ident_r[:],
                                                negmax[:, u % 2, :].unsqueeze(2).broadcast_to([P, 8, 64]),
                                                start=False, stop=True, skip_group_check=True)
                    else:
                        for n in range(2):
                            for t in range(2):
                                out = s[:, n, P:384] if t else s[:, n, 0:P]
                                m = negmax[:, u % 2, 2 * t + n:2 * t + n + 1]
                                last = nc.tensor.matmul(out, ident_r[:], m.broadcast_to([P, out.shape[1]]),
                                                        start=False, stop=True, skip_group_check=True)
                    last.then_inc(shifted, 1)

                def turn(u):
                    pe.wait_ge(exped, at(it, UNITS, u + 1))
                    if u:
                        pe.wait_ge(turned_out, at(it, UNITS, u))
                    p = prob[:, u % 2].rearrange("p a b -> p (a b)")
                    if is_cross(u):
                        for hp in range(2):
                            for t in range(2):
                                last = nc.tensor.transpose(p_prob[:, u % 2, (2 * hp + t) * P:(2 * hp + t + 1) * P],
                                                           p[:, t * 256 + hp * P:t * 256 + (hp + 1) * P], ident[:])
                    else:
                        for n in range(2):
                            for b in range(3):
                                last = nc.tensor.transpose(p_prob[:, n, b * P:(b + 1) * P],
                                                           p[:, n * 384 + b * P:n * 384 + (b + 1) * P], ident[:])
                    last.then_inc(turned, 1)

                def mix(u):
                    pe.wait_ge(turned_out, at(it, UNITS, u + 1))
                    if is_cross(u):
                        g = u - 8
                        pt = prob_t[:, u % 2].rearrange("p a b -> p (a b)")
                        for n in range(4):
                            last = nc.tensor.matmul(p_out[32 * n:32 * n + 32, g // 2, (g % 2) * T:(g % 2 + 1) * T],
                                                    vc_a[:, 4 * g + n, :], pt[:, (n // 2) * T:(n // 2 + 1) * T],
                                                    start=True, stop=True)
                    else:
                        d = u if u < 8 else u - 12
                        for n in range(2):
                            h = 2 * d + n
                            g, rows = h // 4, slice(32 * (h % 4), 32 * (h % 4) + 32)
                            col = (g % 2) * T
                            nc.tensor.matmul(p_out[rows, g // 2, col:col + T], v_a[:, 0, h, :],
                                             prob_t[:, u % 2, n, 0:T], start=True, stop=True)
                            last = nc.tensor.matmul(p_out[rows, g // 2, col + P:col + T], v_a[:, 1, h, :],
                                                    prob_t[:, u % 2, n, T:384], start=False, stop=True,
                                                    skip_group_check=True)
                    last.then_inc(mixed, 1)

                def units(first, last):
                    for u in range(first, last):
                        scores(u)
                        shift(u)
                        if u > first:
                            turn(u - 1)
                        if u > first + 1:
                            mix(u - 2)
                    turn(last - 1)
                    mix(last - 2)
                    mix(last - 1)

                def turn_outputs(n):
                    pe.wait_ge(o_out, at(it, 3, n + 1))
                    for t in range(2):
                        for g in range(4):
                            last = nc.tensor.transpose(p_prob[:, t, g * P:(g + 1) * P], o_t[:, g, t * P:(t + 1) * P],
                                                       ident[:])
                    last.then_inc(o_turned, 1)

                def project_out(blk):
                    pe.wait_ge(o_normed, at(it, 4, 4 if blk else 1))
                    for t in range(2):
                        last = nc.tensor.transpose(p_prob[:, 0, t * P:(t + 1) * P], o_n[:, t, :], ident[:])
                    last.then_inc(on_sum, 1)
                    pe.wait_ge(on_set, at(it, 2, blk + 1))
                    wo = weight(A_SELF + 3 if blk else 3)
                    for t in range(2):
                        out = p_prob[:, 1, t * P:(t + 1) * P]
                        last = nc.tensor.matmul(out, on_t[:, t * P:(t + 1) * P], wo, start=True, stop=not blk)
                        if blk:
                            last = nc.tensor.matmul(out, ones[:], weight(A_BP), start=False, stop=True)
                    last.then_inc(y_sum, 1)

                turn_tokens(0)
                project(0)
                units(0, 8)
                turn_outputs(0)
                project_out(0)
                turn_tokens(1)
                project(1)
                units(8, 12)
                turn_outputs(1)
                pe.wait_ge(o_normed, at(it, 4, 2))
                units(12, 20)
                turn_outputs(2)
                project_out(1)
                turn_tokens(2)

def transformer_layers(nc, c, w_layers, state):
    BF16, F32R = mybir.dt.bfloat16, mybir.dt.float32r

    with ExitStack() as ctx:
        def sb(name, shape, dt=F32):
            return ctx.enter_context(nc.sbuf_tensor("f_" + name, shape, dt))

        def sem(name):
            return ctx.enter_context(nc.semaphore("f_" + name))

        raw = sb("raw", [P, W_COLS])
        wqk_hi = sb("wqk_hi", [P, 2, QUADS, 2, P], F32R)
        wqk_lo = sb("wqk_lo", [P, 2, QUADS, 2, P], F32R)
        w_vo = sb("w_vo", [P, 2, 8, P])
        w1 = sb("w1", [P, 6, P])
        w2 = sb("w2", [P, 3, P])
        vec = sb("vec", [P, VEC])
        b1 = sb("b1", [P, 6])
        trig = sb("trig", [P, 4, T])
        straight = [sb(f"straight{t}", [P, 2, T]) for t in range(2)]
        crossed = [sb(f"crossed{t}", [P, 2, T]) for t in range(2)]
        ident = sb("ident", [P, P])
        ident_r = sb("ident_r", [P, P], F32R)
        ident_b = sb("ident_b", [P, P], BF16)
        mean_w = sb("mean_w", [P, P])
        head_sum = sb("head_sum", [P, 2, 32])
        spread = sb("spread", [P, QUADS, P])
        mask = sb("mask", [P, 512], BF16)
        x = sb("x", [P, NT])
        xs = sb("xs", [P, FRONT + NT + 64])
        xs_now = xs[:, FRONT:FRONT + NT]
        xs_hi = sb("xs_hi", [P, NT], F32R)
        xs_lo = sb("xs_lo", [P, NT], F32R)
        xw = sb("xw", [P, 18, P])
        sq = sb("sq", [P, 2, 2, NT])
        rot = sb("rot", [P, QUADS, 2, NT])
        rotq = sb("rotq", [P, 2, 2, NT])
        q_t = sb("q_t", [P, 8, NT])
        k_t = sb("k_t", [P, 8, 32 + NT])
        rq = sb("rq", [P, QUADS, 2, GROUPS, 2])
        negmax = sb("negmax", [P, 2, 16], F32R)
        den = sb("den", [P, 2, 16])
        rden = sb("rden", [P, 2, 16])
        prob = sb("prob", [P, 2, 1024])
        prob_t = sb("prob_t", [P, QUADS, 2, GROUPS * P])
        y_t = sb("y_t", [P, 2, 8, NT])
        flat_y = y_t[:].rearrange("p a b n -> p (a b n)")
        up = flat_y[:, 0:2048].rearrange("p (s a n) -> p s a n", s=2, a=2)
        vp = flat_y[:, 2048:4096].rearrange("p (s a n) -> p s a n", s=2, a=2)
        zs = flat_y[:, 4096:6144].rearrange("p (s n) -> p s n", s=2)
        norm, rnorm, mask32 = (flat_y[:, 6144 + 512 * n:6656 + 512 * n] for n in range(3))
        x1 = q_t[:, 0, :]
        xs2 = q_t[:, 1, :]
        xc = q_t[:, 2, :]
        xsq = q_t[:, 3, :]
        var = q_t[:, 4, :]
        rstd = q_t[:, 5, :]
        xn = q_t[:, 6, :]
        xo = q_t[:, 7, :]
        gate = sq[:].rearrange("p a b n -> p (a b) n")
        hid = xw[:, 0:16].rearrange("p (a b) n -> p a (b n)", a=4)

        bank = [ctx.enter_context(nc.psum_tensor(f"f_ps{i}", [P, 2, 512], F32)) for i in range(4)]
        pj = [bank[0], bank[1]]
        one = [bank[2][:, 0, :], bank[2][:, 1, :], bank[3][:, 0, :], bank[3][:, 1, :]]

        consts_in, consts_set = sem("consts_in"), sem("consts_set")
        w_in, w_rounded, w_tables, w_vo_sum, w_ready, w_taken = (sem(n) for n in (
            "w_in", "w_rounded", "w_tables", "w_vo_sum", "w_ready", "w_taken"))
        x_in, x_free, x_hi, x_lo, xw_sum, xw_copied = (sem(n) for n in (
            "x_in", "x_free", "x_hi", "x_lo", "xw_sum", "xw_copied"))
        projected, squared, scaled, rotated = (sem(n) for n in ("projected", "squared", "scaled", "rotated"))
        normed2, rooted, recip, rq_sum, rq_set, spread_out, k_normed = (sem(n) for n in (
            "normed2", "rooted", "recip", "rq_sum", "rq_set", "spread_out", "k_normed"))
        q_laid, k_laid = ([sem(f"{n}{j}") for j in range(QUADS)] for n in ("q_laid", "k_laid"))
        scored, maxed, shifted, z_set, exped, summed, inverted, probs_set, turned, turned_out = (sem(n) for n in (
            "scored", "maxed", "shifted", "z_set", "exped", "summed", "inverted", "probs_set", "turned",
            "turned_out"))
        mixed, mixed_a, mixed_v, attended, x1_set, centred, meaned, csq, vared, roots, dve_ln = (sem(n) for n in (
            "mixed", "mixed_a", "mixed_v", "attended", "x1_set", "centred", "meaned", "csq", "vared", "roots",
            "dve_ln"))
        h_sum, gated, hid_set, out_sum, out_set, stored = (sem(n) for n in (
            "h_sum", "gated", "hid_set", "out_sum", "out_set", "stored"))

        block = ctx.enter_context(nc.Block())

        def at(it, per, n):
            return it * per + (n + 1)

        def two(t):
            return t.unsqueeze(2).broadcast_to([P, 2, 2, T])

        @block.sync
        def _(sp):
            for dst, a, b in ((ident[:], *C_IDENT), (mean_w[:], *C_MEAN), (mask32, *C_MASK)):
                sp.dma_start(dst, c[:, a:b]).then_inc(consts_in, 16)
            sp.dma_start(head_sum[:].rearrange("p a b -> p (a b)"), c[:, C_SUM[0]:C_SUM[1]]).then_inc(consts_in, 16)
            sp.dma_start(spread[:].rearrange("p a b -> p (a b)"), c[:, C_SPREAD[0]:C_SPREAD[1]]).then_inc(consts_in, 16)
            sp.dma_start(trig[:].rearrange("p a b -> p (a b)"), c[:, C_TRIG[0]:C_TRIG[1]]).then_inc(consts_in, 16)
            for s, n in ((w_in, 1), (x_in, 1), *((s, 1) for s in q_laid + k_laid), (stored, 1)):
                sp.sem_inc(s, n)
            sp.wait_ge(consts_set, 5)
            with sp.Fori(0, DEPTH) as layer:
                sp.wait_ge(w_taken, at(layer, 1, 0))
                sp.dma_start(raw[:], w_layers[layer]).then_inc(w_in, 16)
                with sp.Fori(0, PAIRS) as pair:
                    it = layer * PAIRS + pair
                    sp.wait_ge(x_free, at(it, 1, 0))
                    sp.wait_ge(stored, at(it, 16, 0))
                    cols = state[:, bass.ts(pair, NT)]
                    sp.dma_start(x[:], cols).then_inc(x_in, 16)
                    sp.dma_start(xs_now[0:64, :], cols[0:64, :]).then_inc(x_in, 16)
                    for s in range(2):
                        sp.dma_start(xs_now[64:P, T * s + 1:T * (s + 1)],
                                     cols[64:P, T * s:T * (s + 1) - 1]).then_inc(x_in, 16)
                    for j in range(QUADS):
                        sp.wait_ge(rotated, at(it, 8, 2 * j + 2))
                        for ab in range(2):
                            for i in range(4):
                                to = 64 * (i % 2) + 32 * ab
                                sp.dma_start(q_t[to:to + 32, 2 * j + i // 2, :],
                                             rotq[32 * i:32 * i + 32, j % 2, ab, :]).then_inc(q_laid[j], 16)
                    for j in range(QUADS):
                        sp.wait_ge(k_normed, at(it, QUADS, j + 1))
                        for ab in range(2):
                            for i in range(4):
                                to = 64 * (i % 2) + 32 * ab
                                sp.dma_start(k_t[to:to + 32, 2 * j + i // 2, 32:32 + NT],
                                             rot[32 * i:32 * i + 32, j, ab, :]).then_inc(k_laid[j], 16)
                    sp.wait_ge(out_set, at(it, 1, 1))
                    sp.dma_start(cols, xo).then_inc(stored, 16)
            sp.wait_ge(stored, at(DEPTH * PAIRS, 16, 0))

        @block.gpsimd
        def _(pool):
            nc.gpsimd.memset(xs[:], 0.0).then_inc(consts_set, 1)
            nc.gpsimd.memset(k_t[:], 0.0).then_inc(consts_set, 1)
            for s in (rotated, probs_set):
                pool.sem_inc(s, 1)
            with pool.Fori(0, DEPTH * PAIRS) as it:
                for n in range(8):
                    j, t = n // 2, n % 2
                    pool.wait_ge(scaled, at(it, 8, n + 1))
                    if t and j >= 2:
                        pool.wait_ge(q_laid[j - 2], at(it, 128, 128))
                    out = rotq[:, j % 2] if t else rot[:, j]
                    nc.gpsimd.tensor_tensor(out=out, in0=up[:, n % 2], in1=vp[:, n % 2, ::-1, :],
                                            op=ALU.add).then_inc(rotated, 1)
                for j in range(QUADS):
                    pool.wait_ge(inverted, at(it, QUADS, j + 1))
                    r = rden[:, j % 2, :].unsqueeze(2).broadcast_to([P, 16, 64])
                    p3 = prob[:, j % 2, :].rearrange("p (c k) -> p c k", k=64)
                    nc.gpsimd.tensor_tensor(out=p3, in0=p3, in1=r, op=ALU.mult).then_inc(probs_set, 1)

        @block.scalar
        def _(act):
            act.wait_ge(consts_in, 16 * 6)
            nc.scalar.copy(ident_r[:], ident[:]).then_inc(consts_set, 1)
            nc.scalar.copy(ident_b[:], ident[:]).then_inc(consts_set, 1)
            nc.scalar.copy(mask[:], mask32).then_inc(consts_set, 1)
            for s in (w_rounded, x_hi, xw_copied, squared, rooted, exped, turned_out, mixed_a, csq, roots, gated):
                act.sem_inc(s, 1)
            with act.Fori(0, DEPTH) as layer:
                act.wait_ge(w_in, at(layer, 16, 16))
                if True:
                    act.wait_ge(out_set, at(layer, PAIRS, 0))
                nc.scalar.copy(wqk_hi[:].rearrange("p t j a n -> p (t j a n)"), raw[:, W_QK[0]:W_QK[1]])\
                    .then_inc(w_rounded, 1)
                for n in range(2):
                    act.wait_ge(w_vo_sum, at(layer, 2, n + 1))
                    nc.scalar.copy(w_vo[:, n].rearrange("p c n -> p (c n)"),
                                   bank[n][:].rearrange("p a n -> p (a n)")).then_inc(w_rounded, 1)
                with act.Fori(0, PAIRS) as pair:
                    it = layer * PAIRS + pair
                    act.wait_ge(x_in, at(it, 64, 64))
                    nc.scalar.copy(xs_hi[:], xs_now).then_inc(x_hi, 1)
                    for n in range(5):
                        act.wait_ge(xw_sum, at(it, 5, n + 1))
                        to = xw[:, 4 * n:min(4 * n + 4, 18)].rearrange("p w n -> p (w n)")
                        nc.scalar.copy(to, (one + [pj[1][:, 1, :]])[n][:, 0:to.shape[1]]).then_inc(xw_copied, 1)
                    for n in range(8):
                        act.wait_ge(projected, at(it, 8, n + 1))
                        if n >= 2:
                            act.wait_ge(normed2, at(it, 8, n - 1))
                        nc.scalar.activation(sq[:, n % 2], pj[n % 2][:], ACT.Square).then_inc(squared, 1)
                    act.wait_ge(normed2, at(it, 8, 8))
                    nc.scalar.activation(norm, one[2], ACT.Sqrt).then_inc(rooted, 1)
                    for j in range(QUADS):
                        act.wait_ge(z_set, at(it, QUADS, j + 1))
                        if j >= 2:
                            act.wait_ge(turned, at(it, 8, 2 * j - 2))
                        nc.scalar.activation(prob[:, j % 2, :], zs[:, j % 2, :], ACT.Exp, scale=QK_SCALE)\
                            .then_inc(exped, 1)
                        for n in ((2 * j - 2, 2 * j - 1) if j else ()):
                            act.wait_ge(turned, at(it, 8, n + 1))
                            nc.scalar.copy(prob_t[:, n // 2, n % 2, :], one[n % 4]).then_inc(turned_out, 1)
                    for n in (6, 7):
                        act.wait_ge(turned, at(it, 8, n + 1))
                        nc.scalar.copy(prob_t[:, n // 2, n % 2, :], one[n % 4]).then_inc(turned_out, 1)
                    for w in range(0, 16, 2):
                        act.wait_ge(mixed, at(it, 16, w + 1))
                        nc.scalar.copy(y_t[:, :, :, 32 * w:32 * w + 32],
                                       pj[w % 2][:, :, 0:256].rearrange("p a (h n) -> p a h n", n=32))\
                            .then_inc(mixed_a, 1)
                    act.wait_ge(centred, at(it, 1, 1))
                    nc.scalar.activation(xsq, xc, ACT.Square).then_inc(csq, 1)
                    act.wait_ge(dve_ln, at(it, 3, 1))
                    nc.scalar.activation(rstd, var, ACT.Sqrt).then_inc(roots, 1)
                    for n in range(3):
                        act.wait_ge(h_sum, at(it, 3, n + 1))
                        nc.scalar.activation(gate[:, n, :], pj[n % 2][:, 1, :], ACT.Gelu, bias=b1[:, 3 + n:4 + n])\
                            .then_inc(gated, 1)

        @block.vector
        def _(dve):
            for s in (w_tables, w_ready, w_taken, x_free, x_lo, scaled, recip, rq_set, k_normed, maxed, z_set,
                      summed, inverted, mixed_v, x1_set, centred, dve_ln, hid_set, out_set):
                dve.sem_inc(s, 1)
            dve.wait_ge(consts_in, 16 * 6)
            with dve.Fori(0, DEPTH) as layer:
                dve.wait_ge(w_in, at(layer, 16, 16))
                nc.vector.tensor_copy(vec[:], raw[:, W_VEC[0]:W_VEC[1]]).then_inc(w_tables, 1)
                nc.vector.tensor_copy(w2[:].rearrange("p c n -> p (c n)"), raw[:, W_2[0]:W_2[1]])
                dve.wait_ge(w_rounded, at(layer, 3, 1))
                nc.vector.tensor_tensor(out=wqk_lo[:].rearrange("p t j a n -> p (t j a n)"),
                                        in0=raw[:, W_QK[0]:W_QK[1]],
                                        in1=wqk_hi[:].rearrange("p t j a n -> p (t j a n)").bitcast(F32),
                                        op=ALU.subtract)
                dve.wait_ge(w_tables, at(layer, 2, 1))
                for t in range(2):
                    base = 2 if t == 0 else 0
                    for ab in range(2):
                        s = vec[:, 2 * t + ab:2 * t + ab + 1]
                        nc.vector.tensor_scalar(straight[t][:, ab, :], trig[:, base, :], s, None, ALU.mult)
                        nc.vector.tensor_scalar(crossed[t][:, ab, :], trig[:, base + 1, :], s,
                                                -1.0 if ab else 1.0, ALU.mult, ALU.mult)
                nc.vector.tensor_scalar(w1[:].rearrange("p c n -> p (c n)"), raw[:, W_1[0]:W_1[1]],
                                        vec[:, 4:5], None, ALU.mult)
                dve.wait_ge(w_vo_sum, at(layer, 2, 2))
                nc.vector.tensor_tensor(out=b1[:], in0=one[0][:, 0:6], in1=vec[:, 6:12], op=ALU.add)\
                    .then_inc(w_tables, 1)
                dve.wait_ge(w_tables, at(layer, 2, 2))
                dve.wait_ge(w_rounded, at(layer, 3, 3))
                dve.sem_inc(w_taken, 1)
                dve.sem_inc(w_ready, 1)
                with dve.Fori(0, PAIRS) as pair:
                    it = layer * PAIRS + pair
                    dve.wait_ge(x_hi, at(it, 1, 1))
                    nc.vector.tensor_tensor(out=xs_lo[:], in0=xs_now, in1=xs_hi[:].bitcast(F32),
                                            op=ALU.subtract).then_inc(x_lo, 1)
                    for n in range(8):
                        t = n % 2
                        dve.wait_ge(squared, at(it, 8, n + 1))
                        if n >= 2:
                            dve.wait_ge(rotated, at(it, 8, n - 1))
                        src = pj[n % 2][:].rearrange("p a (s n) -> p a s n", s=2)
                        nc.vector.tensor_tensor(out=up[:, n % 2].rearrange("p a (s n) -> p a s n", s=2), in0=src,
                                                in1=two(straight[t][:]), op=ALU.mult)
                        nc.vector.tensor_tensor(out=vp[:, n % 2].rearrange("p a (s n) -> p a s n", s=2), in0=src,
                                                in1=two(crossed[t][:]), op=ALU.mult).then_inc(scaled, 1)
                    dve.wait_ge(rooted, at(it, 1, 1))
                    nc.vector.tensor_scalar(norm, norm, 1e-12, None, ALU.max).then_inc(recip, 1)
                    dve.wait_ge(recip, at(it, 2, 1))
                    nc.vector.reciprocal(rnorm, norm).then_inc(recip, 1)
                    dve.wait_ge(rq_sum, at(it, 1, 1))
                    for g in range(GROUPS):
                        last = nc.vector.tensor_copy(
                            rq[:, :, :, g, :],
                            one[3][:, g * P:(g + 1) * P].rearrange("p (j r) -> p j r", j=QUADS)[:, :, 0:4]
                            .rearrange("p j (c a) -> p j a c", a=2))
                    last.then_inc(rq_set, 1)
                    for j in range(QUADS):
                        dve.wait_ge(spread_out, at(it, QUADS, j + 1))
                        dve.wait_ge(rotated, at(it, 8, 2 * j + 1))
                        nc.vector.tensor_tensor(out=rot[:, j], in0=rot[:, j],
                                                in1=one[j % 2].unsqueeze(1).broadcast_to([P, 2, NT]), op=ALU.mult)\
                            .then_inc(k_normed, 1)
                    dve.wait_ge(rq_set, at(it, 1, 1))

                    def sums(j):
                        dve.wait_ge(exped, at(it, QUADS, j + 1))
                        nc.vector.tensor_reduce(den[:, j % 2, :], prob[:, j % 2, :].rearrange("p (c k) -> p c k", k=64),
                                                AX.X, ALU.add).then_inc(summed, 1)
                        dve.wait_ge(summed, at(it, QUADS, j + 1))
                        if j >= 2:
                            dve.wait_ge(probs_set, at(it, QUADS, j - 1))
                        nc.vector.reciprocal(rden[:, j % 2, :], den[:, j % 2, :]).then_inc(inverted, 1)

                    for j in range(QUADS):
                        s4 = pj[j % 2][:].rearrange("p a (c k) -> p a c k", k=64)
                        dve.wait_ge(scored, at(it, QUADS, j + 1))
                        if j >= 2:
                            dve.wait_ge(shifted, at(it, QUADS, j - 1))
                        nc.vector.tensor_reduce(negmax[:, j % 2, :].rearrange("p (a c) -> p a c", a=2), s4, AX.X,
                                                ALU.max, negate=True).then_inc(maxed, 1)
                        dve.wait_ge(shifted, at(it, QUADS, j + 1))
                        if j >= 2:
                            dve.wait_ge(exped, at(it, QUADS, j - 1))
                        nc.vector.tensor_tensor(
                            out=zs[:, j % 2, :].rearrange("p (c k) -> p c k", k=64),
                            in0=pj[j % 2][:].rearrange("p a (c k) -> p (a c) k", k=64),
                            in1=rq[:, j].rearrange("p a g c -> p (a g c)").unsqueeze(2).broadcast_to([P, 16, 64]),
                            op=ALU.mult).then_inc(z_set, 1)
                        if j:
                            sums(j - 1)
                    sums(QUADS - 1)
                    dve.wait_ge(exped, at(it, QUADS, QUADS))
                    for w in range(1, 16, 2):
                        dve.wait_ge(mixed, at(it, 16, w + 1))
                        nc.vector.tensor_copy(y_t[:, :, :, 32 * w:32 * w + 32],
                                              pj[w % 2][:, :, 0:256].rearrange("p a (h n) -> p a h n", n=32))\
                            .then_inc(mixed_v, 1)
                    dve.wait_ge(attended, at(it, 1, 1))
                    nc.vector.tensor_tensor(out=x1, in0=one[0], in1=x[:], op=ALU.add)
                    nc.vector.tensor_tensor(out=xs2[0:64], in0=one[0][0:64], in1=x[0:64], op=ALU.add)
                    nc.vector.memset(xs2.rearrange("p (s n) -> p s n", s=2)[64:P, :, 0:1], 0.0)
                    nc.vector.tensor_tensor(
                        out=xs2.rearrange("p (s n) -> p s n", s=2)[64:P, :, 1:T],
                        in0=one[0].rearrange("p (s n) -> p s n", s=2)[64:P, :, 0:T - 1],
                        in1=x[:].rearrange("p (s n) -> p s n", s=2)[64:P, :, 0:T - 1], op=ALU.add).then_inc(x1_set, 1)
                    dve.wait_ge(x1_set, at(it, 1, 1))
                    dve.sem_inc(x_free, 1)
                    dve.wait_ge(meaned, at(it, 1, 1))
                    nc.vector.tensor_tensor(out=xc, in0=xs2, in1=one[1], op=ALU.subtract).then_inc(centred, 1)
                    dve.wait_ge(vared, at(it, 1, 1))
                    nc.vector.tensor_scalar(var, one[2], LN_EPS, None, ALU.add).then_inc(dve_ln, 1)
                    dve.wait_ge(roots, at(it, 1, 1))
                    nc.vector.reciprocal(rstd, rstd).then_inc(dve_ln, 1)
                    dve.wait_ge(dve_ln, at(it, 3, 2))
                    nc.vector.tensor_tensor(out=xn, in0=xc, in1=rstd, op=ALU.mult).then_inc(dve_ln, 1)
                    for n in range(3):
                        dve.wait_ge(gated, at(it, 3, n + 1))
                        nc.vector.scalar_tensor_tensor(out=hid[:, n, :], in0=pj[n % 2][:, 0, :],
                                                       scalar=b1[:, n:n + 1], in1=gate[:, n, :], op0=ALU.add,
                                                       op1=ALU.mult).then_inc(hid_set, 1)
                    dve.wait_ge(out_sum, at(it, 1, 1))
                    nc.vector.scalar_tensor_tensor(out=xo, in0=one[3], scalar=vec[:, 12:13], in1=x1, op0=ALU.add,
                                                   op1=ALU.add).then_inc(out_set, 1)

        @block.tensor
        def _(pe):
            for s in (w_vo_sum, xw_sum, projected, normed2, rq_sum, spread_out, scored, shifted, turned, mixed,
                      attended, meaned, vared, h_sum, out_sum):
                pe.sem_inc(s, 1)
            pe.wait_ge(consts_in, 16 * 6)
            pe.wait_ge(consts_set, 5)
            with pe.Fori(0, DEPTH) as layer:
                pe.wait_ge(w_in, at(layer, 16, 16))
                pe.wait_ge(out_set, at(layer, PAIRS, 0))
                wv = raw[:, W_V[0]:W_V[1]].rearrange("p (c n) -> p c n", c=8)
                wo = raw[:, W_O[0]:W_O[1]].rearrange("p (c n) -> p c n", c=8)
                for n in range(6):
                    nc.tensor.matmul(one[0][:, n:n + 1], raw[:, W_1[0] + n * P:W_1[0] + (n + 1) * P],
                                     raw[:, W_VEC[0] + 5:W_VEC[0] + 6], start=True, stop=True)
                for par in range(2):
                    r = slice(64 * par, 64 * par + 64)
                    for ch in range(8):
                        last = nc.tensor.matmul(bank[par][:, ch // 4, (ch % 4) * P:(ch % 4 + 1) * P],
                                                wv[r, ch, :], wo[r, ch, :], start=True, stop=True)
                    last.then_inc(w_vo_sum, 1)
                with pe.Fori(0, PAIRS) as pair:
                    it = layer * PAIRS + pair
                    pe.wait_ge(x_in, at(it, 64, 64))
                    pe.wait_ge(w_ready, at(layer, 1, 1))
                    pe.wait_ge(out_set, at(it, 1, 0))
                    for n in range(5):
                        for w in range(4 * n, min(4 * n + 4, 18)):
                            last = nc.tensor.transpose((one + [pj[1][:, 1, :]])[n][:, (w % 4) * P:(w % 4 + 1) * P],
                                                       xs[:, 32 * w:32 * w + P], ident[:])
                        last.then_inc(xw_sum, 1)
                    pe.wait_ge(x_lo, at(it, 1, 1))

                    def sums(n):
                        pe.wait_ge(squared, at(it, 8, n + 1))
                        j, t = n // 2, n % 2
                        for ab in range(2):
                            last = nc.tensor.matmul(one[2][32 * j:32 * j + 32, :], head_sum[:, t, :],
                                                    sq[:, n % 2, ab, :], start=(t == 0 and ab == 0),
                                                    stop=(t == 1 and ab == 1))
                        last.then_inc(normed2, 1)

                    for n in range(8):
                        j, t = n // 2, n % 2
                        if n >= 2:
                            pe.wait_ge(scaled, at(it, 8, n - 1))
                        if n == 1:
                            pe.wait_ge(xw_copied, at(it, 5, 5))
                        for ab in range(2):
                            hi, lo = wqk_hi[:, t, j, ab, :], wqk_lo[:, t, j, ab, :]
                            nc.tensor.matmul(pj[n % 2][:, ab, :], hi, xs_hi[:], start=True, stop=False)
                            nc.tensor.matmul(pj[n % 2][:, ab, :], hi, xs_lo[:], start=False, stop=False)
                            last = nc.tensor.matmul(pj[n % 2][:, ab, :], lo, xs_hi[:], start=False, stop=True)
                        last.then_inc(projected, 1)
                        if n:
                            sums(n - 1)
                    sums(7)
                    pe.wait_ge(recip, at(it, 2, 2))
                    for g in range(GROUPS):
                        last = nc.tensor.transpose(one[3][:, g * P:(g + 1) * P], rnorm[:, g * P:(g + 1) * P], ident[:])
                    last.then_inc(rq_sum, 1)
                    for j in range(QUADS):
                        if j >= 2:
                            pe.wait_ge(k_normed, at(it, QUADS, j - 1))
                        nc.tensor.matmul(one[j % 2], spread[:, j, :], rnorm, start=True, stop=True)\
                            .then_inc(spread_out, 1)
                    pe.wait_ge(k_normed, at(it, QUADS, QUADS))
                    pe.wait_ge(rq_set, at(it, 1, 1))

                    def scores(j):
                        if j >= 2:
                            pe.wait_ge(z_set, at(it, QUADS, j - 1))
                        else:
                            pe.wait_ge(scaled, at(it, 8, 7 + j))
                        pe.wait_ge(q_laid[j], at(it, 128, 128))
                        pe.wait_ge(k_laid[j], at(it, 128, 128))
                        for par in range(2):
                            nc.tensor.matmul(pj[j % 2][:, par, :], ident_b[:], mask[:], start=True, stop=True)
                        for ch in range(2):
                            for g in range(GROUPS):
                                for w in range(4):
                                    for par in range(2):
                                        r = slice(64 * par, 64 * par + 64)
                                        at_w = 32 * (4 * g + w)
                                        col = (g * 2 + ch) * 64
                                        last = nc.tensor.matmul(
                                            pj[j % 2][32 * w:32 * w + 32, par, col:col + 64],
                                            q_t[r, 2 * j + ch, at_w:at_w + 32], k_t[r, 2 * j + ch, at_w:at_w + 64],
                                            start=False, stop=True,
                                            skip_group_check=True)
                        last.then_inc(scored, 1)

                    def shift(j):
                        pe.wait_ge(maxed, at(it, QUADS, j + 1))
                        for par in range(2):
                            last = nc.tensor.matmul(
                                pj[j % 2][:, par, :].rearrange("p (c k) -> p c k", k=64), ident_r[:],
                                negmax[:, j % 2, 8 * par:8 * par + 8].unsqueeze(2).broadcast_to([P, 8, 64]),
                                start=False, stop=True, skip_group_check=True)
                        last.then_inc(shifted, 1)

                    def turn(j):
                        pe.wait_ge(probs_set, at(it, QUADS, j + 1))
                        p4 = prob[:, j % 2, :].rearrange("p (a g k) -> p a g k", a=2, g=GROUPS)
                        for par in range(2):
                            n = 2 * j + par
                            if n >= 4:
                                pe.wait_ge(turned_out, at(it, 8, n - 3))
                            for g in range(GROUPS):
                                last = nc.tensor.transpose(one[n % 4][:, g * P:(g + 1) * P], p4[:, par, g, :],
                                                           ident[:])
                            last.then_inc(turned, 1)

                    for j in range(QUADS):
                        scores(j)
                        shift(j)
                        if j:
                            turn(j - 1)
                    turn(QUADS - 1)
                    pe.wait_ge(turned_out, at(it, 8, 8))
                    pe.wait_ge(z_set, at(it, QUADS, QUADS))
                    for w in range(16):
                        if w >= 2:
                            s = mixed_v if w % 2 else mixed_a
                            pe.wait_ge(s, at(it, 8, w // 2))
                        for ch in range(2):
                            r = slice(64 * ch, 64 * ch + 64)
                            cols = (w // 4) * P + 32 * (w % 4)
                            last = nc.tensor.matmul(
                                pj[w % 2][:, ch, 0:256].rearrange("p (j a n) -> p j a n", j=QUADS, a=2),
                                xw[r, w + 2 * (1 - ch), :], prob_t[r, :, :, cols:cols + 32], start=True, stop=True)
                        last.then_inc(mixed, 1)
                    pe.wait_ge(mixed_a, at(it, 8, 8))
                    pe.wait_ge(mixed_v, at(it, 8, 8))
                    for n in range(16):
                        ch, jp = n // 8, n % 8
                        last = nc.tensor.matmul(one[0], w_vo[:, jp % 2, 2 * (jp // 2) + ch, :], y_t[:, ch, jp, :],
                                                start=(n == 0), stop=(n == 15))
                    last.then_inc(attended, 1)
                    pe.wait_ge(x1_set, at(it, 1, 1))
                    nc.tensor.matmul(one[1], mean_w[:], xs2, start=True, stop=True).then_inc(meaned, 1)
                    pe.wait_ge(csq, at(it, 1, 1))
                    nc.tensor.matmul(one[2], mean_w[:], xsq, start=True, stop=True).then_inc(vared, 1)
                    pe.wait_ge(dve_ln, at(it, 3, 3))
                    for n in range(3):
                        if n >= 2:
                            pe.wait_ge(hid_set, at(it, 3, n - 1))
                        for half in range(2):
                            last = nc.tensor.matmul(pj[n % 2][:, half, :], w1[:, 3 * half + n, :], xn, start=True,
                                                    stop=True)
                        last.then_inc(h_sum, 1)
                    pe.wait_ge(hid_set, at(it, 3, 3))
                    for n in range(3):
                        last = nc.tensor.matmul(one[3], w2[:, n, :], hid[:, n, :], start=(n == 0), stop=(n == 2))
                    last.then_inc(out_sum, 1)

def add_and_store(nc, c, x2, state, out):
    with ExitStack() as ctx:
        ident = ctx.enter_context(nc.sbuf_tensor("o_ident", [P, P], F32))
        x = ctx.enter_context(nc.sbuf_tensor("o_x", [P, 2, GROUPS, DIM], F32))
        s_t = ctx.enter_context(nc.sbuf_tensor("o_s", [P, 2, NT], F32))
        turned = ctx.enter_context(nc.psum_tensor("o_turned", [P, 2, NT], F32))
        consts_in, loaded, turned_in, added, stored = (ctx.enter_context(nc.semaphore("o_" + n)) for n in (
            "consts_in", "loaded", "turned_in", "added", "stored"))
        slot_loaded = [loaded, ctx.enter_context(nc.semaphore("o_loaded1"))]
        slot_stored = [stored, ctx.enter_context(nc.semaphore("o_stored1"))]
        block = ctx.enter_context(nc.Block())

        @block.sync
        def _(sp):
            sp.dma_start(ident[:], c[:, C_IDENT[0]:C_IDENT[1]]).then_inc(consts_in, 16)
            for pair in range(PAIRS):
                k = pair % 2
                if pair >= 2:
                    sp.wait_ge(slot_stored[k], 16 * (pair // 2))
                sp.dma_start(x[:, k], x2[2 * pair:2 * pair + 2].rearrange("s (t p) n -> p (s t) n", p=P))\
                    .then_inc(slot_loaded[k], 16)
                sp.dma_start(s_t[:, k, :], state[:, pair * NT:(pair + 1) * NT]).then_inc(slot_loaded[k], 16)
            for k in range(2):
                sp.wait_ge(slot_stored[k], 16 * (PAIRS // 2))

        @block.tensor
        def _(pe):
            pe.wait_ge(consts_in, 16)
            for pair in range(PAIRS):
                k = pair % 2
                pe.wait_ge(slot_loaded[k], 32 * (pair // 2 + 1))
                if pair >= 2:
                    pe.wait_ge(added, pair - 1)
                for g in range(GROUPS):
                    last = nc.tensor.transpose(turned[:, k, g * P:(g + 1) * P], s_t[:, k, g * P:(g + 1) * P], ident[:])
                last.then_inc(turned_in, 1)

        @block.vector
        def _(dve):
            for pair in range(PAIRS):
                k = pair % 2
                dve.wait_ge(turned_in, pair + 1)
                dve.wait_ge(slot_loaded[k], 32 * (pair // 2 + 1))
                nc.vector.tensor_tensor(out=x[:, k].rearrange("p g n -> p (g n)"), in0=turned[:, k, :],
                                        in1=x[:, k].rearrange("p g n -> p (g n)"), op=ALU.add).then_inc(added, 1)

        @block.scalar
        def _(act):
            for pair in range(PAIRS):
                k = pair % 2
                act.wait_ge(added, pair + 1)
                act.dma_start(out[2 * pair:2 * pair + 2].rearrange("s (t p) n -> p (s t) n", p=P), x[:, k])\
                    .then_inc(slot_stored[k], 16)

def kernel(**inputs):
    import numpy as np
    import concourse.bacc as bacc
    from concourse.bass_utils import run_bass_kernel_spmd

    arrays = {
        "x": np.ascontiguousarray(inputs["x"]),
        "ctx_t": np.ascontiguousarray(np.asarray(inputs["ctx_512"]).transpose(0, 2, 1)),
        "w_attn": attention_weights(np, inputs),
        "w_layers": layer_weights(np, inputs),
        "consts": constants(np),
    }
    nc = bacc.Bacc("TRN2", target_bir_lowering=False, num_devices=1)
    d = {n: nc.dram_tensor(n, a.shape, mybir.dt.from_np(a.dtype), kind="ExternalInput").ap()
         for n, a in arrays.items()}
    out = nc.dram_tensor("out", (B, T, DIM), F32, kind="ExternalOutput").ap()
    x2 = nc.dram_tensor("x2", (B, T, DIM), F32).ap()
    state = nc.dram_tensor("state", (DIM, B * T), F32).ap()
    attention_blocks(nc, d["consts"], d["x"], d["ctx_t"], d["w_attn"], x2, state)
    transformer_layers(nc, d["consts"], d["w_layers"], state)
    add_and_store(nc, d["consts"], x2, state, out)
    return run_bass_kernel_spmd(nc, [arrays], core_ids=[0]).results[0]["out"]
```

```python
from contextlib import ExitStack

import concourse.bass as bass
from concourse import mybir

P = 128
B, T, DIM = 16, 256, 128
DEPTH, HEADS, DIM_HEAD, WINDOW = 6, 16, 64, 32
INNER = HEADS * DIM_HEAD
DIM_INNER = int(DIM * 4 * 2 / 3)
NT = 2 * T
PAIRS = B // 2
QUADS = HEADS // 4
GROUPS = NT // P
FRONT = 3 * WINDOW
QK_SCALE = 8.0
LN_EPS = 1e-5
MASKED = -1e30
VEC = 16

def spans(*widths):
    out, at = [], 0
    for w in widths:
        out.append((at, at + w))
        at += w
    return out

W_QK, W_V, W_O, W_1, W_2, W_VEC = spans(2 * INNER, INNER, INNER, 6 * P, 3 * P, VEC)
W_COLS = W_VEC[1]
C_IDENT, C_MEAN, C_MASK, C_SUM, C_SPREAD, C_TRIG, C_CAUSAL, C_HEAD = spans(P, P, 512, 64, QUADS * P, 4 * T, 384, 4)
C_COLS = C_HEAD[1]
A_SELF, A_CQ, A_CK, A_CV, A_BP, A_BIAS = 4, 8, 9, 10, 11, 12 * P
B_ZERO, B_Q, B_K, B_V, B_CQ, B_CK, B_CV = range(7)
A_COLS = A_BIAS + 8

F32 = mybir.dt.float32
ALU = mybir.AluOpType
ACT = mybir.ActivationFunctionType
AX = mybir.AxisListType

def layer_weights(np, inp):
    wqkv = np.asarray(inp["L0_ffn_Wqkv"])
    w = np.zeros((DEPTH, P, W_COLS), np.float32)
    for t, third in ((0, 1), (1, 0)):
        part = wqkv[:, :, third * INNER:(third + 1) * INNER].reshape(DEPTH, DIM, QUADS, 4, 2, 32)
        w[:, :, W_QK[0] + t * INNER:W_QK[0] + (t + 1) * INNER] = \
            part.transpose(0, 1, 2, 4, 3, 5).reshape(DEPTH, DIM, INNER)
    wv = wqkv[:, :, 2 * INNER:].reshape(DEPTH, DIM, 8, P)
    w[:, :, W_V[0]:W_V[1]] = wv.transpose(0, 3, 2, 1).reshape(DEPTH, P, INNER)
    wo = np.asarray(inp["L0_ffn_Wo"]).reshape(DEPTH, 8, P, DIM)
    w[:, :, W_O[0]:W_O[1]] = wo.transpose(0, 2, 1, 3).reshape(DEPTH, P, INNER)
    for half in range(2):
        at = W_1[0] + half * 3 * P
        w[:, :, at:at + DIM_INNER] = np.asarray(inp["L0_ffn_W1"])[:, :, half * DIM_INNER:(half + 1) * DIM_INNER]
        b = np.zeros((DEPTH, 3 * P), np.float32)
        b[:, :DIM_INNER] = np.asarray(inp["L0_ffn_b1"])[:, half * DIM_INNER:(half + 1) * DIM_INNER]
        w[:, :, W_VEC[0] + 6 + 3 * half:W_VEC[0] + 9 + 3 * half] = b.reshape(DEPTH, 3, P).transpose(0, 2, 1)
    w2 = np.zeros((DEPTH, 3 * P, DIM), np.float32)
    w2[:, :DIM_INNER] = np.asarray(inp["L0_ffn_W2"])
    w[:, :, W_2[0]:W_2[1]] = w2.reshape(DEPTH, 3, P, DIM).transpose(0, 2, 1, 3).reshape(DEPTH, P, 3 * DIM)
    for t, name in ((0, "L0_ffn_k_scale"), (1, "L0_ffn_q_scale")):
        s = np.asarray(inp[name]).reshape(DEPTH, 1, 2, 32)
        w[:, :, W_VEC[0] + 2 * t:W_VEC[0] + 2 * t + 2] = \
            np.broadcast_to(s, (DEPTH, 4, 2, 32)).transpose(0, 1, 3, 2).reshape(DEPTH, P, 2)
    for n, name in ((4, "L0_ffn_ln_g"), (5, "L0_ffn_ln_b"), (12, "L0_ffn_b2")):
        w[:, :, W_VEC[0] + n] = np.asarray(inp[name])
    return np.concatenate([w, np.zeros((1, P, W_COLS), np.float32)])

def constants(np):
    c = np.zeros((P, C_COLS), np.float32)
    c[:, C_IDENT[0]:C_IDENT[1]] = np.eye(P)
    c[:, C_MEAN[0]:C_MEAN[1]] = 1.0 / DIM
    r, s = np.arange(P)[:, None] % 32, np.arange(32)[None, :]
    before = np.where(s >= r, 0.0, MASKED)
    first = np.where(np.arange(P)[:, None] < 32, MASKED, before)
    own = np.where(s <= r, 0.0, MASKED)
    per_group = [np.concatenate([first if g % 2 == 0 else before, own] * 2, 1) for g in range(GROUPS)]
    c[:, C_MASK[0]:C_MASK[1]] = np.concatenate(per_group, 1)
    head = np.arange(P) // 32
    for i in range(4):
        c[head == i, C_SUM[0] + 4 + i] = 1.0
        c[head == i, C_SUM[0] + 32 + i] = 1.0
        for j in range(QUADS):
            c[32 * j + 4 + i, C_SPREAD[0] + j * P + 32 * i:C_SPREAD[0] + j * P + 32 * i + 32] = 1.0
    q, k = np.arange(P)[:, None], np.arange(P)[None, :]
    causal = np.where(k > q, MASKED, 0.0)
    c[:, C_CAUSAL[0]:C_CAUSAL[1]] = np.concatenate([causal, np.zeros((P, P)), causal], 1)
    for n in range(4):
        c[(np.arange(P) // 8) % 4 == n, C_HEAD[0] + n] = 1.0
    f32 = np.float32
    half = np.arange(0, DIM_HEAD, 2, dtype=f32)
    inv_freq = (f32(1.0) / f32(10000.0) ** (half / f32(DIM_HEAD))).astype(f32)
    t = np.arange(T, dtype=f32)
    freqs = (t[:, None] * inv_freq[None, :]).astype(f32)
    base = ((half + f32(0.4 * DIM_HEAD)) / f32(1.4 * DIM_HEAD)).astype(f32)
    power = (t - T // 2) / f32(WINDOW // 2)
    scale = (base[None, :] ** power[:, None]).astype(f32)
    rows = [np.cos(freqs) * scale, np.sin(freqs) * scale, np.cos(freqs) / scale, np.sin(freqs) / scale]
    c[:, C_TRIG[0]:C_TRIG[1]] = np.concatenate([np.tile(x.T.astype(f32), (4, 1)) for x in rows], 1)
    return c

def attention_weights(np, inp):
    w = np.zeros((P, A_COLS), np.float32)
    for n, name in enumerate(("Wq", "Wk", "Wv", "Wo")):
        w[:, n * P:(n + 1) * P] = np.asarray(inp["L0_attn_" + name]).T
    for n, name in ((4, "Wq"), (5, "Wk"), (6, "Wv"), (7, "Wp"), (A_CQ, "Wcq"), (A_CK, "Wck"), (A_CV, "Wcv")):
        m = np.asarray(inp["L0_xattn_" + name])
        w[:m.shape[0], n * P:(n + 1) * P] = m
    w[0, A_BP * P:(A_BP + 1) * P] = np.asarray(inp["L0_xattn_bp"])
    for n, name in ((B_Q, "bq"), (B_K, "bk"), (B_V, "bv"), (B_CQ, "bcq"), (B_CK, "bck"), (B_CV, "bcv")):
        w[:, A_BIAS + n] = np.asarray(inp["L0_xattn_" + name])
    return w

def attention_blocks(nc, c, x_in_dram, ctx_dram, w_attn, x2, state):
    BF16, F32R = mybir.dt.bfloat16, mybir.dt.float32r
    UNITS = 20
    BLOCK_END = (7, 11, 19)
    SELF_SCALE = float(1.0 / (DIM // HEADS) ** 0.5)

    with ExitStack() as ctx:
        def sb(name, shape, dt=F32):
            return ctx.enter_context(nc.sbuf_tensor("a_" + name, shape, dt))

        def sem(name):
            return ctx.enter_context(nc.semaphore("a_" + name))

        w = sb("w", [P, A_COLS])
        ident = sb("ident", [P, P])
        ident_r = sb("ident_r", [P, P], F32R)
        ident_b = sb("ident_b", [P, P], BF16)
        ones = sb("ones", [P, P])
        causal32 = sb("causal32", [P, 384])
        causal = sb("causal", [P, 384], BF16)
        head_of = sb("head_of", [P, 4])
        bias_v = sb("bias_v", [P, 2])
        bias_cq = sb("bias_cq", [P, 4])
        x = sb("x", [P, 2, DIM])
        x_mid = sb("x_mid", [P, 2, DIM])
        x_out = sb("x_out", [P, 2, DIM])
        stats = sb("stats", [P, 2, 6])
        moments = sb("moments", [P, 2, 2])
        rstd = sb("rstd", [P, 2])
        xn = sb("xn", [P, 2, DIM])
        h_t = sb("h_t", [P, T])
        ctx_t = sb("ctx_t", [64, P])
        q_m = sb("q_m", [P, 4, T])
        qc_m = sb("qc_m", [P, 4, T])
        k_t = sb("k_t", [P, T])
        kc_t = sb("kc_t", [P, 64])
        v_a = sb("v_a", [P, 2, HEADS, 32])
        vc_a = sb("vc_a", [P, HEADS, 32])
        negmax = sb("negmax", [P, 2, 8], F32R)
        prob = sb("prob", [P, 2, 2, 384])
        prob_t = sb("prob_t", [P, 2, 2, 384])
        o_t = sb("o_t", [P, 4, T])
        rden = sb("rden", [P, 32])
        o_n = sb("o_n", [P, 2, DIM])
        o_c = sb("o_c", [P, 2, DIM])
        on_t = sb("on_t", [P, T])

        bank = [ctx.enter_context(nc.psum_tensor(f"a_ps{i}", [P, 2, 512], F32)) for i in range(4)]
        p_prob, p_out = bank[2], bank[3]

        consts_in, consts_set, pads_set, ones_set = (sem(n) for n in ("consts_in", "consts_set", "pads_set", "ones_set"))
        x_in, x_free, stored = sem("x_in"), sem("x_free"), sem("stored")
        moment, rooted, normed, h_sum, h_set = (sem(n) for n in ("moment", "rooted", "normed", "h_sum", "h_set"))
        projected, operands, operands_a = sem("projected"), sem("operands"), sem("operands_a")
        scored, maxed, shifted, exped, turned, turned_out, mixed = (sem(n) for n in (
            "scored", "maxed", "shifted", "exped", "turned", "turned_out", "mixed"))
        o_out, o_turned, o_inv, o_normed, on_sum, on_set, y_sum, y_set = (sem(n) for n in (
            "o_out", "o_turned", "o_inv", "o_normed", "on_sum", "on_set", "y_sum", "y_set"))

        block = ctx.enter_context(nc.Block())

        def at(it, per, n):
            return it * per + (n + 1)

        def weight(n):
            return w[:, n * P:(n + 1) * P]

        def bias(n):
            return w[:, A_BIAS + n:A_BIAS + n + 1]

        def is_cross(u):
            return 8 <= u < 12

        def shape_of(u):
            return (1, 512) if is_cross(u) else (2, 384)

        @block.sync
        def _(sp):
            for dst, a, b in ((ident[:], *C_IDENT), (causal32[:], *C_CAUSAL), (head_of[:], *C_HEAD)):
                sp.dma_start(dst, c[:, a:b]).then_inc(consts_in, 16)
            sp.dma_start(w[:], w_attn).then_inc(consts_in, 16)
            sp.sem_inc(x_in, 1)
            with sp.Fori(0, B) as it:
                sp.wait_ge(x_free, at(it, 1, 0))
                sp.dma_start(x[:], x_in_dram[it].rearrange("(t p) n -> p t n", t=2)).then_inc(x_in, 16)
                for n in range(2):
                    sp.dma_start(ctx_t[:, 64 * n:64 * n + 64], ctx_dram[it]).then_inc(x_in, 16)
            sp.wait_ge(stored, at(B, 32, 0))

        @block.gpsimd
        def _(pool):
            nc.gpsimd.memset(ones[:], 1.0)
            nc.gpsimd.memset(v_a[:], 0.0)
            nc.gpsimd.memset(vc_a[:], 0.0).then_inc(pads_set, 1)
            pool.wait_ge(pads_set, 1)
            nc.gpsimd.memset(v_a[:, :, :, 8:9], 1.0).then_inc(pads_set, 1)
            pool.wait_ge(pads_set, 2)
            nc.gpsimd.memset(vc_a[0:64, 0::2, 8:9], 1.0).then_inc(ones_set, 1)
            pool.wait_ge(ones_set, 1)
            nc.gpsimd.memset(vc_a[64:P, 1::2, 8:9], 1.0).then_inc(ones_set, 1)

        @block.scalar
        def _(act):
            act.wait_ge(consts_in, 64)
            nc.scalar.copy(ident_r[:], ident[:]).then_inc(consts_set, 1)
            nc.scalar.copy(ident_b[:], ident[:]).then_inc(consts_set, 1)
            nc.scalar.copy(causal[:], causal32[:]).then_inc(consts_set, 1)
            act.wait_ge(consts_set, 5)
            for s in (rooted, h_set, operands_a, exped, turned_out, on_set, stored):
                act.sem_inc(s, 1)
            with act.Fori(0, B) as it:
                def norm_and_turn(r):
                    act.wait_ge(moment, at(it, 3, r + 1))
                    nc.scalar.activation(rstd[:], rstd[:], ACT.Sqrt).then_inc(rooted, 1)
                    act.wait_ge(h_sum, at(it, 3, r + 1))
                    if r == 0:
                        act.wait_ge(stored, at(it, 32, 0))
                    nc.scalar.copy(h_t[:], p_prob[:, 0, 0:T]).then_inc(h_set, 1)

                def units(first, last):
                    def copy_out(u):
                        if is_cross(u) or u % 2:
                            act.wait_ge(turned, at(it, UNITS, u + 1))
                            if u >= 2:
                                act.wait_ge(mixed, at(it, UNITS, u - 1))
                            n, k = shape_of(u)
                            if is_cross(u):
                                nc.scalar.copy(prob_t[:, u % 2].rearrange("p a b -> p (a b)")[:, 0:512],
                                               p_prob[:, u % 2, :]).then_inc(turned_out, 1)
                            else:
                                nc.scalar.copy(prob_t[:, u % 2], p_prob[:, :, 0:384]).then_inc(turned_out, 1)

                    for u in range(first, last):
                        n, k = shape_of(u)
                        if u > first:
                            copy_out(u - 1)
                        act.wait_ge(shifted, at(it, UNITS, u + 1))
                        if u >= 2:
                            act.wait_ge(turned, at(it, UNITS, u - 1))
                        out = prob[:, u % 2].rearrange("p a b -> p (a b)")[:, 0:n * k] \
                            .rearrange("p (a b) -> p a b", a=n)
                        nc.scalar.activation(out, bank[u % 2][:, 0:n, 0:k], ACT.Exp, scale=SELF_SCALE)\
                            .then_inc(exped, 1)
                    copy_out(last - 1)

                def take_projections(blk):
                    act.wait_ge(projected, at(it, 2, blk + 1))
                    for t in range(2):
                        last = nc.scalar.copy(v_a[:, t, :, 0:8],
                                              p_out[:, 1, t * P:(t + 1) * P].rearrange("p (h d) -> p h d", d=8))
                    if blk:
                        for n in range(4):
                            last = nc.scalar.activation(qc_m[:, n, :], p_out[:, 1, T:2 * T], ACT.Identity,
                                                        bias=bias_cq[:, n:n + 1], scale=head_of[:, n:n + 1])
                    last.then_inc(operands_a, 1)

                norm_and_turn(0)
                take_projections(0)
                units(0, 8)
                act.wait_ge(on_sum, at(it, 2, 1))
                nc.scalar.activation(on_t[:], p_prob[:, 0, 0:T], ACT.Identity, bias=bias_v[:, 0:1])\
                    .then_inc(on_set, 1)
                norm_and_turn(1)
                take_projections(1)
                units(8, 12)
                units(12, 20)
                act.wait_ge(on_sum, at(it, 2, 2))
                nc.scalar.activation(on_t[:], p_prob[:, 0, 0:T], ACT.Identity, bias=bias_v[:, 1:2])\
                    .then_inc(on_set, 1)
                act.wait_ge(moment, at(it, 3, 3))
                nc.scalar.activation(rstd[:], rstd[:], ACT.Sqrt).then_inc(rooted, 1)
                act.wait_ge(h_sum, at(it, 3, 3))
                nc.scalar.copy(h_t[:], p_prob[:, 0, 0:T]).then_inc(h_set, 1)
                act.dma_start(x2[it].rearrange("(t p) n -> p t n", t=2), x_out[:]).then_inc(stored, 16)
                act.wait_ge(h_set, at(it, 3, 3))
                act.dma_start(state[:, bass.ts(it, T)], h_t[:]).then_inc(stored, 16)

        @block.vector
        def _(dve):
            for s in (x_free, moment, normed, operands, maxed, turned_out, o_out, o_inv, o_normed, y_set):
                if s is not turned_out:
                    dve.sem_inc(s, 1)
            dve.wait_ge(consts_in, 64)
            dve.wait_ge(ones_set, 2)
            nc.vector.memset(bias_v[:, 0:1], 0.0)
            nc.vector.tensor_scalar(bias_cq[:], head_of[:], bias(B_CQ), None, ALU.mult).then_inc(consts_set, 1)
            nc.vector.tensor_tensor(out=bias_v[:, 1:2], in0=bias(B_V), in1=bias(B_CV), op=ALU.add)\
                .then_inc(consts_set, 1)
            with dve.Fori(0, B) as it:
                def norm(r, src):
                    steps = at(it, 9, 3 * r)
                    for t in range(2):
                        last = nc.vector.bn_stats(stats[:, t, :], src[:, t, :])
                    last.then_inc(normed, 1)
                    dve.wait_ge(normed, steps + 1)
                    nc.vector.memset(rstd[:], LN_EPS)
                    for t in range(2):
                        last = nc.vector.bn_aggr(moments[:, t, :], stats[:, t, :])
                    last.then_inc(normed, 1)
                    dve.wait_ge(normed, steps + 2)
                    nc.vector.tensor_tensor(out=rstd[:], in0=moments[:, :, 1:2].rearrange("p t o -> p (t o)"),
                                            in1=rstd[:], op=ALU.add).then_inc(moment, 1)
                    dve.wait_ge(rooted, at(it, 3, r + 1))
                    nc.vector.reciprocal(rstd[:], rstd[:]).then_inc(o_inv, 1)
                    dve.wait_ge(o_inv, at(it, 6, (1, 3, 6)[r]))
                    for t in range(2):
                        last = nc.vector.tensor_scalar(xn[:, t, :], src[:, t, :], moments[:, t, 0:1],
                                                       rstd[:, t:t + 1], ALU.subtract, ALU.mult)
                    last.then_inc(normed, 1)

                def heads(out, src, b):
                    for n in range(4):
                        last = nc.vector.tensor_scalar(out[:, n, :], src, b, head_of[:, n:n + 1], ALU.add, ALU.mult)
                    return last

                def take_projections(blk):
                    dve.wait_ge(projected, at(it, 2, blk + 1))
                    heads(q_m, p_out[:, 0, 0:T], bias(B_Q if blk else B_ZERO))
                    last = nc.vector.tensor_scalar(k_t[:], p_out[:, 0, T:2 * T], bias(B_K if blk else B_ZERO), None,
                                                   ALU.add)
                    if blk:
                        nc.vector.tensor_scalar(kc_t[:], p_prob[:, 1, 0:64], bias(B_CK), None, ALU.add)
                        for n in range(2):
                            r = slice(64 * n, 64 * n + 64)
                            last = nc.vector.tensor_copy(
                                vc_a[r, n::2, 0:8], p_prob[r, 1, P:2 * P].rearrange("p (h d) -> p h d", d=8)[:, n::2])
                    last.then_inc(operands, 1)

                def units(first, last):
                    def copy_out(u):
                        if not is_cross(u) and u % 2 == 0:
                            dve.wait_ge(turned, at(it, UNITS, u + 1))
                            if u >= 2:
                                dve.wait_ge(mixed, at(it, UNITS, u - 1))
                            nc.vector.tensor_copy(prob_t[:, u % 2], p_prob[:, :, 0:384]).then_inc(turned_out, 1)

                    for u in range(first, last):
                        dve.wait_ge(scored, at(it, UNITS, u + 1))
                        if u >= 2:
                            dve.wait_ge(shifted, at(it, UNITS, u - 1))
                        if is_cross(u):
                            nc.vector.tensor_reduce(negmax[:, u % 2, :],
                                                    bank[u % 2][:, 0, :].rearrange("p (c k) -> p c k", k=64), AX.X,
                                                    ALU.max, negate=True).then_inc(maxed, 1)
                        else:
                            nc.vector.tensor_reduce(negmax[:, u % 2, 0:2], bank[u % 2][:, :, 0:P], AX.X, ALU.max,
                                                    negate=True)
                            nc.vector.tensor_reduce(negmax[:, u % 2, 2:4], bank[u % 2][:, :, P:384], AX.X, ALU.max,
                                                    negate=True).then_inc(maxed, 1)
                        if u > first:
                            copy_out(u - 1)
                    copy_out(last - 1)

                def take_outputs(n, out):
                    dve.wait_ge(mixed, at(it, UNITS, BLOCK_END[n] + 1))
                    nc.vector.tensor_copy(o_t[:].rearrange("p a b -> p (a b)"), p_out[:].rearrange("p a b -> p (a b)"))\
                        .then_inc(o_out, 1)
                    dve.wait_ge(o_turned, at(it, 3, n + 1))
                    o = p_prob[:].rearrange("p a (h k) -> p (a h) k", k=32)
                    nc.vector.reciprocal(rden[:], o[:, :, 8:9].rearrange("p a b -> p (a b)")).then_inc(o_inv, 1)
                    dve.wait_ge(o_inv, at(it, 6, (2, 4, 5)[n]))
                    nc.vector.tensor_tensor(out=out[:].rearrange("p t (h d) -> p (t h) d", d=8), in0=o[:, :, 0:8],
                                            in1=rden[:].unsqueeze(2).broadcast_to([P, 32, 8]), op=ALU.mult)\
                        .then_inc(o_normed, 1)

                dve.wait_ge(x_in, at(it, 48, 48))
                norm(0, x)
                take_projections(0)
                units(0, 8)
                take_outputs(0, o_n)
                dve.wait_ge(y_sum, at(it, 2, 1))
                nc.vector.tensor_tensor(out=x_mid[:].rearrange("p t n -> p (t n)"), in0=p_prob[:, 1, 0:T],
                                        in1=x[:].rearrange("p t n -> p (t n)"), op=ALU.add).then_inc(y_set, 1)
                dve.wait_ge(y_set, at(it, 2, 1))
                norm(1, x_mid)
                take_projections(1)
                dve.sem_inc(x_free, 1)
                units(8, 12)
                take_outputs(1, o_c)
                units(12, 20)
                take_outputs(2, o_n)
                dve.wait_ge(o_normed, at(it, 4, 3))
                nc.vector.tensor_tensor(out=o_n[:], in0=o_n[:], in1=o_c[:], op=ALU.add).then_inc(o_normed, 1)
                dve.wait_ge(y_sum, at(it, 2, 2))
                dve.wait_ge(stored, at(it, 32, 0))
                nc.vector.tensor_tensor(out=x_out[:].rearrange("p t n -> p (t n)"), in0=p_prob[:, 1, 0:T],
                                        in1=x_mid[:].rearrange("p t n -> p (t n)"), op=ALU.add).then_inc(y_set, 1)
                dve.wait_ge(y_set, at(it, 2, 2))
                norm(2, x_out)

        @block.tensor
        def _(pe):
            for s in (h_sum, projected, scored, shifted, turned, mixed, o_turned, on_sum, y_sum):
                pe.sem_inc(s, 1)
            pe.wait_ge(consts_in, 64)
            pe.wait_ge(consts_set, 5)
            pe.wait_ge(ones_set, 2)
            with pe.Fori(0, B) as it:
                def turn_tokens(r):
                    pe.wait_ge(normed, at(it, 9, 3 * r + 3))
                    for t in range(2):
                        last = nc.tensor.transpose(p_prob[:, 0, t * P:(t + 1) * P], xn[:, t, :], ident[:])
                    last.then_inc(h_sum, 1)

                def project(blk):
                    pe.wait_ge(h_set, at(it, 3, blk + 1))
                    wq, wk, wv = (weight(n + (A_SELF if blk else 0)) for n in range(3))
                    nc.tensor.matmul(p_out[:, 0, 0:T], wq, h_t[:], start=True, stop=True)
                    nc.tensor.matmul(p_out[:, 0, T:2 * T], wk, h_t[:], start=True, stop=True)
                    for t in range(2):
                        last = nc.tensor.matmul(p_out[:, 1, t * P:(t + 1) * P], h_t[:, t * P:(t + 1) * P], wv,
                                                start=True, stop=True)
                    if blk:
                        nc.tensor.matmul(p_out[:, 1, T:2 * T], weight(A_CQ), h_t[:], start=True, stop=True)
                        nc.tensor.matmul(p_prob[:, 1, 0:64], weight(A_CK)[0:64], ctx_t[:, 0:64], start=True, stop=True)
                        last = nc.tensor.matmul(p_prob[:, 1, P:2 * P], ctx_t[:], weight(A_CV)[0:64], start=True,
                                                stop=True)
                    last.then_inc(projected, 1)
                    pe.wait_ge(operands, at(it, 2, blk + 1))
                    pe.wait_ge(operands_a, at(it, 2, blk + 1))

                def scores(u):
                    s = bank[u % 2]
                    if u >= 2:
                        pe.wait_ge(exped, at(it, UNITS, u - 1))
                    if is_cross(u):
                        g = u - 8
                        r = slice(32 * g, 32 * g + 32)
                        for t in range(2):
                            for n in range(4):
                                col = t * 256 + n * 64
                                last = nc.tensor.matmul(s[:, 0, col:col + 64], qc_m[r, n, t * P:(t + 1) * P],
                                                        kc_t[r, :], start=not col, stop=True,
                                                        skip_group_check=True)
                    else:
                        d = u if u < 8 else u - 12
                        for n in range(2):
                            h = 2 * d + n
                            r = slice(32 * (h // 4), 32 * (h // 4) + 32)
                            q = q_m[r, h % 4, :]
                            nc.tensor.matmul(s[:, n, 0:384], ident_b[:], causal[:], start=True, stop=True)
                            nc.tensor.matmul(s[:, n, 0:P], q[:, 0:P], k_t[r, 0:P], start=False, stop=True,
                                             skip_group_check=True)
                            last = nc.tensor.matmul(s[:, n, P:384], q[:, P:T], k_t[r, :], start=False, stop=True,
                                                    skip_group_check=True)
                    last.then_inc(scored, 1)

                def shift(u):
                    s = bank[u % 2]
                    pe.wait_ge(maxed, at(it, UNITS, u + 1))
                    if is_cross(u):
                        last = nc.tensor.matmul(s[:, 0, :].rearrange("p (c k) -> p c k", k=64), ident_r[:],
                                                negmax[:, u % 2, :].unsqueeze(2).broadcast_to([P, 8, 64]),
                                                start=False, stop=True, skip_group_check=True)
                    else:
                        for n in range(2):
                            for t in range(2):
                                out = s[:, n, P:384] if t else s[:, n, 0:P]
                                m = negmax[:, u % 2, 2 * t + n:2 * t + n + 1]
                                last = nc.tensor.matmul(out, ident_r[:], m.broadcast_to([P, out.shape[1]]),
                                                        start=False, stop=True, skip_group_check=True)
                    last.then_inc(shifted, 1)

                def turn(u):
                    pe.wait_ge(exped, at(it, UNITS, u + 1))
                    if u:
                        pe.wait_ge(turned_out, at(it, UNITS, u))
                    p = prob[:, u % 2].rearrange("p a b -> p (a b)")
                    if is_cross(u):
                        for hp in range(2):
                            for t in range(2):
                                last = nc.tensor.transpose(p_prob[:, u % 2, (2 * hp + t) * P:(2 * hp + t + 1) * P],
                                                           p[:, t * 256 + hp * P:t * 256 + (hp + 1) * P], ident[:])
                    else:
                        for n in range(2):
                            for b in range(3):
                                last = nc.tensor.transpose(p_prob[:, n, b * P:(b + 1) * P],
                                                           p[:, n * 384 + b * P:n * 384 + (b + 1) * P], ident[:])
                    last.then_inc(turned, 1)

                def mix(u):
                    pe.wait_ge(turned_out, at(it, UNITS, u + 1))
                    if is_cross(u):
                        g = u - 8
                        pt = prob_t[:, u % 2].rearrange("p a b -> p (a b)")
                        for n in range(4):
                            last = nc.tensor.matmul(p_out[32 * n:32 * n + 32, g // 2, (g % 2) * T:(g % 2 + 1) * T],
                                                    vc_a[:, 4 * g + n, :], pt[:, (n // 2) * T:(n // 2 + 1) * T],
                                                    start=True, stop=True)
                    else:
                        d = u if u < 8 else u - 12
                        for n in range(2):
                            h = 2 * d + n
                            g, rows = h // 4, slice(32 * (h % 4), 32 * (h % 4) + 32)
                            col = (g % 2) * T
                            nc.tensor.matmul(p_out[rows, g // 2, col:col + T], v_a[:, 0, h, :],
                                             prob_t[:, u % 2, n, 0:T], start=True, stop=True)
                            last = nc.tensor.matmul(p_out[rows, g // 2, col + P:col + T], v_a[:, 1, h, :],
                                                    prob_t[:, u % 2, n, T:384], start=False, stop=True,
                                                    skip_group_check=True)
                    last.then_inc(mixed, 1)

                def units(first, last):
                    for u in range(first, last):
                        scores(u)
                        if u > first:
                            turn(u - 1)
                        shift(u)
                        if u > first + 1:
                            mix(u - 2)
                    turn(last - 1)
                    mix(last - 2)
                    mix(last - 1)

                def turn_outputs(n):
                    pe.wait_ge(o_out, at(it, 3, n + 1))
                    for t in range(2):
                        for g in range(4):
                            last = nc.tensor.transpose(p_prob[:, t, g * P:(g + 1) * P], o_t[:, g, t * P:(t + 1) * P],
                                                       ident[:])
                    last.then_inc(o_turned, 1)

                def project_out(blk):
                    pe.wait_ge(o_normed, at(it, 4, 4 if blk else 1))
                    for t in range(2):
                        last = nc.tensor.transpose(p_prob[:, 0, t * P:(t + 1) * P], o_n[:, t, :], ident[:])
                    last.then_inc(on_sum, 1)
                    pe.wait_ge(on_set, at(it, 2, blk + 1))
                    wo = weight(A_SELF + 3 if blk else 3)
                    for t in range(2):
                        out = p_prob[:, 1, t * P:(t + 1) * P]
                        last = nc.tensor.matmul(out, on_t[:, t * P:(t + 1) * P], wo, start=True, stop=not blk)
                        if blk:
                            last = nc.tensor.matmul(out, ones[:], weight(A_BP), start=False, stop=True)
                    last.then_inc(y_sum, 1)

                turn_tokens(0)
                project(0)
                units(0, 8)
                turn_outputs(0)
                project_out(0)
                turn_tokens(1)
                project(1)
                units(8, 12)
                turn_outputs(1)
                pe.wait_ge(o_normed, at(it, 4, 2))
                units(12, 20)
                turn_outputs(2)
                project_out(1)
                turn_tokens(2)

def transformer_layers(nc, c, w_layers, state):
    BF16, F32R = mybir.dt.bfloat16, mybir.dt.float32r

    with ExitStack() as ctx:
        def sb(name, shape, dt=F32):
            return ctx.enter_context(nc.sbuf_tensor("f_" + name, shape, dt))

        def sem(name):
            return ctx.enter_context(nc.semaphore("f_" + name))

        raw = sb("raw", [P, W_COLS])
        wqk_hi = sb("wqk_hi", [P, 2, QUADS, 2, P], F32R)
        wqk_lo = sb("wqk_lo", [P, 2, QUADS, 2, P], F32R)
        w_vo = sb("w_vo", [P, 2, 8, P])
        w1 = sb("w1", [P, 6, P])
        w2 = sb("w2", [P, 3, P])
        vec = sb("vec", [P, VEC])
        b1 = sb("b1", [P, 6])
        trig = sb("trig", [P, 4, T])
        straight = [sb(f"straight{t}", [P, 2, T]) for t in range(2)]
        crossed = [sb(f"crossed{t}", [P, 2, T]) for t in range(2)]
        ident = sb("ident", [P, P])
        ident_r = sb("ident_r", [P, P], F32R)
        ident_b = sb("ident_b", [P, P], BF16)
        mean_w = sb("mean_w", [P, P])
        head_sum = sb("head_sum", [P, 2, 32])
        spread = sb("spread", [P, QUADS, P])
        mask = sb("mask", [P, 512], BF16)
        eps = sb("eps", [P, 1])
        xs = sb("xs", [P, FRONT + NT + 64])
        xs_now = xs[:, FRONT:FRONT + NT]
        xs_hi = sb("xs_hi", [P, NT], F32R)
        xs_lo = sb("xs_lo", [P, NT], F32R)
        xw = sb("xw", [P, 18, P])
        sq = sb("sq", [P, 2, 2, NT])
        rot = sb("rot", [P, QUADS, 2, NT])
        rotq = sb("rotq", [P, 2, 2, NT])
        norm = sb("norm", [P, NT])
        q_t = sb("q_t", [P, 8, NT])
        k_t = sb("k_t", [P, 8, 32 + NT])
        rq = sb("rq", [P, QUADS, 2, GROUPS, 2])
        x = sb("x", [P, NT])
        negmax = sb("negmax", [P, 2, 16], F32R)
        zs = sb("zs", [P, 2, NT * 2])
        mask32 = zs[:, 0, 0:512]
        den = sb("den", [P, 2, 16])
        rden = sb("rden", [P, 2, 16])
        prob = sb("prob", [P, 2, 1024])
        prob_t = sb("prob_t", [P, QUADS, 2, GROUPS * P])
        y_t = sb("y_t", [P, 2, 2, 8, P])
        flat_y = y_t[:].rearrange("p s a b n -> p (s a b n)")
        up = flat_y[:, 0:2048].rearrange("p (s a n) -> p s a n", s=2, a=2)
        vp = flat_y[:, 2048:4096].rearrange("p (s a n) -> p s a n", s=2, a=2)
        hid = flat_y[:, 0:2048].rearrange("p (a n) -> p a n", a=4)
        x1, xs2, xc, xsq, root, xn, xo = (prob_t[:, n // 2, n % 2, :] for n in range(7))
        gate = sq[:].rearrange("p a b n -> p (a b) n")

        bank = [ctx.enter_context(nc.psum_tensor(f"f_ps{i}", [P, 2, 512], F32)) for i in range(4)]
        p_qk = bank[0]
        pj = [bank[1], bank[2]]
        p_sum, p_turn = bank[3][:, 0, :], bank[3][:, 1, :]
        p_att, p_var, p_mean, p_ffn = p_qk[:, 0, :], p_qk[:, 0, :], p_qk[:, 1, :], p_qk[:, 1, :]
        p_spread = [p_sum, p_qk[:, 1, :]]
        p_xw = [p_turn, p_sum]

        x_granted = sem("x_granted")
        consts_in, consts_set = sem("consts_in"), sem("consts_set")
        w_in, hi_made, lo_made, w_tables, w_vo_sum, w_vo_set, w_ready, w_taken = (sem(n) for n in (
            "w_in", "hi_made", "lo_made", "w_tables", "w_vo_sum", "w_vo_set", "w_ready", "w_taken"))
        xs_in, x_in, x_free, x_hi, x_lo, xw_sum, xw_copied = (sem(n) for n in (
            "xs_in", "x_in", "x_free", "x_hi", "x_lo", "xw_sum", "xw_copied"))
        projected, squared, scaled, rotated = (sem(n) for n in ("projected", "squared", "scaled", "rotated"))
        normed2, rooted, guarded, inverse_set, norm_turned, rq_set, spread_out, k_normed = (sem(n) for n in (
            "normed2", "rooted", "guarded", "inverse_set", "norm_turned", "rq_set", "spread_out", "k_normed"))
        q_laid, k_laid = ([sem(f"{n}{j}") for j in range(QUADS)] for n in ("q_laid", "k_laid"))
        scored, maxed, shifted, z_set, exped, summed, inverted, probs_set, turned, turned_out = (sem(n) for n in (
            "scored", "maxed", "shifted", "z_set", "exped", "summed", "inverted", "probs_set", "turned",
            "turned_out"))
        mixed, mixed_a, mixed_v, attended, x1_set, centred, meaned, csq, vared, root_inv, roots, ln_set = (sem(n) for n in (
            "mixed", "mixed_a", "mixed_v", "attended", "x1_set", "centred", "meaned", "csq", "vared", "root_inv", "roots",
            "ln_set"))
        h_sum, gated, hid_set, out_sum, out_set, stored = (sem(n) for n in (
            "h_sum", "gated", "hid_set", "out_sum", "out_set", "stored"))

        block = ctx.enter_context(nc.Block())

        def at(it, per, n):
            return it * per + (n + 1)

        def two(t):
            return t.unsqueeze(1).broadcast_to([P, 2, T])

        def p_turned(m):
            return p_turn if m < 7 else pj[0][:, 0, :]

        @block.sync
        def _(sp):
            for dst, a, b in ((ident[:], *C_IDENT), (mean_w[:], *C_MEAN), (mask32, *C_MASK)):
                sp.dma_start(dst, c[:, a:b]).then_inc(consts_in, 16)
            sp.dma_start(head_sum[:].rearrange("p a b -> p (a b)"), c[:, C_SUM[0]:C_SUM[1]]).then_inc(consts_in, 16)
            sp.dma_start(spread[:].rearrange("p a b -> p (a b)"), c[:, C_SPREAD[0]:C_SPREAD[1]]).then_inc(consts_in, 16)
            sp.dma_start(trig[:].rearrange("p a b -> p (a b)"), c[:, C_TRIG[0]:C_TRIG[1]]).then_inc(consts_in, 16)
            for s in (w_in, xs_in, x_in, *q_laid, *k_laid):
                sp.sem_inc(s, 1)
            sp.wait_ge(consts_set, 6)
            sp.dma_start(raw[:], w_layers[0]).then_inc(w_in, 16)

            def load_shifted(n, cols):
                sp.wait_ge(xw_sum, at(n, 5, 0))
                sp.dma_start(xs_now[0:64, :], cols[0:64, :]).then_inc(xs_in, 16)
                for s in range(2):
                    sp.dma_start(xs_now[64:P, T * s + 1:T * (s + 1)],
                                 cols[64:P, T * s:T * (s + 1) - 1]).then_inc(xs_in, 16)

            def lay_out(n):
                for j in range(QUADS):
                    sp.wait_ge(rotated, at(n, 8, 2 * j + 2))
                    for ab in range(2):
                        for i in range(4):
                            to = 64 * (i % 2) + 32 * ab
                            sp.dma_start(q_t[to:to + 32, 2 * j + i // 2, :],
                                         rotq[32 * i:32 * i + 32, j % 2, ab, :]).then_inc(q_laid[j], 16)
                for j in range(QUADS):
                    sp.wait_ge(k_normed, at(n, QUADS, j + 1))
                    for ab in range(2):
                        for i in range(4):
                            to = 64 * (i % 2) + 32 * ab
                            sp.dma_start(k_t[to:to + 32, 2 * j + i // 2, 32:32 + NT],
                                         rot[32 * i:32 * i + 32, j, ab, :]).then_inc(k_laid[j], 16)

            def turn(it, n, next_cols, cols):
                load_shifted(n, next_cols)
                sp.wait_ge(stored, at(it, 16, 0))
                sp.sem_inc(x_granted, 1)
                sp.wait_ge(x_free, at(it, 1, 0))
                sp.sem_inc(x_granted, 1)
                sp.dma_start(x[:], cols).then_inc(x_in, 16)
                lay_out(n)

            load_shifted(0, state[:, 0:NT])
            lay_out(0)
            with sp.Fori(0, DEPTH) as layer:
                sp.wait_ge(w_taken, at(layer, 1, 1))
                sp.dma_start(raw[:], w_layers[1:DEPTH + 1][layer]).then_inc(w_in, 16)
                with sp.Fori(0, PAIRS - 1) as pair:
                    it = layer * PAIRS + pair
                    turn(it, it + 1, state[:, NT:][:, bass.ts(pair, NT)], state[:, bass.ts(pair, NT)])
                it = layer * PAIRS + (PAIRS - 1)
                turn(it, it + 1, state[:, 0:NT], state[:, (PAIRS - 1) * NT:PAIRS * NT])
            sp.wait_ge(stored, at(DEPTH * PAIRS, 16, 0))
            for s in q_laid + k_laid:
                sp.wait_ge(s, at(DEPTH * PAIRS, 128, 128))

        @block.gpsimd
        def _(pool):
            nc.gpsimd.memset(xs[:], 0.0).then_inc(consts_set, 1)
            nc.gpsimd.memset(k_t[:], 0.0).then_inc(consts_set, 1)
            nc.gpsimd.memset(eps[:], LN_EPS).then_inc(consts_set, 1)
            for s in (rotated, probs_set):
                pool.sem_inc(s, 1)

            def rotate(n, m, it):
                j, t = m // 2, m % 2
                if t and it is not None:
                    pool.wait_ge(scored, at(it, QUADS, j + 1))
                pool.wait_ge(scaled, at(n, 16, 2 * m + 2))
                if t and j >= 2:
                    pool.wait_ge(q_laid[j - 2], at(n, 128, 128))
                elif t:
                    pool.wait_ge(q_laid[j + 2], at(n, 128, 0))
                else:
                    pool.wait_ge(k_laid[j], at(n, 128, 0))
                out = rotq[:, j % 2] if t else rot[:, j]
                nc.gpsimd.tensor_tensor(out=out, in0=up[:, m % 2], in1=vp[:, m % 2, ::-1, :],
                                        op=ALU.add).then_inc(rotated, 1)

            def normalise(it, j):
                pool.wait_ge(inverted, at(it, QUADS, j + 1))
                r = rden[:, j % 2, :].unsqueeze(2).broadcast_to([P, 16, 64])
                p3 = prob[:, j % 2, :].rearrange("p (c k) -> p c k", k=64)
                nc.gpsimd.tensor_tensor(out=p3, in0=p3, in1=r, op=ALU.mult).then_inc(probs_set, 1)

            for m in range(8):
                rotate(0, m, None)
            with pool.Fori(0, DEPTH) as layer:
                with pool.Fori(0, PAIRS) as pair:
                    it = layer * PAIRS + pair
                    for j in range(QUADS):
                        if j:
                            normalise(it, j - 1)
                        rotate(it + 1, 2 * j, it)
                        if j == QUADS - 1:
                            normalise(it, j)
                        rotate(it + 1, 2 * j + 1, it)

        @block.scalar
        def _(act):
            act.wait_ge(consts_in, 16 * 6)
            nc.scalar.copy(ident_r[:], ident[:]).then_inc(consts_set, 1)
            nc.scalar.copy(ident_b[:], ident[:]).then_inc(consts_set, 1)
            nc.scalar.copy(mask[:], mask32).then_inc(consts_set, 1)
            for s in (hi_made, w_vo_set, x_hi, xw_copied, squared, exped, turned_out, mixed_a, csq, roots, rooted,
                      gated, stored):
                act.sem_inc(s, 1)

            def round_weights(layer):
                act.wait_ge(w_in, at(layer, 16, 16))
                nc.scalar.copy(wqk_hi[:].rearrange("p t j a n -> p (t j a n)"), raw[:, W_QK[0]:W_QK[1]])\
                    .then_inc(hi_made, 1)

            def round_inputs(n):
                act.wait_ge(xs_in, at(n, 48, 48))
                nc.scalar.copy(xs_hi[:], xs_now).then_inc(x_hi, 1)

            def square(n, m, it):
                if m >= 2:
                    act.wait_ge(normed2, at(n, 8, m - 1))
                elif it is not None:
                    act.wait_ge(hid_set, at(it, 3, 0))
                for ab in range(2):
                    act.wait_ge(projected, at(n, 16, 2 * m + ab + 1))
                    nc.scalar.activation(sq[:, m % 2, ab], p_qk[:, ab, :], ACT.Square).then_inc(squared, 1)

            def take_norms(n):
                act.wait_ge(normed2, at(n, 8, 8))
                nc.scalar.activation(norm[:], p_sum, ACT.Sqrt).then_inc(rooted, 1)

            def copy_windows(n, ch):
                act.wait_ge(xw_sum, at(n, 5, ch + 1))
                to = xw[:, 4 * ch:min(4 * ch + 4, 18)].rearrange("p w n -> p (w n)")
                nc.scalar.copy(to, p_xw[ch % 2][:, 0:to.shape[1]]).then_inc(xw_copied, 1)

            def copy_turned(it, m):
                act.wait_ge(turned, at(it, 8, m + 1))
                if m == 0:
                    act.wait_ge(stored, at(it, 16, 0))
                nc.scalar.copy(prob_t[:, m // 2, m % 2, :], p_turned(m)).then_inc(turned_out, 1)

            def turn(it, n, cols):
                round_inputs(n)
                for j in range(QUADS):
                    square(n, 2 * j, it)
                    if j:
                        copy_turned(it, 2 * j - 2)
                    act.wait_ge(z_set, at(it, QUADS, j + 1))
                    if j >= 2:
                        act.wait_ge(turned, at(it, 8, 2 * j - 2))
                    nc.scalar.activation(prob[:, j % 2, :], zs[:, j % 2, :], ACT.Exp, scale=QK_SCALE)\
                        .then_inc(exped, 1)
                    square(n, 2 * j + 1, it)
                    if j:
                        copy_turned(it, 2 * j - 1)
                copy_turned(it, 6)
                copy_turned(it, 7)
                take_norms(n)
                act.wait_ge(rotated, at(n, 8, 8))
                for w in range(0, 16, 2):
                    act.wait_ge(mixed, at(it, 16, w + 1))
                    nc.scalar.copy(y_t[:, (w // 4) % 2, :, :, 32 * (w % 4):32 * (w % 4) + 32],
                                   pj[w % 2][:, :, 0:256].rearrange("p a (h n) -> p a h n", n=32))\
                        .then_inc(mixed_a, 1)
                copy_windows(n, 0)
                copy_windows(n, 1)
                act.wait_ge(centred, at(it, 1, 1))
                nc.scalar.activation(xsq, xc, ACT.Square).then_inc(csq, 1)
                copy_windows(n, 2)
                act.wait_ge(vared, at(it, 1, 1))
                nc.scalar.activation(root, p_var, ACT.Sqrt, bias=eps[:, 0:1]).then_inc(roots, 1)
                copy_windows(n, 3)
                copy_windows(n, 4)
                for m in range(3):
                    act.wait_ge(h_sum, at(it, 3, m + 1))
                    nc.scalar.activation(gate[:, m, :], pj[m % 2][:, 1, :], ACT.Gelu, bias=b1[:, 3 + m:4 + m])\
                        .then_inc(gated, 1)
                act.wait_ge(out_set, at(it, 1, 1))
                act.dma_start(cols, xo).then_inc(stored, 16)

            round_weights(0)
            round_inputs(0)
            for m in range(8):
                square(0, m, None)
            take_norms(0)
            for ch in range(5):
                copy_windows(0, ch)
            with act.Fori(0, DEPTH) as layer:
                for m in range(2):
                    act.wait_ge(w_vo_sum, at(layer, 2, m + 1))
                    nc.scalar.copy(w_vo[:, m].rearrange("p c n -> p (c n)"),
                                   pj[m][:].rearrange("p a n -> p (a n)")).then_inc(w_vo_set, 1)
                with act.Fori(0, PAIRS - 1) as pair:
                    it = layer * PAIRS + pair
                    turn(it, it + 1, state[:, bass.ts(pair, NT)])
                round_weights(layer + 1)
                it = layer * PAIRS + (PAIRS - 1)
                turn(it, it + 1, state[:, (PAIRS - 1) * NT:PAIRS * NT])

        @block.vector
        def _(dve):
            for s in (lo_made, w_tables, w_ready, w_taken, x_free, x_lo, scaled, guarded, inverse_set, root_inv, rq_set, k_normed, maxed,
                      z_set, summed, inverted, mixed_v, x1_set, centred, ln_set, hid_set, out_set):
                dve.sem_inc(s, 1)
            dve.wait_ge(consts_in, 16 * 6)

            def weight_tables(layer):
                dve.wait_ge(w_in, at(layer, 16, 16))
                for t in range(2):
                    base = 2 if t == 0 else 0
                    for ab in range(2):
                        at_s = W_VEC[0] + 2 * t + ab
                        s = raw[:, at_s:at_s + 1]
                        nc.vector.tensor_scalar(straight[t][:, ab, :], trig[:, base, :], s, None, ALU.mult)
                        nc.vector.tensor_scalar(crossed[t][:, ab, :], trig[:, base + 1, :], s,
                                                -1.0 if ab else 1.0, ALU.mult, ALU.mult)
                dve.wait_ge(hi_made, at(layer, 1, 1))
                nc.vector.tensor_tensor(out=wqk_lo[:].rearrange("p t j a n -> p (t j a n)"),
                                        in0=raw[:, W_QK[0]:W_QK[1]],
                                        in1=wqk_hi[:].rearrange("p t j a n -> p (t j a n)").bitcast(F32),
                                        op=ALU.subtract).then_inc(lo_made, 1)
                dve.wait_ge(lo_made, at(layer, 1, 1))

            def split_inputs(n):
                dve.wait_ge(x_hi, at(n, 1, 1))
                nc.vector.tensor_tensor(out=xs_lo[:], in0=xs_now, in1=xs_hi[:].bitcast(F32),
                                        op=ALU.subtract).then_inc(x_lo, 1)

            def scale(n, m):
                t = m % 2
                if m >= 2:
                    dve.wait_ge(rotated, at(n, 8, m - 1))
                for ab in range(2):
                    dve.wait_ge(squared, at(n, 16, 2 * m + ab + 1))
                    src, to_up, to_vp = (a.rearrange("p (s n) -> p s n", s=2)
                                         for a in (p_qk[:, ab, :], up[:, m % 2, ab], vp[:, m % 2, ab]))
                    nc.vector.tensor_tensor(out=to_up, in0=src, in1=two(straight[t][:, ab, :]), op=ALU.mult)
                    nc.vector.tensor_tensor(out=to_vp, in0=src, in1=two(crossed[t][:, ab, :]), op=ALU.mult)\
                        .then_inc(scaled, 1)

            def invert_norms(n):
                dve.wait_ge(rooted, at(n, 1, 1))
                nc.vector.tensor_scalar(norm[:], norm[:], 1e-12, None, ALU.max).then_inc(guarded, 1)
                dve.wait_ge(guarded, at(n, 1, 1))
                nc.vector.reciprocal(norm[:], norm[:]).then_inc(inverse_set, 1)

            def take_q_norms(n):
                dve.wait_ge(norm_turned, at(n, 1, 1))
                for g in range(GROUPS):
                    last = nc.vector.tensor_copy(
                        rq[:, :, :, g, :],
                        p_turn[:, g * P:(g + 1) * P].rearrange("p (j r) -> p j r", j=QUADS)[:, :, 0:4]
                        .rearrange("p j (c a) -> p j a c", a=2))
                last.then_inc(rq_set, 1)

            def norm_k(n, j):
                dve.wait_ge(spread_out, at(n, QUADS, j + 1))
                dve.wait_ge(rotated, at(n, 8, 2 * j + 1))
                nc.vector.tensor_tensor(out=rot[:, j], in0=rot[:, j],
                                        in1=p_spread[j % 2].unsqueeze(1).broadcast_to([P, 2, NT]),
                                        op=ALU.mult).then_inc(k_normed, 1)

            def turn(it, n):
                def highest(j):
                    dve.wait_ge(scored, at(it, QUADS, j + 1))
                    if j >= 2:
                        dve.wait_ge(shifted, at(it, QUADS, j - 1))
                    nc.vector.tensor_reduce(negmax[:, j % 2, :].rearrange("p (a c) -> p a c", a=2),
                                            pj[j % 2][:].rearrange("p a (c k) -> p a c k", k=64), AX.X,
                                            ALU.max, negate=True).then_inc(maxed, 1)

                def times_rq(j):
                    dve.wait_ge(shifted, at(it, QUADS, j + 1))
                    if j >= 2:
                        dve.wait_ge(exped, at(it, QUADS, j - 1))
                    nc.vector.tensor_tensor(
                        out=zs[:, j % 2, :].rearrange("p (c k) -> p c k", k=64),
                        in0=pj[j % 2][:].rearrange("p a (c k) -> p (a c) k", k=64),
                        in1=rq[:, j].rearrange("p a g c -> p (a g c)").unsqueeze(2).broadcast_to([P, 16, 64]),
                        op=ALU.mult).then_inc(z_set, 1)

                def sums(j):
                    dve.wait_ge(exped, at(it, QUADS, j + 1))
                    nc.vector.tensor_reduce(den[:, j % 2, :], prob[:, j % 2, :].rearrange("p (c k) -> p c k", k=64),
                                            AX.X, ALU.add).then_inc(summed, 1)
                    dve.wait_ge(summed, at(it, QUADS, j + 1))
                    if j >= 2:
                        dve.wait_ge(probs_set, at(it, QUADS, j - 1))
                    nc.vector.reciprocal(rden[:, j % 2, :], den[:, j % 2, :]).then_inc(inverted, 1)

                def copy_mix(w):
                    dve.wait_ge(mixed, at(it, 16, w + 1))
                    nc.vector.tensor_copy(y_t[:, (w // 4) % 2, :, :, 32 * (w % 4):32 * (w % 4) + 32],
                                          pj[w % 2][:, :, 0:256].rearrange("p a (h n) -> p a h n", n=32))\
                        .then_inc(mixed_v, 1)

                split_inputs(n)
                dve.wait_ge(rq_set, at(it, 1, 1))
                for j in range(QUADS):
                    highest(j)
                    scale(n, 2 * j)
                    times_rq(j)
                    if j < QUADS - 1:
                        scale(n, 2 * j + 1)
                    sums(j)
                scale(n, 7)
                dve.wait_ge(rotated, at(n, 8, 8))
                copy_mix(1)
                copy_mix(3)
                invert_norms(n)
                copy_mix(5)
                copy_mix(7)
                take_q_norms(n)
                for j in range(QUADS):
                    norm_k(n, j)
                    copy_mix(9 + 2 * j)
                dve.wait_ge(attended, at(it, GROUPS, GROUPS))
                dve.wait_ge(x_in, at(it, 16, 16))
                nc.vector.tensor_tensor(out=xs2[0:64], in0=p_att[0:64], in1=x[0:64], op=ALU.add)
                nc.vector.memset(xs2.rearrange("p (s n) -> p s n", s=2)[64:P, :, 0:1], 0.0)
                nc.vector.tensor_tensor(
                    out=xs2.rearrange("p (s n) -> p s n", s=2)[64:P, :, 1:T],
                    in0=p_att.rearrange("p (s n) -> p s n", s=2)[64:P, :, 0:T - 1],
                    in1=x[:].rearrange("p (s n) -> p s n", s=2)[64:P, :, 0:T - 1], op=ALU.add).then_inc(x1_set, 1)
                nc.vector.tensor_tensor(out=x1, in0=p_att, in1=x[:], op=ALU.add).then_inc(x1_set, 1)
                dve.wait_ge(x1_set, at(it, 2, 2))
                dve.sem_inc(x_free, 1)
                dve.wait_ge(meaned, at(it, 1, 1))
                nc.vector.tensor_tensor(out=xc, in0=xs2, in1=p_mean, op=ALU.subtract).then_inc(centred, 1)
                dve.wait_ge(roots, at(it, 1, 1))
                for h in range(2):
                    part = slice(h * T, (h + 1) * T)
                    nc.vector.reciprocal(root[:, part], root[:, part]).then_inc(root_inv, 1)
                    dve.wait_ge(root_inv, at(it, 2, h + 1))
                    nc.vector.tensor_tensor(out=xn[:, part], in0=xc[:, part], in1=root[:, part], op=ALU.mult)\
                        .then_inc(ln_set, 1)
                for m in range(3):
                    dve.wait_ge(gated, at(it, 3, m + 1))
                    nc.vector.scalar_tensor_tensor(out=hid[:, m, :], in0=pj[m % 2][:, 0, :],
                                                   scalar=b1[:, m:m + 1], in1=gate[:, m, :], op0=ALU.add,
                                                   op1=ALU.mult).then_inc(hid_set, 1)
                dve.wait_ge(out_sum, at(it, 1, 1))
                nc.vector.scalar_tensor_tensor(out=xo, in0=p_ffn, scalar=vec[:, 12:13], in1=x1, op0=ALU.add,
                                               op1=ALU.add).then_inc(out_set, 1)

            weight_tables(0)
            split_inputs(0)
            for m in range(8):
                scale(0, m)
            invert_norms(0)
            take_q_norms(0)
            for j in range(QUADS):
                norm_k(0, j)
            with dve.Fori(0, DEPTH) as layer:
                dve.wait_ge(out_set, at(layer, PAIRS, 0))
                nc.vector.tensor_copy(vec[:], raw[:, W_VEC[0]:W_VEC[1]]).then_inc(w_tables, 1)
                nc.vector.tensor_copy(w2[:].rearrange("p c n -> p (c n)"), raw[:, W_2[0]:W_2[1]])
                dve.wait_ge(w_tables, at(layer, 2, 1))
                nc.vector.tensor_scalar(w1[:].rearrange("p c n -> p (c n)"), raw[:, W_1[0]:W_1[1]],
                                        vec[:, 4:5], None, ALU.mult)
                dve.wait_ge(w_vo_sum, at(layer, 2, 2))
                nc.vector.tensor_tensor(out=b1[:], in0=p_att[:, 0:6], in1=vec[:, 6:12], op=ALU.add)\
                    .then_inc(w_tables, 1)
                dve.wait_ge(w_tables, at(layer, 2, 2))
                dve.sem_inc(w_taken, 1)
                dve.sem_inc(w_ready, 1)
                with dve.Fori(0, PAIRS - 1) as pair:
                    it = layer * PAIRS + pair
                    turn(it, it + 1)
                weight_tables(layer + 1)
                it = layer * PAIRS + (PAIRS - 1)
                turn(it, it + 1)

        @block.tensor
        def _(pe):
            for s in (w_vo_sum, xw_sum, projected, normed2, norm_turned, spread_out, scored, shifted, turned, mixed,
                      attended, meaned, vared, h_sum, out_sum):
                pe.sem_inc(s, 1)
            pe.wait_ge(consts_in, 16 * 6)
            pe.wait_ge(consts_set, 6)

            def turn_windows(n, ch):
                if ch >= 2:
                    pe.wait_ge(xw_copied, at(n, 5, ch - 1))
                elif ch:
                    pe.wait_ge(k_normed, at(n, QUADS, QUADS))
                else:
                    pe.wait_ge(rq_set, at(n, 1, 1))
                for w in range(4 * ch, min(4 * ch + 4, 18)):
                    last = nc.tensor.transpose(p_xw[ch % 2][:, (w % 4) * P:(w % 4 + 1) * P],
                                               xs[:, 32 * w:32 * w + P], ident[:])
                last.then_inc(xw_sum, 1)

            def project(n, m, layer, it):
                j, t = m // 2, m % 2
                if m == 0:
                    pe.wait_ge(lo_made, at(layer, 1, 1))
                    pe.wait_ge(x_lo, at(n, 1, 1))
                    if it is not None:
                        pe.wait_ge(out_set, at(it, 1, 0))
                for ab in range(2):
                    if m:
                        pe.wait_ge(scaled, at(n, 16, 2 * m + ab - 1))
                    hi, lo = wqk_hi[:, t, j, ab, :], wqk_lo[:, t, j, ab, :]
                    nc.tensor.matmul(p_qk[:, ab, :], hi, xs_hi[:], start=True, stop=False)
                    nc.tensor.matmul(p_qk[:, ab, :], hi, xs_lo[:], start=False, stop=False)
                    nc.tensor.matmul(p_qk[:, ab, :], lo, xs_hi[:], start=False, stop=True).then_inc(projected, 1)

            def sums(n, m):
                pe.wait_ge(squared, at(n, 16, 2 * m + 2))
                if m == 0:
                    pe.wait_ge(xw_copied, at(n, 5, 0))
                j, t = m // 2, m % 2
                for ab in range(2):
                    last = nc.tensor.matmul(p_sum[32 * j:32 * j + 32, :], head_sum[:, t, :],
                                            sq[:, m % 2, ab, :], start=(t == 0 and ab == 0),
                                            stop=(t == 1 and ab == 1))
                last.then_inc(normed2, 1)

            def turn_norms(n):
                pe.wait_ge(inverse_set, at(n, 1, 1))
                for g in range(GROUPS):
                    last = nc.tensor.transpose(p_turn[:, g * P:(g + 1) * P], norm[:, g * P:(g + 1) * P], ident[:])
                last.then_inc(norm_turned, 1)

            def spread_norms(n, j):
                if j >= 2:
                    pe.wait_ge(k_normed, at(n, QUADS, j - 1))
                elif j:
                    pe.wait_ge(scaled, at(n, 16, 16))
                nc.tensor.matmul(p_spread[j % 2], spread[:, j, :], norm[:], start=True, stop=True)\
                    .then_inc(spread_out, 1)

            def turn(it, n, layer, next_layer):
                def scores(j):
                    if j >= 2:
                        pe.wait_ge(z_set, at(it, QUADS, j - 1))
                    else:
                        pe.wait_ge(hid_set, at(it, 3, 0))
                        pe.wait_ge(w_vo_set, at(layer, 2, 2))
                    pe.wait_ge(q_laid[j], at(it, 128, 128))
                    pe.wait_ge(k_laid[j], at(it, 128, 128))
                    for par in range(2):
                        nc.tensor.matmul(pj[j % 2][:, par, :], ident_b[:], mask[:], start=True, stop=True)
                    for ch in range(2):
                        for g in range(GROUPS):
                            for w in range(4):
                                for par in range(2):
                                    r = slice(64 * par, 64 * par + 64)
                                    at_w = 32 * (4 * g + w)
                                    col = (g * 2 + ch) * 64
                                    last = nc.tensor.matmul(
                                        pj[j % 2][32 * w:32 * w + 32, par, col:col + 64],
                                        q_t[r, 2 * j + ch, at_w:at_w + 32], k_t[r, 2 * j + ch, at_w:at_w + 64],
                                        start=False, stop=True, skip_group_check=True)
                    last.then_inc(scored, 1)

                def shift(j):
                    pe.wait_ge(maxed, at(it, QUADS, j + 1))
                    for par in range(2):
                        last = nc.tensor.matmul(
                            pj[j % 2][:, par, :].rearrange("p (c k) -> p c k", k=64), ident_r[:],
                            negmax[:, j % 2, 8 * par:8 * par + 8].unsqueeze(2).broadcast_to([P, 8, 64]),
                            start=False, stop=True, skip_group_check=True)
                    last.then_inc(shifted, 1)

                def turn_probs(m):
                    j, par = m // 2, m % 2
                    pe.wait_ge(probs_set, at(it, QUADS, j + 1))
                    if m == 7:
                        pe.wait_ge(z_set, at(it, QUADS, QUADS))
                    elif m:
                        pe.wait_ge(turned_out, at(it, 8, m))
                    else:
                        pe.wait_ge(xw_copied, at(n, 5, 0))
                    p4 = prob[:, j % 2, :].rearrange("p (a g k) -> p a g k", a=2, g=GROUPS)
                    for g in range(GROUPS):
                        last = nc.tensor.transpose(p_turned(m)[:, g * P:(g + 1) * P], p4[:, par, g, :], ident[:])
                    last.then_inc(turned, 1)

                def mix(w):
                    if w >= 2:
                        pe.wait_ge(mixed_v if w % 2 else mixed_a, at(it, 8, w // 2))
                    for ch in range(2):
                        r = slice(64 * ch, 64 * ch + 64)
                        cols = (w // 4) * P + 32 * (w % 4)
                        last = nc.tensor.matmul(
                            pj[w % 2][:, ch, 0:256].rearrange("p (j a n) -> p j a n", j=QUADS, a=2),
                            xw[r, w + 2 * (1 - ch), :], prob_t[r, :, :, cols:cols + 32], start=True, stop=True)
                    last.then_inc(mixed, 1)

                def attend(g):
                    pe.wait_ge(mixed_a, at(it, 8, 2 * g + 2))
                    pe.wait_ge(mixed_v, at(it, 8, 2 * g + 2))
                    for m in range(16):
                        ch, jp = m // 8, m % 8
                        last = nc.tensor.matmul(p_att[:, g * P:(g + 1) * P], w_vo[:, jp % 2, 2 * (jp // 2) + ch, :],
                                                y_t[:, g % 2, ch, jp, :], start=(m == 0), stop=(m == 15))
                    last.then_inc(attended, 1)

                for j in range(QUADS):
                    scores(j)
                    project(n, 2 * j, next_layer, it)
                    shift(j)
                    if j:
                        sums(n, 2 * j - 1)
                        turn_probs(2 * j - 2)
                    project(n, 2 * j + 1, next_layer, it)
                    sums(n, 2 * j)
                    if j:
                        turn_probs(2 * j - 1)
                turn_probs(6)
                sums(n, 7)
                turn_probs(7)
                pe.wait_ge(turned_out, at(it, 8, 8))
                pe.wait_ge(z_set, at(it, QUADS, QUADS))
                pe.wait_ge(w_ready, at(layer, 1, 1))
                pe.wait_ge(scaled, at(n, 16, 16))
                for g in range(GROUPS):
                    for w in range(4 * g, 4 * g + 4):
                        mix(w)
                    if g:
                        attend(g - 1)
                        if g == 1:
                            turn_norms(n)
                            spread_norms(n, 0)
                        spread_norms(n, g)
                attend(GROUPS - 1)
                turn_windows(n, 0)
                pe.wait_ge(x1_set, at(it, 2, 1))
                pe.wait_ge(k_normed, at(n, QUADS, QUADS))
                nc.tensor.matmul(p_mean, mean_w[:], xs2, start=True, stop=True).then_inc(meaned, 1)
                turn_windows(n, 1)
                pe.wait_ge(csq, at(it, 1, 1))
                nc.tensor.matmul(p_var, mean_w[:], xsq, start=True, stop=True).then_inc(vared, 1)
                for ch in range(2, 5):
                    turn_windows(n, ch)
                def hidden(m, part):
                    for half in range(2):
                        last = nc.tensor.matmul(pj[m % 2][:, half, part], w1[:, 3 * half + m, :], xn[:, part],
                                                start=True, stop=True)
                    return last

                for h in range(2):
                    pe.wait_ge(ln_set, at(it, 2, h + 1))
                    for m in range(2):
                        last = hidden(m, slice(h * T, (h + 1) * T))
                        if h:
                            last.then_inc(h_sum, 1)
                pe.wait_ge(hid_set, at(it, 3, 1))
                hidden(2, slice(0, NT)).then_inc(h_sum, 1)
                pe.wait_ge(hid_set, at(it, 3, 3))
                for m in range(3):
                    last = nc.tensor.matmul(p_ffn, w2[:, m, :], hid[:, m, :], start=(m == 0), stop=(m == 2))
                last.then_inc(out_sum, 1)

            for m in range(8):
                project(0, m, 0, None)
                if m:
                    sums(0, m - 1)
            sums(0, 7)
            turn_norms(0)
            for j in range(QUADS):
                spread_norms(0, j)
            for ch in range(5):
                turn_windows(0, ch)
            with pe.Fori(0, DEPTH) as layer:
                pe.wait_ge(out_set, at(layer, PAIRS, 0))
                wv = raw[:, W_V[0]:W_V[1]].rearrange("p (c n) -> p c n", c=8)
                wo = raw[:, W_O[0]:W_O[1]].rearrange("p (c n) -> p c n", c=8)
                for m in range(6):
                    nc.tensor.matmul(p_att[:, m:m + 1], raw[:, W_1[0] + m * P:W_1[0] + (m + 1) * P],
                                     raw[:, W_VEC[0] + 5:W_VEC[0] + 6], start=True, stop=True)
                for par in range(2):
                    r = slice(64 * par, 64 * par + 64)
                    for ch in range(8):
                        last = nc.tensor.matmul(pj[par][:, ch // 4, (ch % 4) * P:(ch % 4 + 1) * P],
                                                wv[r, ch, :], wo[r, ch, :], start=True, stop=True)
                    last.then_inc(w_vo_sum, 1)
                with pe.Fori(0, PAIRS - 1) as pair:
                    it = layer * PAIRS + pair
                    turn(it, it + 1, layer, layer)
                it = layer * PAIRS + (PAIRS - 1)
                turn(it, it + 1, layer, layer + 1)

def add_and_store(nc, c, x2, state, out):
    with ExitStack() as ctx:
        ident = ctx.enter_context(nc.sbuf_tensor("o_ident", [P, P], F32))
        x = ctx.enter_context(nc.sbuf_tensor("o_x", [P, 2, GROUPS, DIM], F32))
        s_t = ctx.enter_context(nc.sbuf_tensor("o_s", [P, 2, NT], F32))
        turned = ctx.enter_context(nc.psum_tensor("o_turned", [P, 2, NT], F32))
        consts_in, loaded, turned_in, added, stored = (ctx.enter_context(nc.semaphore("o_" + n)) for n in (
            "consts_in", "loaded", "turned_in", "added", "stored"))
        slot_loaded = [loaded, ctx.enter_context(nc.semaphore("o_loaded1"))]
        slot_stored = [stored, ctx.enter_context(nc.semaphore("o_stored1"))]
        block = ctx.enter_context(nc.Block())

        @block.sync
        def _(sp):
            sp.dma_start(ident[:], c[:, C_IDENT[0]:C_IDENT[1]]).then_inc(consts_in, 16)
            for pair in range(PAIRS):
                k = pair % 2
                if pair >= 2:
                    sp.wait_ge(slot_stored[k], 16 * (pair // 2))
                sp.dma_start(x[:, k], x2[2 * pair:2 * pair + 2].rearrange("s (t p) n -> p (s t) n", p=P))\
                    .then_inc(slot_loaded[k], 16)
                sp.dma_start(s_t[:, k, :], state[:, pair * NT:(pair + 1) * NT]).then_inc(slot_loaded[k], 16)
            for k in range(2):
                sp.wait_ge(slot_stored[k], 16 * (PAIRS // 2))

        @block.tensor
        def _(pe):
            pe.wait_ge(consts_in, 16)
            for pair in range(PAIRS):
                k = pair % 2
                pe.wait_ge(slot_loaded[k], 32 * (pair // 2 + 1))
                if pair >= 2:
                    pe.wait_ge(added, pair - 1)
                for g in range(GROUPS):
                    last = nc.tensor.transpose(turned[:, k, g * P:(g + 1) * P], s_t[:, k, g * P:(g + 1) * P], ident[:])
                last.then_inc(turned_in, 1)

        @block.vector
        def _(dve):
            for pair in range(PAIRS):
                k = pair % 2
                dve.wait_ge(turned_in, pair + 1)
                dve.wait_ge(slot_loaded[k], 32 * (pair // 2 + 1))
                nc.vector.tensor_tensor(out=x[:, k].rearrange("p g n -> p (g n)"), in0=turned[:, k, :],
                                        in1=x[:, k].rearrange("p g n -> p (g n)"), op=ALU.add).then_inc(added, 1)

        @block.scalar
        def _(act):
            for pair in range(PAIRS):
                k = pair % 2
                act.wait_ge(added, pair + 1)
                act.dma_start(out[2 * pair:2 * pair + 2].rearrange("s (t p) n -> p (s t) n", p=P), x[:, k])\
                    .then_inc(slot_stored[k], 16)

def kernel(**inputs):
    import numpy as np
    import concourse.bacc as bacc
    from concourse.bass_utils import run_bass_kernel_spmd

    arrays = {
        "x": np.ascontiguousarray(inputs["x"]),
        "ctx_t": np.ascontiguousarray(np.asarray(inputs["ctx_512"]).transpose(0, 2, 1)),
        "w_attn": attention_weights(np, inputs),
        "w_layers": layer_weights(np, inputs),
        "consts": constants(np),
    }
    nc = bacc.Bacc("TRN2", target_bir_lowering=False, num_devices=1)
    d = {n: nc.dram_tensor(n, a.shape, mybir.dt.from_np(a.dtype), kind="ExternalInput").ap()
         for n, a in arrays.items()}
    out = nc.dram_tensor("out", (B, T, DIM), F32, kind="ExternalOutput").ap()
    x2 = nc.dram_tensor("x2", (B, T, DIM), F32).ap()
    state = nc.dram_tensor("state", (DIM, B * T), F32).ap()
    attention_blocks(nc, d["consts"], d["x"], d["ctx_t"], d["w_attn"], x2, state)
    transformer_layers(nc, d["consts"], d["w_layers"], state)
    add_and_store(nc, d["consts"], x2, state, out)
    return run_bass_kernel_spmd(nc, [arrays], core_ids=[0]).results[0]["out"]
```

```python
from contextlib import ExitStack

import concourse.bass as bass
from concourse import mybir

P = 128
B, T, DIM = 16, 256, 128
DEPTH, HEADS, DIM_HEAD, WINDOW = 6, 16, 64, 32
INNER = HEADS * DIM_HEAD
DIM_INNER = int(DIM * 4 * 2 / 3)
NT = 2 * T
PAIRS = B // 2
QUADS = HEADS // 4
GROUPS = NT // P
FRONT = 3 * WINDOW
QK_SCALE = 8.0
LN_EPS = 1e-5
MASKED = -1e30
VEC = 16

def spans(*widths):
    out, at = [], 0
    for w in widths:
        out.append((at, at + w))
        at += w
    return out

W_QK, W_V, W_O, W_1, W_2, W_VEC = spans(2 * INNER, INNER, INNER, 6 * P, 3 * P, VEC)
W_COLS = W_VEC[1]
C_IDENT, C_MEAN, C_MASK, C_SUM, C_SPREAD, C_TRIG, C_CAUSAL, C_HEAD = spans(P, P, 512, 64, QUADS * P, 4 * T, 384, 4)
C_COLS = C_HEAD[1]
A_SELF, A_CQ, A_CK, A_CV, A_BP, A_BIAS = 4, 8, 9, 10, 11, 12 * P
B_ZERO, B_Q, B_K, B_V, B_CQ, B_CK, B_CV = range(7)
A_COLS = A_BIAS + 8

F32 = mybir.dt.float32
ALU = mybir.AluOpType
ACT = mybir.ActivationFunctionType
AX = mybir.AxisListType

def layer_weights(np, inp):
    wqkv = np.asarray(inp["L0_ffn_Wqkv"])
    w = np.zeros((DEPTH, P, W_COLS), np.float32)
    for t, third in ((0, 1), (1, 0)):
        part = wqkv[:, :, third * INNER:(third + 1) * INNER].reshape(DEPTH, DIM, QUADS, 4, 2, 32)
        w[:, :, W_QK[0] + t * INNER:W_QK[0] + (t + 1) * INNER] = \
            part.transpose(0, 1, 2, 4, 3, 5).reshape(DEPTH, DIM, INNER)
    wv = wqkv[:, :, 2 * INNER:].reshape(DEPTH, DIM, 8, P)
    w[:, :, W_V[0]:W_V[1]] = wv.transpose(0, 3, 2, 1).reshape(DEPTH, P, INNER)
    wo = np.asarray(inp["L0_ffn_Wo"]).reshape(DEPTH, 8, P, DIM)
    w[:, :, W_O[0]:W_O[1]] = wo.transpose(0, 2, 1, 3).reshape(DEPTH, P, INNER)
    for half in range(2):
        at = W_1[0] + half * 3 * P
        w[:, :, at:at + DIM_INNER] = np.asarray(inp["L0_ffn_W1"])[:, :, half * DIM_INNER:(half + 1) * DIM_INNER]
        b = np.zeros((DEPTH, 3 * P), np.float32)
        b[:, :DIM_INNER] = np.asarray(inp["L0_ffn_b1"])[:, half * DIM_INNER:(half + 1) * DIM_INNER]
        w[:, :, W_VEC[0] + 6 + 3 * half:W_VEC[0] + 9 + 3 * half] = b.reshape(DEPTH, 3, P).transpose(0, 2, 1)
    w2 = np.zeros((DEPTH, 3 * P, DIM), np.float32)
    w2[:, :DIM_INNER] = np.asarray(inp["L0_ffn_W2"])
    w[:, :, W_2[0]:W_2[1]] = w2.reshape(DEPTH, 3, P, DIM).transpose(0, 2, 1, 3).reshape(DEPTH, P, 3 * DIM)
    for t, name in ((0, "L0_ffn_k_scale"), (1, "L0_ffn_q_scale")):
        s = np.asarray(inp[name]).reshape(DEPTH, 1, 2, 32)
        w[:, :, W_VEC[0] + 2 * t:W_VEC[0] + 2 * t + 2] = \
            np.broadcast_to(s, (DEPTH, 4, 2, 32)).transpose(0, 1, 3, 2).reshape(DEPTH, P, 2)
    for n, name in ((4, "L0_ffn_ln_g"), (5, "L0_ffn_ln_b"), (12, "L0_ffn_b2")):
        w[:, :, W_VEC[0] + n] = np.asarray(inp[name])
    return np.concatenate([w, np.zeros((1, P, W_COLS), np.float32)])

def constants(np):
    c = np.zeros((P, C_COLS), np.float32)
    c[:, C_IDENT[0]:C_IDENT[1]] = np.eye(P)
    c[:, C_MEAN[0]:C_MEAN[1]] = 1.0 / DIM
    r, s = np.arange(P)[:, None] % 32, np.arange(32)[None, :]
    before = np.where(s >= r, 0.0, MASKED)
    first = np.where(np.arange(P)[:, None] < 32, MASKED, before)
    own = np.where(s <= r, 0.0, MASKED)
    per_group = [np.concatenate([first if g % 2 == 0 else before, own] * 2, 1) for g in range(GROUPS)]
    c[:, C_MASK[0]:C_MASK[1]] = np.concatenate(per_group, 1)
    head = np.arange(P) // 32
    for i in range(4):
        c[head == i, C_SUM[0] + 4 + i] = 1.0
        c[head == i, C_SUM[0] + 32 + i] = 1.0
        for j in range(QUADS):
            c[32 * j + 4 + i, C_SPREAD[0] + j * P + 32 * i:C_SPREAD[0] + j * P + 32 * i + 32] = 1.0
    q, k = np.arange(P)[:, None], np.arange(P)[None, :]
    causal = np.where(k > q, MASKED, 0.0)
    c[:, C_CAUSAL[0]:C_CAUSAL[1]] = np.concatenate([causal, np.zeros((P, P)), causal], 1)
    for n in range(4):
        c[(np.arange(P) // 8) % 4 == n, C_HEAD[0] + n] = 1.0
    f32 = np.float32
    half = np.arange(0, DIM_HEAD, 2, dtype=f32)
    inv_freq = (f32(1.0) / f32(10000.0) ** (half / f32(DIM_HEAD))).astype(f32)
    t = np.arange(T, dtype=f32)
    freqs = (t[:, None] * inv_freq[None, :]).astype(f32)
    base = ((half + f32(0.4 * DIM_HEAD)) / f32(1.4 * DIM_HEAD)).astype(f32)
    power = (t - T // 2) / f32(WINDOW // 2)
    scale = (base[None, :] ** power[:, None]).astype(f32)
    rows = [np.cos(freqs) * scale, np.sin(freqs) * scale, np.cos(freqs) / scale, np.sin(freqs) / scale]
    c[:, C_TRIG[0]:C_TRIG[1]] = np.concatenate([np.tile(x.T.astype(f32), (4, 1)) for x in rows], 1)
    return c

def attention_weights(np, inp):
    w = np.zeros((P, A_COLS), np.float32)
    for n, name in enumerate(("Wq", "Wk", "Wv", "Wo")):
        w[:, n * P:(n + 1) * P] = np.asarray(inp["L0_attn_" + name]).T
    for n, name in ((4, "Wq"), (5, "Wk"), (6, "Wv"), (7, "Wp"), (A_CQ, "Wcq"), (A_CK, "Wck"), (A_CV, "Wcv")):
        m = np.asarray(inp["L0_xattn_" + name])
        w[:m.shape[0], n * P:(n + 1) * P] = m
    w[0, A_BP * P:(A_BP + 1) * P] = np.asarray(inp["L0_xattn_bp"])
    for n, name in ((B_Q, "bq"), (B_K, "bk"), (B_V, "bv"), (B_CQ, "bcq"), (B_CK, "bck"), (B_CV, "bcv")):
        w[:, A_BIAS + n] = np.asarray(inp["L0_xattn_" + name])
    return w

def attention_blocks(nc, c, x_in_dram, ctx_dram, w_attn, x2, state):
    BF16, F32R = mybir.dt.bfloat16, mybir.dt.float32r
    units_of = [[(s, False, d) for s in range(2) for d in range(8)],
                [(s, n == 2, g if n == 2 else 2 * g + n) for s in range(2) for g in range(4) for n in range(3)]]
    unit = units_of[0] + units_of[1]
    UNITS = len(unit)
    first_of = (0, len(units_of[0]), UNITS)
    group_end = [u for u in range(UNITS) if u + 1 in first_of or unit[u][0] != unit[u + 1][0]]
    GROUPS_OUT = len(group_end)
    SELF_SCALE = float(1.0 / (DIM // HEADS) ** 0.5)

    with ExitStack() as ctx:
        def sb(name, shape, dt=F32):
            return ctx.enter_context(nc.sbuf_tensor("a_" + name, shape, dt))

        def sem(name):
            return ctx.enter_context(nc.semaphore("a_" + name))

        w = sb("w", [P, A_COLS])
        ident = sb("ident", [P, P])
        ident_r = sb("ident_r", [P, P], F32R)
        ident_b = sb("ident_b", [P, P], BF16)
        ones = sb("ones", [P, P])
        causal32 = sb("causal32", [P, 384])
        causal = sb("causal", [P, 384], BF16)
        head_of = sb("head_of", [P, 4])
        bias_v = sb("bias_v", [P, 2])
        bias_cq = sb("bias_cq", [P, 4])
        x = sb("x", [P, 4, DIM])
        x_mid = sb("x_mid", [P, 4, DIM])
        x_out = sb("x_out", [P, 4, DIM])
        stats = sb("stats", [P, 4, 6])
        moments = sb("moments", [P, 4, 2])
        rstd = sb("rstd", [P, 4])
        xn = sb("xn", [P, 4, DIM])
        h_t = sb("h_t", [P, NT])
        ctx_t = sb("ctx_t", [64, 2, 2, 64])
        q_m = sb("q_m", [P, 4, NT])
        qc_m = sb("qc_m", [P, 4, NT])
        k_t = sb("k_t", [P, NT])
        kc_t = sb("kc_t", [P, 2, 64])
        v_a = sb("v_a", [P, 4, HEADS, 32])
        vc_a = sb("vc_a", [P, 2, HEADS, 32])
        negmax = sb("negmax", [P, 2, 8], F32R)
        prob = sb("prob", [P, 2, 2, 384])
        prob_t = sb("prob_t", [P, 2, 2, 384])
        o_t = sb("o_t", [P, 4, T])
        rden = sb("rden", [P, 32, 2])
        o_n = sb("o_n", [P, 4, DIM])
        o_c = sb("o_c", [P, 2, DIM])
        on_t = sb("on_t", [P, NT])

        bank = [ctx.enter_context(nc.psum_tensor(f"a_ps{i}", [P, 2, 512], F32)) for i in range(4)]
        p_prob, p_out = bank[2], bank[3]

        consts_in, consts_set, pads_set, ones_set = (sem(n) for n in ("consts_in", "consts_set", "pads_set", "ones_set"))
        x_in, x_free, stored = sem("x_in"), sem("x_free"), sem("stored")
        moment, rooted, root_inv, normed, h_sum, h_set = (sem(n) for n in (
            "moment", "rooted", "root_inv", "normed", "h_sum", "h_set"))
        projected, operands, operands_a = sem("projected"), sem("operands"), sem("operands_a")
        scored, maxed, shifted, exped, turned, turned_out, mixed = (sem(n) for n in (
            "scored", "maxed", "shifted", "exped", "turned", "turned_out", "mixed"))
        o_out, o_turned, o_inv, o_normed, on_sum, on_set, y_sum, y_set = (sem(n) for n in (
            "o_out", "o_turned", "o_inv", "o_normed", "on_sum", "on_set", "y_sum", "y_set"))

        block = ctx.enter_context(nc.Block())

        def at(it, per, n):
            return it * per + (n + 1)

        def weight(n):
            return w[:, n * P:(n + 1) * P]

        def bias(n):
            return w[:, A_BIAS + n:A_BIAS + n + 1]

        def is_cross(u):
            return unit[u][1]

        def by_act(u):
            return is_cross(u) or u % 2 == 1

        x_pairs = x_in_dram.rearrange("(i s) (t p) n -> i p (s t) n", s=2, p=P)
        x2_pairs = x2.rearrange("(i s) (t p) n -> i p (s t) n", s=2, p=P)
        ctx_pairs = ctx_dram.rearrange("(i s) c k -> i c s k", s=2)

        @block.sync
        def _(sp):
            for dst, a, b in ((ident[:], *C_IDENT), (causal32[:], *C_CAUSAL), (head_of[:], *C_HEAD)):
                sp.dma_start(dst, c[:, a:b]).then_inc(consts_in, 16)
            sp.dma_start(w[:], w_attn).then_inc(consts_in, 16)
            sp.sem_inc(x_in, 1)
            with sp.Fori(0, PAIRS) as it:
                sp.wait_ge(x_free, at(it, 1, 0))
                sp.dma_start(x[:], x_pairs[it]).then_inc(x_in, 16)
                for n in range(2):
                    sp.dma_start(ctx_t[:, :, n, :], ctx_pairs[it]).then_inc(x_in, 16)
            sp.wait_ge(stored, at(PAIRS, 32, 0))

        @block.gpsimd
        def _(pool):
            nc.gpsimd.memset(ones[:], 1.0)
            nc.gpsimd.memset(v_a[:], 0.0)
            nc.gpsimd.memset(vc_a[:], 0.0).then_inc(pads_set, 1)
            pool.wait_ge(pads_set, 1)
            nc.gpsimd.memset(v_a[:, :, :, 8:9], 1.0).then_inc(pads_set, 1)
            pool.wait_ge(pads_set, 2)
            nc.gpsimd.memset(vc_a[0:64, :, 0::2, 24:25], 1.0).then_inc(ones_set, 1)
            pool.wait_ge(ones_set, 1)
            nc.gpsimd.memset(vc_a[64:P, :, 1::2, 24:25], 1.0).then_inc(ones_set, 1)

        @block.scalar
        def _(act):
            act.wait_ge(consts_in, 64)
            nc.scalar.copy(ident_r[:], ident[:]).then_inc(consts_set, 1)
            nc.scalar.copy(ident_b[:], ident[:]).then_inc(consts_set, 1)
            nc.scalar.copy(causal[:], causal32[:]).then_inc(consts_set, 1)
            act.wait_ge(consts_set, 5)
            for s in (rooted, h_set, operands_a, exped, turned_out, on_set, stored):
                act.sem_inc(s, 1)
            with act.Fori(0, PAIRS) as it:
                def norm_and_turn(r):
                    act.wait_ge(moment, at(it, 3, r + 1))
                    nc.scalar.activation(rstd[:], rstd[:], ACT.Sqrt).then_inc(rooted, 1)
                    act.wait_ge(h_sum, at(it, 3, r + 1))
                    if r == 0:
                        act.wait_ge(stored, at(it, 32, 0))
                    nc.scalar.copy(h_t[:], p_prob[:, 0, :]).then_inc(h_set, 1)

                def take_projections(blk):
                    act.wait_ge(projected, at(it, 2, blk + 1))
                    last = nc.scalar.copy(v_a[:, :, :, 0:8],
                                          bank[1][:, 0, :].rearrange("p (t h d) -> p t h d", t=4, d=8))
                    if blk:
                        for n in range(4):
                            last = nc.scalar.activation(qc_m[:, n, :], bank[1][:, 1, :], ACT.Identity,
                                                        bias=bias_cq[:, n:n + 1], scale=head_of[:, n:n + 1])
                    last.then_inc(operands_a, 1)

                def units(first, last):
                    def copy_out(u):
                        if by_act(u):
                            act.wait_ge(turned, at(it, UNITS, u + 1))
                            if u >= 2:
                                act.wait_ge(mixed, at(it, UNITS, u - 1))
                            if is_cross(u):
                                nc.scalar.copy(prob_t[:, u % 2].rearrange("p a b -> p (a b)")[:, 0:512],
                                               p_prob[:, u % 2, :]).then_inc(turned_out, 1)
                            else:
                                nc.scalar.copy(prob_t[:, u % 2], p_prob[:, :, 0:384]).then_inc(turned_out, 1)

                    for u in range(first, last):
                        if u > first:
                            copy_out(u - 1)
                        n, k = (1, 512) if is_cross(u) else (2, 384)
                        act.wait_ge(shifted, at(it, UNITS, u + 1))
                        if u >= 2:
                            act.wait_ge(turned, at(it, UNITS, u - 1))
                        out = prob[:, u % 2].rearrange("p a b -> p (a b)")[:, 0:n * k] \
                            .rearrange("p (a b) -> p a b", a=n)
                        nc.scalar.activation(out, bank[u % 2][:, 0:n, 0:k], ACT.Exp, scale=SELF_SCALE)\
                            .then_inc(exped, 1)
                    copy_out(last - 1)

                for blk in range(2):
                    norm_and_turn(blk)
                    take_projections(blk)
                    units(first_of[blk], first_of[blk + 1])
                    act.wait_ge(on_sum, at(it, 2, blk + 1))
                    nc.scalar.activation(on_t[:], p_prob[:, 0, :], ACT.Identity, bias=bias_v[:, blk:blk + 1])\
                        .then_inc(on_set, 1)
                norm_and_turn(2)
                act.dma_start(x2_pairs[it], x_out[:]).then_inc(stored, 16)
                act.wait_ge(h_set, at(it, 3, 3))
                act.dma_start(state[:, bass.ts(it, NT)], h_t[:]).then_inc(stored, 16)

        @block.vector
        def _(dve):
            for s in (x_free, moment, normed, operands, maxed, turned_out, o_out, o_inv, root_inv, o_normed, y_set):
                if s is not turned_out:
                    dve.sem_inc(s, 1)
            dve.wait_ge(consts_in, 64)
            dve.wait_ge(ones_set, 2)
            nc.vector.memset(bias_v[:, 0:1], 0.0)
            nc.vector.tensor_scalar(bias_cq[:], head_of[:], bias(B_CQ), None, ALU.mult).then_inc(consts_set, 1)
            nc.vector.tensor_tensor(out=bias_v[:, 1:2], in0=bias(B_V), in1=bias(B_CV), op=ALU.add)\
                .then_inc(consts_set, 1)
            with dve.Fori(0, PAIRS) as it:
                def norm(r, src):
                    steps = at(it, 9, 3 * r)
                    for t in range(4):
                        last = nc.vector.bn_stats(stats[:, t, :], src[:, t, :])
                    last.then_inc(normed, 1)
                    dve.wait_ge(normed, steps + 1)
                    nc.vector.memset(rstd[:], LN_EPS)
                    for t in range(4):
                        last = nc.vector.bn_aggr(moments[:, t, :], stats[:, t, :])
                    last.then_inc(normed, 1)
                    dve.wait_ge(normed, steps + 2)
                    nc.vector.tensor_tensor(out=rstd[:], in0=moments[:, :, 1:2].rearrange("p t o -> p (t o)"),
                                            in1=rstd[:], op=ALU.add).then_inc(moment, 1)
                    dve.wait_ge(rooted, at(it, 3, r + 1))
                    nc.vector.reciprocal(rstd[:], rstd[:]).then_inc(root_inv, 1)
                    dve.wait_ge(root_inv, at(it, 3, r + 1))
                    for t in range(4):
                        last = nc.vector.tensor_scalar(xn[:, t, :], src[:, t, :], moments[:, t, 0:1],
                                                       rstd[:, t:t + 1], ALU.subtract, ALU.mult)
                    last.then_inc(normed, 1)

                def take_projections(blk):
                    dve.wait_ge(projected, at(it, 2, blk + 1))
                    for n in range(4):
                        nc.vector.tensor_scalar(q_m[:, n, :], p_out[:, 0, :], bias(B_Q if blk else B_ZERO),
                                                head_of[:, n:n + 1], ALU.add, ALU.mult)
                    last = nc.vector.tensor_scalar(k_t[:], p_out[:, 1, :], bias(B_K if blk else B_ZERO), None, ALU.add)
                    if blk:
                        nc.vector.tensor_scalar(kc_t[:].rearrange("p s k -> p (s k)"), bank[0][:, 0, 0:P],
                                                bias(B_CK), None, ALU.add)
                        for n in range(2):
                            r = slice(64 * n, 64 * n + 64)
                            last = nc.vector.tensor_copy(
                                vc_a[r, :, n::2, 16:24],
                                bank[0][r, 1, 0:T].rearrange("p (s h d) -> p s h d", s=2, d=8)[:, :, n::2])
                    last.then_inc(operands, 1)

                def copy_outputs(k):
                    dve.wait_ge(mixed, at(it, UNITS, group_end[k] + 1))
                    nc.vector.tensor_copy(o_t[:].rearrange("p a b -> p (a b)"), p_out[:].rearrange("p a b -> p (a b)"))\
                        .then_inc(o_out, 1)

                def divide_outputs(k):
                    s = k % 2
                    dve.wait_ge(o_turned, at(it, GROUPS_OUT, k + 1))
                    o = p_prob[:].rearrange("p a (h k) -> p (a h) k", k=32)
                    to = [a.rearrange("p t (h d) -> p (t h) d", d=8) for a in (o_n[:, 2 * s:2 * s + 2], o_c[:])]
                    parts = 2 if k >= 2 else 1
                    nc.vector.reciprocal(rden[:, :, 0:parts], o[:, :, 8:16 * parts - 7:16]).then_inc(o_inv, 1)
                    dve.wait_ge(o_inv, at(it, GROUPS_OUT, k + 1))
                    for n in range(parts):
                        last = nc.vector.tensor_tensor(out=to[n], in0=o[:, :, 16 * n:16 * n + 8],
                                                       in1=rden[:, :, n:n + 1].broadcast_to([P, 32, 8]), op=ALU.mult)
                    last.then_inc(o_normed, 1)
                    if parts == 2:
                        dve.wait_ge(o_normed, at(it, 6, 2 * k - 1))
                        nc.vector.tensor_tensor(out=o_n[:, 2 * s:2 * s + 2], in0=o_n[:, 2 * s:2 * s + 2], in1=o_c[:],
                                                op=ALU.add).then_inc(o_normed, 1)

                def units(first, last):
                    def copy_out(u):
                        if not by_act(u):
                            dve.wait_ge(turned, at(it, UNITS, u + 1))
                            if u >= 2:
                                dve.wait_ge(mixed, at(it, UNITS, u - 1))
                            nc.vector.tensor_copy(prob_t[:, u % 2], p_prob[:, :, 0:384]).then_inc(turned_out, 1)

                    for u in range(first, last):
                        dve.wait_ge(scored, at(it, UNITS, u + 1))
                        if u >= 2:
                            dve.wait_ge(shifted, at(it, UNITS, u - 1))
                        if is_cross(u):
                            nc.vector.tensor_reduce(negmax[:, u % 2, :],
                                                    bank[u % 2][:, 0, :].rearrange("p (c k) -> p c k", k=64), AX.X,
                                                    ALU.max, negate=True).then_inc(maxed, 1)
                        else:
                            nc.vector.tensor_reduce(negmax[:, u % 2, 0:2], bank[u % 2][:, :, 0:P], AX.X, ALU.max,
                                                    negate=True)
                            nc.vector.tensor_reduce(negmax[:, u % 2, 2:4], bank[u % 2][:, :, P:384], AX.X, ALU.max,
                                                    negate=True).then_inc(maxed, 1)
                        if u > first:
                            copy_out(u - 1)
                        if u - 2 >= first and u - 2 in group_end:
                            copy_outputs(group_end.index(u - 2))
                        if u - 3 >= first and u - 3 in group_end:
                            divide_outputs(group_end.index(u - 3))
                    copy_out(last - 1)

                dve.wait_ge(x_in, at(it, 48, 48))
                norm(0, x)
                for blk in range(2):
                    take_projections(blk)
                    if blk:
                        dve.sem_inc(x_free, 1)
                    units(first_of[blk], first_of[blk + 1])
                    copy_outputs(2 * blk + 1)
                    divide_outputs(2 * blk + 1)
                    dve.wait_ge(y_sum, at(it, 2, blk + 1))
                    if blk:
                        dve.wait_ge(stored, at(it, 32, 0))
                    src, to = (x_mid, x_out) if blk else (x, x_mid)
                    nc.vector.tensor_tensor(out=to[:].rearrange("p t n -> p (t n)"), in0=p_prob[:, 1, :],
                                            in1=src[:].rearrange("p t n -> p (t n)"), op=ALU.add).then_inc(y_set, 1)
                    dve.wait_ge(y_set, at(it, 2, blk + 1))
                    norm(blk + 1, to)

        @block.tensor
        def _(pe):
            for s in (h_sum, projected, scored, shifted, turned, mixed, o_turned, on_sum, y_sum):
                pe.sem_inc(s, 1)
            pe.wait_ge(consts_in, 64)
            pe.wait_ge(consts_set, 5)
            pe.wait_ge(ones_set, 2)
            with pe.Fori(0, PAIRS) as it:
                def turn_tokens(r):
                    pe.wait_ge(normed, at(it, 9, 3 * r + 3))
                    for t in range(4):
                        last = nc.tensor.transpose(p_prob[:, 0, t * P:(t + 1) * P], xn[:, t, :], ident[:])
                    last.then_inc(h_sum, 1)

                def project(blk):
                    pe.wait_ge(h_set, at(it, 3, blk + 1))
                    pe.wait_ge(exped, at(it, UNITS, first_of[blk]))
                    wq, wk, wv = (weight(n + (A_SELF if blk else 0)) for n in range(3))
                    nc.tensor.matmul(p_out[:, 0, :], wq, h_t[:], start=True, stop=True)
                    nc.tensor.matmul(p_out[:, 1, :], wk, h_t[:], start=True, stop=True)
                    for t in range(4):
                        last = nc.tensor.matmul(bank[1][:, 0, t * P:(t + 1) * P], h_t[:, t * P:(t + 1) * P], wv,
                                                start=True, stop=True)
                    if blk:
                        nc.tensor.matmul(bank[1][:, 1, :], weight(A_CQ), h_t[:], start=True, stop=True)
                        nc.tensor.matmul(bank[0][:, 0, 0:P], weight(A_CK)[0:64], ctx_t[:, :, 0, :], start=True, stop=True)
                        for s in range(2):
                            last = nc.tensor.matmul(bank[0][:, 1, s * P:(s + 1) * P],
                                                    ctx_t[:, s].rearrange("c n k -> c (n k)"), weight(A_CV)[0:64],
                                                    start=True, stop=True)
                    last.then_inc(projected, 1)
                    pe.wait_ge(operands, at(it, 2, blk + 1))
                    pe.wait_ge(operands_a, at(it, 2, blk + 1))

                def scores(u):
                    at_s, d = T * unit[u][0], unit[u][2]
                    s = bank[u % 2]
                    if u >= 2:
                        pe.wait_ge(exped, at(it, UNITS, u - 1))
                    if is_cross(u):
                        r = slice(32 * d, 32 * d + 32)
                        for t in range(2):
                            for n in range(4):
                                col = t * 256 + n * 64
                                last = nc.tensor.matmul(s[:, 0, col:col + 64],
                                                        qc_m[r, n, at_s + t * P:at_s + (t + 1) * P],
                                                        kc_t[r, unit[u][0], :], start=not col, stop=True,
                                                        skip_group_check=True)
                    else:
                        for n in range(2):
                            h = 2 * d + n
                            r = slice(32 * (h // 4), 32 * (h // 4) + 32)
                            q = q_m[r, h % 4, at_s:at_s + T]
                            nc.tensor.matmul(s[:, n, 0:384], ident_b[:], causal[:], start=True, stop=True)
                            nc.tensor.matmul(s[:, n, 0:P], q[:, 0:P], k_t[r, at_s:at_s + P], start=False, stop=True,
                                             skip_group_check=True)
                            last = nc.tensor.matmul(s[:, n, P:384], q[:, P:T], k_t[r, at_s:at_s + T], start=False,
                                                    stop=True, skip_group_check=True)
                    last.then_inc(scored, 1)

                def shift(u):
                    s = bank[u % 2]
                    pe.wait_ge(maxed, at(it, UNITS, u + 1))
                    if is_cross(u):
                        last = nc.tensor.matmul(s[:, 0, :].rearrange("p (c k) -> p c k", k=64), ident_r[:],
                                                negmax[:, u % 2, :].unsqueeze(2).broadcast_to([P, 8, 64]),
                                                start=False, stop=True, skip_group_check=True)
                    else:
                        for n in range(2):
                            for t in range(2):
                                out = s[:, n, P:384] if t else s[:, n, 0:P]
                                m = negmax[:, u % 2, 2 * t + n:2 * t + n + 1]
                                last = nc.tensor.matmul(out, ident_r[:], m.broadcast_to([P, out.shape[1]]),
                                                        start=False, stop=True, skip_group_check=True)
                    last.then_inc(shifted, 1)

                def turn(u):
                    pe.wait_ge(exped, at(it, UNITS, u + 1))
                    if u:
                        pe.wait_ge(turned_out, at(it, UNITS, u))
                    p = prob[:, u % 2].rearrange("p a b -> p (a b)")
                    if is_cross(u):
                        for hp in range(2):
                            for t in range(2):
                                last = nc.tensor.transpose(p_prob[:, u % 2, (2 * hp + t) * P:(2 * hp + t + 1) * P],
                                                           p[:, t * 256 + hp * P:t * 256 + (hp + 1) * P], ident[:])
                    else:
                        for n in range(2):
                            for b in range(3):
                                last = nc.tensor.transpose(p_prob[:, n, b * P:(b + 1) * P],
                                                           p[:, n * 384 + b * P:n * 384 + (b + 1) * P], ident[:])
                    last.then_inc(turned, 1)

                def mix(u):
                    pe.wait_ge(turned_out, at(it, UNITS, u + 1))
                    if u - 1 in group_end:
                        pe.wait_ge(o_out, at(it, GROUPS_OUT, group_end.index(u - 1) + 1))
                    seq, _, d = unit[u]
                    if is_cross(u):
                        pt = prob_t[:, u % 2].rearrange("p a b -> p (a b)")
                        for n in range(4):
                            last = nc.tensor.matmul(p_out[32 * n:32 * n + 32, d // 2, (d % 2) * T:(d % 2 + 1) * T],
                                                    vc_a[:, seq, 4 * d + n, :], pt[:, (n // 2) * T:(n // 2 + 1) * T],
                                                    start=False, stop=True, skip_group_check=True)
                    else:
                        for n in range(2):
                            h = 2 * d + n
                            g, rows = h // 4, slice(32 * (h % 4), 32 * (h % 4) + 32)
                            col = (g % 2) * T
                            nc.tensor.matmul(p_out[rows, g // 2, col:col + T], v_a[:, 2 * seq, h, :],
                                             prob_t[:, u % 2, n, 0:T], start=True, stop=True)
                            last = nc.tensor.matmul(p_out[rows, g // 2, col + P:col + T], v_a[:, 2 * seq + 1, h, :],
                                                    prob_t[:, u % 2, n, T:384], start=False, stop=True,
                                                    skip_group_check=True)
                    last.then_inc(mixed, 1)

                def turn_outputs(k):
                    pe.wait_ge(o_out, at(it, GROUPS_OUT, k + 1))
                    for t in range(2):
                        for g in range(4):
                            last = nc.tensor.transpose(p_prob[:, t, g * P:(g + 1) * P], o_t[:, g, t * P:(t + 1) * P],
                                                       ident[:])
                    last.then_inc(o_turned, 1)

                def units(first, last):
                    for u in range(first, last):
                        scores(u)
                        if u - 4 >= first and u - 4 in group_end:
                            pe.wait_ge(o_normed, at(it, 6, 1 if first == 0 else 4))
                        if u > first:
                            turn(u - 1)
                        shift(u)
                        if u > first + 1:
                            mix(u - 2)
                        if u - 3 >= first and u - 3 in group_end:
                            pe.wait_ge(turned_out, at(it, UNITS, u))
                            turn_outputs(group_end.index(u - 3))
                    turn(last - 1)
                    mix(last - 2)
                    mix(last - 1)

                def project_out(blk):
                    pe.wait_ge(o_normed, at(it, 6, 6 if blk else 2))
                    for t in range(4):
                        last = nc.tensor.transpose(p_prob[:, 0, t * P:(t + 1) * P], o_n[:, t, :], ident[:])
                    last.then_inc(on_sum, 1)
                    pe.wait_ge(on_set, at(it, 2, blk + 1))
                    wo = weight(A_SELF + 3 if blk else 3)
                    for t in range(4):
                        out = p_prob[:, 1, t * P:(t + 1) * P]
                        last = nc.tensor.matmul(out, on_t[:, t * P:(t + 1) * P], wo, start=True, stop=not blk)
                        if blk:
                            last = nc.tensor.matmul(out, ones[:], weight(A_BP), start=False, stop=True)
                    last.then_inc(y_sum, 1)

                turn_tokens(0)
                for blk in range(2):
                    project(blk)
                    units(first_of[blk], first_of[blk + 1])
                    turn_outputs(2 * blk + 1)
                    project_out(blk)
                    turn_tokens(blk + 1)

def transformer_layers(nc, c, w_layers, state):
    BF16, F32R = mybir.dt.bfloat16, mybir.dt.float32r
    KEEP_BUSY = 5

    with ExitStack() as ctx:
        def sb(name, shape, dt=F32):
            return ctx.enter_context(nc.sbuf_tensor("f_" + name, shape, dt))

        def sem(name):
            return ctx.enter_context(nc.semaphore("f_" + name))

        raw = sb("raw", [P, W_COLS])
        wqk_hi = sb("wqk_hi", [P, 2, QUADS, 2, P], F32R)
        wqk_lo = sb("wqk_lo", [P, 2, QUADS, 2, P], F32R)
        w_vo = sb("w_vo", [P, 2, 8, P])
        w1 = sb("w1", [P, 6, P])
        w2 = sb("w2", [P, 3, P])
        vec = sb("vec", [P, VEC])
        b1 = sb("b1", [P, 6])
        trig = sb("trig", [P, 4, T])
        straight = [sb(f"straight{t}", [P, 2, T]) for t in range(2)]
        crossed = [sb(f"crossed{t}", [P, 2, T]) for t in range(2)]
        ident = sb("ident", [P, P])
        ident_r = sb("ident_r", [P, P], F32R)
        ident_b = sb("ident_b", [P, P], BF16)
        mean_w = sb("mean_w", [P, P])
        head_sum = sb("head_sum", [P, 2, 32])
        spread = sb("spread", [P, QUADS, P], F32R)
        mask = sb("mask", [P, 512], BF16)
        eps = sb("eps", [P, 1])
        xs = sb("xs", [P, FRONT + NT + 64])
        xs_now = xs[:, FRONT:FRONT + NT]
        xs_hi = sb("xs_hi", [P, NT], F32R)
        xs_lo = sb("xs_lo", [P, NT], F32R)
        xw = sb("xw", [P, 18, P])
        sq = sb("sq", [P, 2, 2, NT])
        rot = sb("rot", [P, QUADS, 2, NT])
        rotq = sb("rotq", [P, 2, 2, NT])
        norm = sb("norm", [P, NT])
        norm_hi = sb("norm_hi", [P, NT], F32R)
        norm_lo = sb("norm_lo", [P, NT], F32R)
        q_t = sb("q_t", [P, 8, NT])
        k_t = sb("k_t", [P, 8, 32 + NT])
        rq = sb("rq", [P, QUADS, 2, GROUPS, 2])
        x = sb("x", [P, NT])
        negmax = sb("negmax", [P, 2, 16], F32R)
        zs = sb("zs", [P, 2, NT * 2])
        mask32, spread32 = zs[:, 0, 0:512], zs[:, 0, 512:1024]
        den = sb("den", [P, 2, 16])
        rden = sb("rden", [P, 2, 16])
        prob = sb("prob", [P, 2, 1024])
        prob_t = sb("prob_t", [P, QUADS, 2, GROUPS * P])
        y_t = sb("y_t", [P, 2, 2, 8, P])
        flat_y = y_t[:].rearrange("p s a b n -> p (s a b n)")
        up, vp = (y_t[:, :, n].rearrange("p s b n -> p s (b n)").rearrange("p s (a n) -> p s a n", a=2)
                  for n in range(2))
        hid = flat_y[:, 0:2048].rearrange("p (a n) -> p a n", a=4)
        x1, xs2, xc, xsq, root, xn, xo = (prob_t[:, n // 2, n % 2, :] for n in range(7))
        gate = sq[:].rearrange("p a b n -> p (a b) n")

        bank = [ctx.enter_context(nc.psum_tensor(f"f_ps{i}", [P, 2, 512], F32)) for i in range(4)]
        p_qk = bank[0]
        pj = [bank[1], bank[2]]
        p_sum, p_turn = bank[3][:, 0, :], bank[3][:, 1, :]
        p_att, p_var, p_mean, p_ffn = p_qk[:, 0, :], p_qk[:, 0, :], p_qk[:, 1, :], p_qk[:, 1, :]
        p_spread = [p_sum, p_qk[:, 1, :]]
        p_xw = [p_turn, p_sum]

        x_granted = sem("x_granted")
        consts_in, consts_set = sem("consts_in"), sem("consts_set")
        w_in, hi_made, lo_made, w_tables, w_vo_sum, b1_sum, w_vo_set, w_ready, w_taken = (sem(n) for n in (
            "w_in", "hi_made", "lo_made", "w_tables", "w_vo_sum", "b1_sum", "w_vo_set", "w_ready", "w_taken"))
        xs_in, x_in, x_free, x_hi, x_lo, xw_sum, xw_copied = (sem(n) for n in (
            "xs_in", "x_in", "x_free", "x_hi", "x_lo", "xw_sum", "xw_copied"))
        projected, squared, scaled, rotated = (sem(n) for n in ("projected", "squared", "scaled", "rotated"))
        normed2, rooted, guarded, inverse_set, norm_rounded, norm_split, norm_turned, rq_set, spread_out, k_normed = (sem(n) for n in (
            "normed2", "rooted", "guarded", "inverse_set", "norm_rounded", "norm_split", "norm_turned", "rq_set", "spread_out", "k_normed"))
        q_laid, k_laid = ([sem(f"{n}{j}") for j in range(QUADS)] for n in ("q_laid", "k_laid"))
        scored, maxed, shifted, z_set, exped, summed, inverted, probs_set, last_probs_set, turned, turned_out = (sem(n) for n in (
            "scored", "maxed", "shifted", "z_set", "exped", "summed", "inverted", "probs_set", "last_probs_set", "turned",
            "turned_out"))
        mixed, mixed_a, mixed_v, attended, x1_set, centred, meaned, csq, vared, root_inv, roots, ln_set = (sem(n) for n in (
            "mixed", "mixed_a", "mixed_v", "attended", "x1_set", "centred", "meaned", "csq", "vared", "root_inv", "roots",
            "ln_set"))
        h_sum, gated, hid_set, out_sum, out_set, stored = (sem(n) for n in (
            "h_sum", "gated", "hid_set", "out_sum", "out_set", "stored"))

        block = ctx.enter_context(nc.Block())

        def at(it, per, n):
            return it * per + (n + 1)

        def two(t):
            return t.unsqueeze(1).broadcast_to([P, 2, T])

        def p_turned(m):
            return p_turn if m < 6 else pj[0][:, m - 6, :]

        @block.sync
        def _(sp):
            for dst, a, b in ((ident[:], *C_IDENT), (mean_w[:], *C_MEAN), (mask32, *C_MASK)):
                sp.dma_start(dst, c[:, a:b]).then_inc(consts_in, 16)
            sp.dma_start(head_sum[:].rearrange("p a b -> p (a b)"), c[:, C_SUM[0]:C_SUM[1]]).then_inc(consts_in, 16)
            sp.dma_start(spread32, c[:, C_SPREAD[0]:C_SPREAD[1]]).then_inc(consts_in, 16)
            sp.dma_start(trig[:].rearrange("p a b -> p (a b)"), c[:, C_TRIG[0]:C_TRIG[1]]).then_inc(consts_in, 16)
            for s in (w_in, xs_in, x_in, *q_laid, *k_laid):
                sp.sem_inc(s, 1)
            sp.wait_ge(consts_set, 7)
            sp.dma_start(raw[:], w_layers[0]).then_inc(w_in, 16)

            def load_shifted(n, cols):
                sp.wait_ge(xw_sum, at(n, 5, 0))
                sp.dma_start(xs_now[0:64, :], cols[0:64, :]).then_inc(xs_in, 16)
                for s in range(2):
                    sp.dma_start(xs_now[64:P, T * s + 1:T * (s + 1)],
                                 cols[64:P, T * s:T * (s + 1) - 1]).then_inc(xs_in, 16)

            def lay_out(n):
                for j in range(QUADS):
                    sp.wait_ge(rotated, at(n, 8, 2 * j + 2))
                    for ab in range(2):
                        for i in range(4):
                            to = 64 * (i % 2) + 32 * ab
                            sp.dma_start(q_t[to:to + 32, 2 * j + i // 2, :],
                                         rotq[32 * i:32 * i + 32, j % 2, ab, :]).then_inc(q_laid[j], 16)
                for j in range(QUADS):
                    sp.wait_ge(k_normed, at(n, QUADS, j + 1))
                    for ab in range(2):
                        for i in range(4):
                            to = 64 * (i % 2) + 32 * ab
                            sp.dma_start(k_t[to:to + 32, 2 * j + i // 2, 32:32 + NT],
                                         rot[32 * i:32 * i + 32, j, ab, :]).then_inc(k_laid[j], 16)

            def turn(it, n, next_cols, cols):
                load_shifted(n, next_cols)
                sp.wait_ge(stored, at(it, 16, 0))
                sp.sem_inc(x_granted, 1)
                sp.wait_ge(x_free, at(it, 1, 0))
                sp.sem_inc(x_granted, 1)
                sp.dma_start(x[:], cols).then_inc(x_in, 16)
                lay_out(n)

            last = DEPTH * PAIRS
            load_shifted(0, state[:, 0:NT])
            lay_out(0)
            with sp.Fori(0, DEPTH) as layer:
                with sp.Fori(0, PAIRS - 1) as pair:
                    it = layer * PAIRS + pair
                    turn(it, it + 1, state[:, NT:][:, bass.ts(pair, NT)], state[:, bass.ts(pair, NT)])
                it = layer * PAIRS + (PAIRS - 1)
                turn(it, it + 1, state[:, 0:NT], state[:, (PAIRS - 1) * NT:PAIRS * NT])
            load_shifted(last + 1, state[:, 0:NT])
            sp.wait_ge(xs_in, at(last + 1, 48, 48))
            sp.wait_ge(stored, at(last, 16, 0))
            for s in q_laid + k_laid:
                sp.wait_ge(s, at(last, 128, 128))

        @block.gpsimd
        def _(pool):
            nc.gpsimd.memset(xs[:], 0.0).then_inc(consts_set, 1)
            nc.gpsimd.memset(k_t[:], 0.0).then_inc(consts_set, 1)
            nc.gpsimd.memset(eps[:], LN_EPS).then_inc(consts_set, 1)
            for s in (rotated, probs_set, norm_split):
                pool.sem_inc(s, 1)

            def rotate(n, m, it):
                j, t = m // 2, m % 2
                if t and it is not None:
                    pool.wait_ge(scored, at(it, QUADS, j + 1))
                pool.wait_ge(scaled, at(n, 16, 2 * m + 2))
                if t and j >= 2:
                    pool.wait_ge(q_laid[j - 2], at(n, 128, 128))
                elif t:
                    pool.wait_ge(q_laid[j + 2], at(n, 128, 0))
                else:
                    pool.wait_ge(k_laid[j], at(n, 128, 0))
                out = rotq[:, j % 2] if t else rot[:, j]
                nc.gpsimd.tensor_tensor(out=out, in0=up[:, m % 2], in1=vp[:, m % 2, ::-1, :],
                                        op=ALU.add).then_inc(rotated, 1)

            def normalise(it, j):
                pool.wait_ge(inverted, at(it, QUADS, j + 1))
                r = rden[:, j % 2, :].unsqueeze(2).broadcast_to([P, 16, 64])
                p3 = prob[:, j % 2, :].rearrange("p (c k) -> p c k", k=64)
                nc.gpsimd.tensor_tensor(out=p3, in0=p3, in1=r, op=ALU.mult).then_inc(probs_set, 1)

            def split_norms(n):
                pool.wait_ge(norm_rounded, at(n, 1, 1))
                nc.gpsimd.tensor_tensor(out=norm_lo[:], in0=norm[:], in1=norm_hi[:].bitcast(F32), op=ALU.subtract)\
                    .then_inc(norm_split, 1)

            for m in range(8):
                rotate(0, m, None)
            split_norms(0)
            with pool.Fori(0, DEPTH) as layer:
                with pool.Fori(0, PAIRS) as pair:
                    it = layer * PAIRS + pair
                    for j in range(QUADS):
                        if j:
                            normalise(it, j - 1)
                        rotate(it + 1, 2 * j, it)
                        rotate(it + 1, 2 * j + 1, it)
                    split_norms(it + 1)

        @block.scalar
        def _(act):
            act.wait_ge(consts_in, 16 * 6)
            nc.scalar.copy(ident_r[:], ident[:]).then_inc(consts_set, 1)
            nc.scalar.copy(ident_b[:], ident[:]).then_inc(consts_set, 1)
            nc.scalar.copy(mask[:], mask32).then_inc(consts_set, 1)
            nc.scalar.copy(spread[:].rearrange("p a b -> p (a b)"), spread32).then_inc(consts_set, 1)
            for s in (hi_made, w_vo_set, x_hi, xw_copied, squared, exped, turned_out, mixed_a, csq, roots, rooted, norm_rounded,
                      gated, stored):
                act.sem_inc(s, 1)

            def round_weights(layer):
                act.wait_ge(w_in, at(layer, 16, 16))
                nc.scalar.copy(wqk_hi[:].rearrange("p t j a n -> p (t j a n)"), raw[:, W_QK[0]:W_QK[1]])\
                    .then_inc(hi_made, 1)

            def round_inputs(n):
                act.wait_ge(xs_in, at(n, 48, 48))
                nc.scalar.copy(xs_hi[:], xs_now).then_inc(x_hi, 1)

            def square(n, m, it):
                if m >= 2:
                    act.wait_ge(normed2, at(n, 8, m - 1))
                elif it is not None:
                    act.wait_ge(hid_set, at(it, 3, 0))
                for ab in range(2):
                    act.wait_ge(projected, at(n, 16, 2 * m + ab + 1))
                    nc.scalar.activation(sq[:, m % 2, ab], p_qk[:, ab, :], ACT.Square).then_inc(squared, 1)

            def take_norms(n):
                act.wait_ge(normed2, at(n, 8, 8))
                nc.scalar.activation(norm[:], p_sum, ACT.Sqrt).then_inc(rooted, 1)

            def round_norms(n):
                act.wait_ge(inverse_set, at(n, 2, 2))
                nc.scalar.copy(norm_hi[:], norm[:]).then_inc(norm_rounded, 1)

            def copy_windows(n, ch):
                act.wait_ge(xw_sum, at(n, 5, ch + 1))
                to = xw[:, 4 * ch:min(4 * ch + 4, 18)].rearrange("p w n -> p (w n)")
                nc.scalar.copy(to, p_xw[ch % 2][:, 0:to.shape[1]]).then_inc(xw_copied, 1)

            def copy_turned(it, m):
                act.wait_ge(turned, at(it, 8, m + 1))
                if m == 0:
                    act.wait_ge(stored, at(it, 16, 0))
                nc.scalar.copy(prob_t[:, m // 2, m % 2, :], p_turned(m)).then_inc(turned_out, 1)

            def take_weights(layer):
                for m in range(2):
                    act.wait_ge(w_vo_sum, at(layer, 2, m + 1))
                    nc.scalar.copy(w_vo[:, m].rearrange("p c n -> p (c n)"),
                                   pj[m][:].rearrange("p a n -> p (a n)")).then_inc(w_vo_set, 1)

            def turn(it, n, cols, next_layer):
                for j in range(QUADS):
                    square(n, 2 * j, it)
                    if j:
                        copy_turned(it, 2 * j - 2)
                    act.wait_ge(z_set, at(it, QUADS, j + 1))
                    if j >= 2:
                        act.wait_ge(turned, at(it, 8, 2 * j - 2))
                    nc.scalar.activation(prob[:, j % 2, :], zs[:, j % 2, :], ACT.Exp, scale=QK_SCALE)\
                        .then_inc(exped, 1)
                    square(n, 2 * j + 1, it)
                    if j:
                        copy_turned(it, 2 * j - 1)
                copy_turned(it, 6)
                copy_turned(it, 7)
                take_norms(n)
                for w in range(0, 16, 2):
                    if w in (0, 4):
                        act.wait_ge(rotated, at(n, 8, 7 + w // 4))
                    act.wait_ge(mixed, at(it, 16, w + 1))
                    nc.scalar.copy(y_t[:, (w // 4) % 2, :, :, 32 * (w % 4):32 * (w % 4) + 32],
                                   pj[w % 2][:, :, 0:256].rearrange("p a (h n) -> p a h n", n=32))\
                        .then_inc(mixed_a, 1)
                    if w == 4:
                        round_norms(n)
                copy_windows(n, 0)
                copy_windows(n, 1)
                act.wait_ge(centred, at(it, 1, 1))
                nc.scalar.activation(xsq, xc, ACT.Square).then_inc(csq, 1)
                copy_windows(n, 2)
                act.wait_ge(vared, at(it, 1, 1))
                nc.scalar.activation(root, p_var, ACT.Sqrt, bias=eps[:, 0:1]).then_inc(roots, 1)
                copy_windows(n, 3)
                copy_windows(n, 4)
                if next_layer is not None:
                    take_weights(next_layer)
                for m in range(3):
                    act.wait_ge(h_sum, at(it, 3, m + 1))
                    nc.scalar.activation(gate[:, m, :], pj[m % 2][:, 1, :], ACT.Gelu, bias=b1[:, 3 + m:4 + m])\
                        .then_inc(gated, 1)
                round_inputs(n + 1)
                act.wait_ge(out_set, at(it, 1, 1))
                act.dma_start(cols, xo).then_inc(stored, 16)

            round_weights(0)
            round_inputs(0)
            for m in range(8):
                square(0, m, None)
            take_norms(0)
            round_norms(0)
            for ch in range(5):
                copy_windows(0, ch)
            take_weights(0)
            round_inputs(1)
            with act.Fori(0, DEPTH) as layer:
                act.wait_ge(w_taken, at(layer, 1, 1))
                act.dma_start(raw[:], w_layers[1:DEPTH + 1][layer]).then_inc(w_in, 16)
                with act.Fori(0, PAIRS - 1) as pair:
                    it = layer * PAIRS + pair
                    turn(it, it + 1, state[:, bass.ts(pair, NT)], None)
                round_weights(layer + 1)
                it = layer * PAIRS + (PAIRS - 1)
                turn(it, it + 1, state[:, (PAIRS - 1) * NT:PAIRS * NT], layer + 1)

        @block.vector
        def _(dve):
            for s in (lo_made, w_tables, w_ready, w_taken, x_free, x_lo, scaled, guarded, inverse_set, root_inv, rq_set, k_normed, maxed,
                      z_set, summed, inverted, last_probs_set, mixed_v, x1_set, centred, ln_set, hid_set, out_set):
                dve.sem_inc(s, 1)
            dve.wait_ge(consts_in, 16 * 6)

            def weight_tables(layer):
                dve.wait_ge(w_in, at(layer, 16, 16))
                for t in range(2):
                    base = 2 if t == 0 else 0
                    for ab in range(2):
                        at_s = W_VEC[0] + 2 * t + ab
                        s = raw[:, at_s:at_s + 1]
                        nc.vector.tensor_scalar(straight[t][:, ab, :], trig[:, base, :], s, None, ALU.mult)
                        nc.vector.tensor_scalar(crossed[t][:, ab, :], trig[:, base + 1, :], s,
                                                -1.0 if ab else 1.0, ALU.mult, ALU.mult)
                dve.wait_ge(hi_made, at(layer, 1, 1))
                nc.vector.tensor_tensor(out=wqk_lo[:].rearrange("p t j a n -> p (t j a n)"),
                                        in0=raw[:, W_QK[0]:W_QK[1]],
                                        in1=wqk_hi[:].rearrange("p t j a n -> p (t j a n)").bitcast(F32),
                                        op=ALU.subtract).then_inc(lo_made, 1)
                dve.wait_ge(lo_made, at(layer, 1, 1))

            def split_inputs(n):
                dve.wait_ge(x_hi, at(n, 1, 1))
                nc.vector.tensor_tensor(out=xs_lo[:], in0=xs_now, in1=xs_hi[:].bitcast(F32),
                                        op=ALU.subtract).then_inc(x_lo, 1)

            def scale(n, m):
                t = m % 2
                if m >= 2:
                    dve.wait_ge(rotated, at(n, 8, m - 1))
                for ab in range(2):
                    dve.wait_ge(squared, at(n, 16, 2 * m + ab + 1))
                    src, to_up, to_vp = (a.rearrange("p (s n) -> p s n", s=2)
                                         for a in (p_qk[:, ab, :], up[:, m % 2, ab], vp[:, m % 2, ab]))
                    nc.vector.tensor_tensor(out=to_up, in0=src, in1=two(straight[t][:, ab, :]), op=ALU.mult)
                    nc.vector.tensor_tensor(out=to_vp, in0=src, in1=two(crossed[t][:, ab, :]), op=ALU.mult)\
                        .then_inc(scaled, 1)

            def guard_norms(n):
                dve.wait_ge(rooted, at(n, 1, 1))
                nc.vector.tensor_scalar(norm[:], norm[:], 1e-12, None, ALU.max).then_inc(guarded, 1)

            def invert_norms(n, h):
                dve.wait_ge(guarded, at(n, 1, 1))
                part = slice(h * T, (h + 1) * T)
                nc.vector.reciprocal(norm[:, part], norm[:, part]).then_inc(inverse_set, 1)

            def take_q_norms(n):
                dve.wait_ge(norm_turned, at(n, 1, 1))
                for g in range(GROUPS):
                    last = nc.vector.tensor_copy(
                        rq[:, :, :, g, :],
                        p_turn[:, g * P:(g + 1) * P].rearrange("p (j r) -> p j r", j=QUADS)[:, :, 0:4]
                        .rearrange("p j (c a) -> p j a c", a=2))
                last.then_inc(rq_set, 1)

            def norm_k(n, j):
                dve.wait_ge(spread_out, at(n, QUADS, j + 1))
                dve.wait_ge(rotated, at(n, 8, 2 * j + 1))
                nc.vector.tensor_tensor(out=rot[:, j], in0=rot[:, j],
                                        in1=p_spread[j % 2].unsqueeze(1).broadcast_to([P, 2, NT]),
                                        op=ALU.mult).then_inc(k_normed, 1)

            def turn(it, n):
                def highest(j):
                    dve.wait_ge(scored, at(it, QUADS, j + 1))
                    if j >= 2:
                        dve.wait_ge(shifted, at(it, QUADS, j - 1))
                    nc.vector.tensor_reduce(negmax[:, j % 2, :].rearrange("p (a c) -> p a c", a=2),
                                            pj[j % 2][:].rearrange("p a (c k) -> p a c k", k=64), AX.X,
                                            ALU.max, negate=True).then_inc(maxed, 1)

                def times_rq(j):
                    dve.wait_ge(shifted, at(it, QUADS, j + 1))
                    if j >= 2:
                        dve.wait_ge(exped, at(it, QUADS, j - 1))
                    nc.vector.tensor_tensor(
                        out=zs[:, j % 2, :].rearrange("p (c k) -> p c k", k=64),
                        in0=pj[j % 2][:].rearrange("p a (c k) -> p (a c) k", k=64),
                        in1=rq[:, j].rearrange("p a g c -> p (a g c)").unsqueeze(2).broadcast_to([P, 16, 64]),
                        op=ALU.mult).then_inc(z_set, 1)

                def sums(j):
                    dve.wait_ge(exped, at(it, QUADS, j + 1))
                    nc.vector.tensor_reduce(den[:, j % 2, :], prob[:, j % 2, :].rearrange("p (c k) -> p c k", k=64),
                                            AX.X, ALU.add).then_inc(summed, 1)
                    dve.wait_ge(summed, at(it, QUADS, j + 1))
                    if j >= 2:
                        dve.wait_ge(probs_set, at(it, QUADS - 1, j - 1))
                    nc.vector.reciprocal(rden[:, j % 2, :], den[:, j % 2, :]).then_inc(inverted, 1)

                def copy_mix(w):
                    dve.wait_ge(mixed, at(it, 16, w + 1))
                    nc.vector.tensor_copy(y_t[:, (w // 4) % 2, :, :, 32 * (w % 4):32 * (w % 4) + 32],
                                          pj[w % 2][:, :, 0:256].rearrange("p a (h n) -> p a h n", n=32))\
                        .then_inc(mixed_v, 1)

                dve.wait_ge(rq_set, at(it, 1, 1))
                for j in range(QUADS - 1):
                    highest(j)
                    scale(n, 2 * j)
                    times_rq(j)
                    scale(n, 2 * j + 1)
                    sums(j)
                highest(QUADS - 1)
                times_rq(QUADS - 1)
                scale(n, 6)
                sums(QUADS - 1)
                dve.wait_ge(inverted, at(it, QUADS, QUADS))
                nc.vector.tensor_tensor(out=prob[:, 1, :].rearrange("p (c k) -> p c k", k=64),
                                        in0=prob[:, 1, :].rearrange("p (c k) -> p c k", k=64),
                                        in1=rden[:, 1, :].unsqueeze(2).broadcast_to([P, 16, 64]), op=ALU.mult)\
                    .then_inc(last_probs_set, 1)
                scale(n, 7)
                dve.wait_ge(rotated, at(n, 8, 7))
                copy_mix(1)
                copy_mix(3)
                guard_norms(n)
                invert_norms(n, 0)
                dve.wait_ge(rotated, at(n, 8, 8))
                copy_mix(5)
                invert_norms(n, 1)
                copy_mix(7)
                take_q_norms(n)
                copy_mix(9)
                copy_mix(11)
                norm_k(n, 0)
                copy_mix(13)
                norm_k(n, 1)
                copy_mix(15)
                norm_k(n, 2)
                norm_k(n, 3)
                dve.wait_ge(attended, at(it, GROUPS, GROUPS))
                dve.wait_ge(x_in, at(it, 16, 16))
                nc.vector.tensor_tensor(out=xs2[0:64], in0=p_att[0:64], in1=x[0:64], op=ALU.add)
                nc.vector.memset(xs2.rearrange("p (s n) -> p s n", s=2)[64:P, :, 0:1], 0.0)
                nc.vector.tensor_tensor(
                    out=xs2.rearrange("p (s n) -> p s n", s=2)[64:P, :, 1:T],
                    in0=p_att.rearrange("p (s n) -> p s n", s=2)[64:P, :, 0:T - 1],
                    in1=x[:].rearrange("p (s n) -> p s n", s=2)[64:P, :, 0:T - 1], op=ALU.add).then_inc(x1_set, 1)
                nc.vector.tensor_tensor(out=x1, in0=p_att, in1=x[:], op=ALU.add).then_inc(x1_set, 1)
                dve.wait_ge(x1_set, at(it, 2, 2))
                dve.sem_inc(x_free, 1)
                dve.wait_ge(meaned, at(it, 1, 1))
                nc.vector.tensor_tensor(out=xc, in0=xs2, in1=p_mean, op=ALU.subtract).then_inc(centred, 1)
                dve.wait_ge(roots, at(it, 1, 1))
                for h in range(2):
                    part = slice(h * T, (h + 1) * T)
                    nc.vector.reciprocal(root[:, part], root[:, part]).then_inc(root_inv, 1)
                    dve.wait_ge(root_inv, at(it, 2, h + 1))
                    nc.vector.tensor_tensor(out=xn[:, part], in0=xc[:, part], in1=root[:, part], op=ALU.mult)\
                        .then_inc(ln_set, 1)
                for m in range(3):
                    dve.wait_ge(gated, at(it, 3, m + 1))
                    nc.vector.scalar_tensor_tensor(out=hid[:, m, :], in0=pj[m % 2][:, 0, :],
                                                   scalar=b1[:, m:m + 1], in1=gate[:, m, :], op0=ALU.add,
                                                   op1=ALU.mult).then_inc(hid_set, 1)
                split_inputs(n + 1)
                dve.wait_ge(out_sum, at(it, 1, 1))
                nc.vector.scalar_tensor_tensor(out=xo, in0=p_ffn, scalar=vec[:, 12:13], in1=x1, op0=ALU.add,
                                               op1=ALU.add).then_inc(out_set, 1)

            weight_tables(0)
            split_inputs(0)
            for m in range(8):
                scale(0, m)
            guard_norms(0)
            for h in range(2):
                invert_norms(0, h)
            take_q_norms(0)
            for j in range(QUADS):
                norm_k(0, j)
            split_inputs(1)
            with dve.Fori(0, DEPTH) as layer:
                dve.wait_ge(out_set, at(layer, PAIRS, 0))
                nc.vector.tensor_copy(vec[:], raw[:, W_VEC[0]:W_VEC[1]]).then_inc(w_tables, 1)
                nc.vector.tensor_copy(w2[:].rearrange("p c n -> p (c n)"), raw[:, W_2[0]:W_2[1]])
                dve.wait_ge(w_tables, at(layer, 2, 1))
                nc.vector.tensor_scalar(w1[:].rearrange("p c n -> p (c n)"), raw[:, W_1[0]:W_1[1]],
                                        vec[:, 4:5], None, ALU.mult)
                dve.wait_ge(b1_sum, at(layer, 1, 1))
                nc.vector.tensor_tensor(out=b1[:], in0=p_att[:, 0:6], in1=vec[:, 6:12], op=ALU.add)\
                    .then_inc(w_tables, 1)
                dve.wait_ge(w_tables, at(layer, 2, 2))
                dve.sem_inc(w_taken, 1)
                dve.sem_inc(w_ready, 1)
                with dve.Fori(0, PAIRS - 1) as pair:
                    it = layer * PAIRS + pair
                    turn(it, it + 1)
                weight_tables(layer + 1)
                it = layer * PAIRS + (PAIRS - 1)
                turn(it, it + 1)

        @block.tensor
        def _(pe):
            for s in (w_vo_sum, b1_sum, xw_sum, projected, normed2, norm_turned, spread_out, scored, shifted, turned, mixed,
                      attended, meaned, vared, h_sum, out_sum):
                pe.sem_inc(s, 1)
            pe.wait_ge(consts_in, 16 * 6)
            pe.wait_ge(consts_set, 7)

            def turn_windows(n, ch):
                if ch >= 2:
                    pe.wait_ge(xw_copied, at(n, 5, ch - 1))
                elif ch:
                    pe.wait_ge(k_normed, at(n, QUADS, QUADS))
                else:
                    pe.wait_ge(rq_set, at(n, 1, 1))
                for w in range(4 * ch, min(4 * ch + 4, 18)):
                    last = nc.tensor.transpose(p_xw[ch % 2][:, (w % 4) * P:(w % 4 + 1) * P],
                                               xs[:, 32 * w:32 * w + P], ident[:])
                last.then_inc(xw_sum, 1)

            def project(n, m, layer, it):
                j, t = m // 2, m % 2
                if m == 0:
                    pe.wait_ge(lo_made, at(layer, 1, 1))
                    pe.wait_ge(x_lo, at(n, 1, 1))
                    if it is not None:
                        pe.wait_ge(out_set, at(it, 1, 0))
                for ab in range(2):
                    if m:
                        pe.wait_ge(scaled, at(n, 16, 2 * m + ab - 1))
                    hi, lo = wqk_hi[:, t, j, ab, :], wqk_lo[:, t, j, ab, :]
                    nc.tensor.matmul(p_qk[:, ab, :], hi, xs_hi[:], start=True, stop=False)
                    nc.tensor.matmul(p_qk[:, ab, :], hi, xs_lo[:], start=False, stop=False)
                    nc.tensor.matmul(p_qk[:, ab, :], lo, xs_hi[:], start=False, stop=True).then_inc(projected, 1)

            def sums(n, m):
                pe.wait_ge(squared, at(n, 16, 2 * m + 2))
                if m == 0:
                    pe.wait_ge(xw_copied, at(n, 5, 0))
                j, t = m // 2, m % 2
                for ab in range(2):
                    last = nc.tensor.matmul(p_sum[32 * j:32 * j + 32, :], head_sum[:, t, :],
                                            sq[:, m % 2, ab, :], start=(t == 0 and ab == 0),
                                            stop=(t == 1 and ab == 1))
                last.then_inc(normed2, 1)

            def turn_norms(n):
                pe.wait_ge(inverse_set, at(n, 2, 2))
                for g in range(GROUPS):
                    last = nc.tensor.transpose(p_turn[:, g * P:(g + 1) * P], norm[:, g * P:(g + 1) * P], ident[:])
                last.then_inc(norm_turned, 1)

            def spread_norms(n, j):
                if j >= 2:
                    pe.wait_ge(k_normed, at(n, QUADS, j - 1))
                elif j:
                    pe.wait_ge(scaled, at(n, 16, 16))
                if j == 0:
                    pe.wait_ge(norm_split, at(n, 1, 1))
                nc.tensor.matmul(p_spread[j % 2], spread[:, j, :], norm_hi[:], start=True, stop=False)
                nc.tensor.matmul(p_spread[j % 2], spread[:, j, :], norm_lo[:], start=False, stop=True)\
                    .then_inc(spread_out, 1)

            def multiply_weights(layer):
                pe.wait_ge(w_in, at(layer, 16, 16))
                wv = raw[:, W_V[0]:W_V[1]].rearrange("p (c n) -> p c n", c=8)
                wo = raw[:, W_O[0]:W_O[1]].rearrange("p (c n) -> p c n", c=8)
                for par in range(2):
                    r = slice(64 * par, 64 * par + 64)
                    for ch in range(8):
                        last = nc.tensor.matmul(pj[par][:, ch // 4, (ch % 4) * P:(ch % 4 + 1) * P],
                                                wv[r, ch, :], wo[r, ch, :], start=True, stop=True)
                    last.then_inc(w_vo_sum, 1)

            def turn(it, n, layer, next_layer):
                ends_layer = next_layer is not layer

                def scores(j):
                    if j >= 2:
                        pe.wait_ge(z_set, at(it, QUADS, j - 1))
                    else:
                        pe.wait_ge(hid_set, at(it, 3, 0))
                        pe.wait_ge(w_ready, at(layer, 1, 1))
                    pe.wait_ge(q_laid[j], at(it, 128, 128))
                    pe.wait_ge(k_laid[j], at(it, 128, 128))
                    for par in range(2):
                        nc.tensor.matmul(pj[j % 2][:, par, :], ident_b[:], mask[:], start=True, stop=True)
                    for ch in range(2):
                        for g in range(GROUPS):
                            for w in range(4):
                                for par in range(2):
                                    r = slice(64 * par, 64 * par + 64)
                                    at_w = 32 * (4 * g + w)
                                    col = (g * 2 + ch) * 64
                                    last = nc.tensor.matmul(
                                        pj[j % 2][32 * w:32 * w + 32, par, col:col + 64],
                                        q_t[r, 2 * j + ch, at_w:at_w + 32], k_t[r, 2 * j + ch, at_w:at_w + 64],
                                        start=False, stop=True, skip_group_check=True)
                    last.then_inc(scored, 1)

                def shift(j):
                    pe.wait_ge(maxed, at(it, QUADS, j + 1))
                    for par in range(2):
                        last = nc.tensor.matmul(
                            pj[j % 2][:, par, :].rearrange("p (c k) -> p c k", k=64), ident_r[:],
                            negmax[:, j % 2, 8 * par:8 * par + 8].unsqueeze(2).broadcast_to([P, 8, 64]),
                            start=False, stop=True, skip_group_check=True)
                    last.then_inc(shifted, 1)

                def turn_probs(m):
                    j, par = m // 2, m % 2
                    if j == QUADS - 1:
                        pe.wait_ge(last_probs_set, at(it, 1, 1))
                    else:
                        pe.wait_ge(probs_set, at(it, QUADS - 1, j + 1))
                    if m >= 6:
                        pe.wait_ge(z_set, at(it, QUADS, QUADS - 1))
                    elif m:
                        pe.wait_ge(turned_out, at(it, 8, m))
                    else:
                        pe.wait_ge(xw_copied, at(n, 5, 0))
                    p4 = prob[:, j % 2, :].rearrange("p (a g k) -> p a g k", a=2, g=GROUPS)
                    for g in range(GROUPS):
                        last = nc.tensor.transpose(p_turned(m)[:, g * P:(g + 1) * P], p4[:, par, g, :], ident[:])
                    last.then_inc(turned, 1)

                def mix(w):
                    if w >= 2:
                        pe.wait_ge(mixed_v if w % 2 else mixed_a, at(it, 8, w // 2))
                    for ch in range(2):
                        r = slice(64 * ch, 64 * ch + 64)
                        cols = (w // 4) * P + 32 * (w % 4)
                        last = nc.tensor.matmul(
                            pj[w % 2][:, ch, 0:256].rearrange("p (j a n) -> p j a n", j=QUADS, a=2),
                            xw[r, w + 2 * (1 - ch), :], prob_t[r, :, :, cols:cols + 32], start=True, stop=True)
                    last.then_inc(mixed, 1)

                def attend(g):
                    pe.wait_ge(mixed_a, at(it, 8, 2 * g + 2))
                    pe.wait_ge(mixed_v, at(it, 8, 2 * g + 2))
                    for m in range(16):
                        ch, jp = m // 8, m % 8
                        last = nc.tensor.matmul(p_att[:, g * P:(g + 1) * P], w_vo[:, jp % 2, 2 * (jp // 2) + ch, :],
                                                y_t[:, g % 2, ch, jp, :], start=(m == 0), stop=(m == 15))
                    last.then_inc(attended, 1)

                for j in range(QUADS):
                    scores(j)
                    project(n, 2 * j, next_layer, it)
                    shift(j)
                    if j:
                        sums(n, 2 * j - 1)
                        turn_probs(2 * j - 2)
                    project(n, 2 * j + 1, next_layer, it)
                    sums(n, 2 * j)
                    if j:
                        turn_probs(2 * j - 1)
                pe.wait_ge(z_set, at(it, QUADS, QUADS - 1))
                for _ in range(KEEP_BUSY):
                    nc.tensor.matmul(pj[0][:, 0, :], ident_b[:], mask[:], start=True, stop=True)
                turn_probs(6)
                turn_probs(7)
                sums(n, 7)
                pe.wait_ge(turned_out, at(it, 8, 8))
                pe.wait_ge(z_set, at(it, QUADS, QUADS))
                pe.wait_ge(scaled, at(n, 16, 16))
                for g in range(GROUPS):
                    for w in range(4 * g, 4 * g + 4):
                        mix(w)
                    if g:
                        attend(g - 1)
                        if g == 1:
                            turn_norms(n)
                        else:
                            spread_norms(n, 2 * g - 4)
                            spread_norms(n, 2 * g - 3)
                attend(GROUPS - 1)
                turn_windows(n, 0)
                turn_windows(n, 1)
                if ends_layer:
                    multiply_weights(next_layer)
                pe.wait_ge(x1_set, at(it, 2, 1))
                pe.wait_ge(k_normed, at(n, QUADS, QUADS))
                nc.tensor.matmul(p_mean, mean_w[:], xs2, start=True, stop=True).then_inc(meaned, 1)
                turn_windows(n, 2)
                pe.wait_ge(csq, at(it, 1, 1))
                nc.tensor.matmul(p_var, mean_w[:], xsq, start=True, stop=True).then_inc(vared, 1)
                for ch in range(3, 5):
                    turn_windows(n, ch)
                def hidden(m, part):
                    for half in range(2):
                        last = nc.tensor.matmul(pj[m % 2][:, half, part], w1[:, 3 * half + m, :], xn[:, part],
                                                start=True, stop=True)
                    return last

                if ends_layer:
                    pe.wait_ge(w_vo_set, at(next_layer, 2, 2))
                for h in range(2):
                    pe.wait_ge(ln_set, at(it, 2, h + 1))
                    for m in range(2):
                        last = hidden(m, slice(h * T, (h + 1) * T))
                        if h:
                            last.then_inc(h_sum, 1)
                pe.wait_ge(hid_set, at(it, 3, 1))
                hidden(2, slice(0, NT)).then_inc(h_sum, 1)
                pe.wait_ge(hid_set, at(it, 3, 3))
                for m in range(3):
                    last = nc.tensor.matmul(p_ffn, w2[:, m, :], hid[:, m, :], start=(m == 0), stop=(m == 2))
                last.then_inc(out_sum, 1)

            for m in range(8):
                project(0, m, 0, None)
                if m:
                    sums(0, m - 1)
            sums(0, 7)
            turn_norms(0)
            for j in range(QUADS):
                spread_norms(0, j)
            for ch in range(5):
                turn_windows(0, ch)
            multiply_weights(0)
            pe.wait_ge(w_vo_set, at(0, 2, 2))
            with pe.Fori(0, DEPTH) as layer:
                pe.wait_ge(out_set, at(layer, PAIRS, 0))
                for m in range(6):
                    last = nc.tensor.matmul(p_att[:, m:m + 1], raw[:, W_1[0] + m * P:W_1[0] + (m + 1) * P],
                                            raw[:, W_VEC[0] + 5:W_VEC[0] + 6], start=True, stop=True)
                last.then_inc(b1_sum, 1)
                with pe.Fori(0, PAIRS - 1) as pair:
                    it = layer * PAIRS + pair
                    turn(it, it + 1, layer, layer)
                it = layer * PAIRS + (PAIRS - 1)
                turn(it, it + 1, layer, layer + 1)

def add_and_store(nc, c, x2, state, out):
    with ExitStack() as ctx:
        ident = ctx.enter_context(nc.sbuf_tensor("o_ident", [P, P], F32))
        x = ctx.enter_context(nc.sbuf_tensor("o_x", [P, 2, GROUPS, DIM], F32))
        s_t = ctx.enter_context(nc.sbuf_tensor("o_s", [P, 2, NT], F32))
        turned = ctx.enter_context(nc.psum_tensor("o_turned", [P, 2, NT], F32))
        consts_in, loaded, turned_in, added, stored = (ctx.enter_context(nc.semaphore("o_" + n)) for n in (
            "consts_in", "loaded", "turned_in", "added", "stored"))
        slot_loaded = [loaded, ctx.enter_context(nc.semaphore("o_loaded1"))]
        slot_stored = [stored, ctx.enter_context(nc.semaphore("o_stored1"))]
        block = ctx.enter_context(nc.Block())

        @block.sync
        def _(sp):
            sp.dma_start(ident[:], c[:, C_IDENT[0]:C_IDENT[1]]).then_inc(consts_in, 16)
            for pair in range(PAIRS):
                k = pair % 2
                if pair >= 2:
                    sp.wait_ge(slot_stored[k], 16 * (pair // 2))
                sp.dma_start(x[:, k], x2[2 * pair:2 * pair + 2].rearrange("s (t p) n -> p (s t) n", p=P))\
                    .then_inc(slot_loaded[k], 16)
                sp.dma_start(s_t[:, k, :], state[:, pair * NT:(pair + 1) * NT]).then_inc(slot_loaded[k], 16)
            for k in range(2):
                sp.wait_ge(slot_stored[k], 16 * (PAIRS // 2))

        @block.tensor
        def _(pe):
            pe.wait_ge(consts_in, 16)
            for pair in range(PAIRS):
                k = pair % 2
                pe.wait_ge(slot_loaded[k], 32 * (pair // 2 + 1))
                if pair >= 2:
                    pe.wait_ge(added, pair - 1)
                for g in range(GROUPS):
                    last = nc.tensor.transpose(turned[:, k, g * P:(g + 1) * P], s_t[:, k, g * P:(g + 1) * P], ident[:])
                last.then_inc(turned_in, 1)

        @block.vector
        def _(dve):
            for pair in range(PAIRS):
                k = pair % 2
                dve.wait_ge(turned_in, pair + 1)
                dve.wait_ge(slot_loaded[k], 32 * (pair // 2 + 1))
                nc.vector.tensor_tensor(out=x[:, k].rearrange("p g n -> p (g n)"), in0=turned[:, k, :],
                                        in1=x[:, k].rearrange("p g n -> p (g n)"), op=ALU.add).then_inc(added, 1)

        @block.scalar
        def _(act):
            for pair in range(PAIRS):
                k = pair % 2
                act.wait_ge(added, pair + 1)
                act.dma_start(out[2 * pair:2 * pair + 2].rearrange("s (t p) n -> p (s t) n", p=P), x[:, k])\
                    .then_inc(slot_stored[k], 16)

def kernel(**inputs):
    import numpy as np
    import concourse.bacc as bacc
    from concourse.bass_utils import run_bass_kernel_spmd

    arrays = {
        "x": np.ascontiguousarray(inputs["x"]),
        "ctx_t": np.ascontiguousarray(np.asarray(inputs["ctx_512"]).transpose(0, 2, 1)),
        "w_attn": attention_weights(np, inputs),
        "w_layers": layer_weights(np, inputs),
        "consts": constants(np),
    }
    nc = bacc.Bacc("TRN2", target_bir_lowering=False, num_devices=1)
    d = {n: nc.dram_tensor(n, a.shape, mybir.dt.from_np(a.dtype), kind="ExternalInput").ap()
         for n, a in arrays.items()}
    out = nc.dram_tensor("out", (B, T, DIM), F32, kind="ExternalOutput").ap()
    x2 = nc.dram_tensor("x2", (B, T, DIM), F32).ap()
    state = nc.dram_tensor("state", (DIM, B * T), F32).ap()
    attention_blocks(nc, d["consts"], d["x"], d["ctx_t"], d["w_attn"], x2, state)
    transformer_layers(nc, d["consts"], d["w_layers"], state)
    add_and_store(nc, d["consts"], x2, state, out)
    return run_bass_kernel_spmd(nc, [arrays], core_ids=[0]).results[0]["out"]
```
